# Optimizing a Trainium2 kernel written in Bass

```python
import numpy as np
import jax
import jax.numpy as jnp

def _softmax(x, axis=-1):
    return jax.nn.softmax(x, axis=axis)

def _gelu(x):
    return jax.nn.gelu(x, approximate=True)

def _silu(x):
    return jax.nn.silu(x)

def _sigmoid(x):
    return jax.nn.sigmoid(x)

def _layernorm(x, axis=-1, eps=1e-05):
    m = jnp.mean(x, axis=axis, keepdims=True)
    v = jnp.var(x, axis=axis, keepdims=True)
    return (x - m) / jnp.sqrt(v + eps)

def _scatter_add(tgt, idx, src, axis=0):
    return tgt.at[idx].add(src)

def _segment_sum(src, seg, n):
    return jax.ops.segment_sum(src, seg, n)
kernel_name = 'mk_metaformer_d1_conv_nhwc768_r4_23c597'

def setup_inputs(seed: int=0):
    np.random.seed(seed)
    _w = jnp.asarray

    def _rec_inputs():
        import jax
        import jax.numpy as jnp
        _gk = jax.random.key(seed)
        x = -0.0005058 + 1 * jax.random.normal(jax.random.fold_in(_gk, 1), (2, 48, 48, 192), jnp.float32)
        return x
    x = _rec_inputs()

    def _L0_conv_setup():
        import jax, jax.numpy as jnp
        import numpy as np
        D_MODEL = 192
        D_HEAD = 16
        N_HEADS = D_MODEL // D_HEAD
        KERNEL = 7
        NEG_INF = -1e+30

        def make_neighbourhood_mask(kernel_h, kernel_w, canvas_h, canvas_w):
            h_ramp = jnp.arange(canvas_h)
            w_ramp = jnp.arange(canvas_w)
            h_pos, w_pos = jnp.meshgrid(h_ramp, w_ramp, indexing='ij')
            start_h = jnp.clip(h_pos - kernel_h // 2, 0, canvas_h - kernel_h)[..., None, None]
            end_h = start_h + kernel_h
            start_w = jnp.clip(w_pos - kernel_w // 2, 0, canvas_w - kernel_w)[..., None, None]
            end_w = start_w + kernel_w
            h_range = h_ramp.reshape(1, 1, canvas_h, 1)
            w_range = w_ramp.reshape(1, 1, 1, canvas_w)
            mask = (h_range >= start_h) & (h_range < end_h) & (w_range >= start_w) & (w_range < end_w)
            return mask.reshape(canvas_h * canvas_w, canvas_h * canvas_w)
        key = jax.random.key(seed)
        k1, k2, k3, k4, k5, k6 = jax.random.split(key, 6)
        x = jax.random.normal(k1, (2, 48, 48, D_MODEL), dtype=jnp.float32)
        registers = jax.random.normal(k2, (16, D_MODEL), dtype=jnp.float32)
        scale = 1.0 / np.sqrt(D_MODEL)
        qkv_w = jax.random.normal(k3, (3 * D_MODEL, D_MODEL), dtype=jnp.float32) * scale
        qkv_b = jax.random.normal(k4, (3 * D_MODEL,), dtype=jnp.float32) * 0.01
        out_w = jax.random.normal(k5, (D_MODEL, D_MODEL), dtype=jnp.float32) * scale
        out_b = jax.random.normal(k6, (D_MODEL,), dtype=jnp.float32) * 0.01
        return {'x': x, 'registers': registers, 'qkv_w': qkv_w, 'qkv_b': qkv_b, 'out_w': out_w, 'out_b': out_b}
    _L0_conv_all = _L0_conv_setup()
    _L0_conv_in = {k: v for k, v in _L0_conv_all.items() if k in ('registers', 'qkv_w', 'qkv_b', 'out_w', 'out_b')}
    del _L0_conv_all

    def _L0_ffn_setup():
        import jax, jax.numpy as jnp
        import numpy as np
        DIM = 192
        MOE_INTER = 512
        N_EXPERTS = 16
        TOP_K = 2
        SHARED_INTER = 2 * 512
        ROUTE_SCALE = 1.0
        B, S = (8, 49)
        key = jax.random.key(seed)
        ks = jax.random.split(key, 8)
        sc = 0.02
        return {'x': jax.random.normal(ks[0], (B, S, DIM), jnp.float32), 'gate_w': jax.random.normal(ks[1], (N_EXPERTS, DIM), jnp.float32) * sc, 'w1': jax.random.normal(ks[2], (N_EXPERTS, MOE_INTER, DIM), jnp.float32) * sc, 'w2': jax.random.normal(ks[3], (N_EXPERTS, DIM, MOE_INTER), jnp.float32) * sc, 'w3': jax.random.normal(ks[4], (N_EXPERTS, MOE_INTER, DIM), jnp.float32) * sc, 'sw1': jax.random.normal(ks[5], (SHARED_INTER, DIM), jnp.float32) * sc, 'sw2': jax.random.normal(ks[6], (DIM, SHARED_INTER), jnp.float32) * sc, 'sw3': jax.random.normal(ks[7], (SHARED_INTER, DIM), jnp.float32) * sc}
    _L0_ffn_all = _L0_ffn_setup()
    _L0_ffn_in = {k: v for k, v in _L0_ffn_all.items() if k in ('gate_w', 'w1', 'w2', 'w3', 'sw1', 'sw2', 'sw3')}
    del _L0_ffn_all
    return {'x': x, 'L0_conv_registers': _L0_conv_in['registers'], 'L0_conv_qkv_w': _L0_conv_in['qkv_w'], 'L0_conv_qkv_b': _L0_conv_in['qkv_b'], 'L0_conv_out_w': _L0_conv_in['out_w'], 'L0_conv_out_b': _L0_conv_in['out_b'], 'L0_ffn_gate_w': _L0_ffn_in['gate_w'], 'L0_ffn_w1': _L0_ffn_in['w1'], 'L0_ffn_w2': _L0_ffn_in['w2'], 'L0_ffn_w3': _L0_ffn_in['w3'], 'L0_ffn_sw1': _L0_ffn_in['sw1'], 'L0_ffn_sw2': _L0_ffn_in['sw2'], 'L0_ffn_sw3': _L0_ffn_in['sw3']}

def reference(x, L0_conv_registers, L0_conv_qkv_w, L0_conv_qkv_b, L0_conv_out_w, L0_conv_out_b, L0_ffn_gate_w, L0_ffn_w1, L0_ffn_w2, L0_ffn_w3, L0_ffn_sw1, L0_ffn_sw2, L0_ffn_sw3):
    import jax
    import jax.numpy as jnp

    def _L0_conv_ref(x, registers, qkv_w, qkv_b, out_w, out_b):
        import jax, jax.numpy as jnp
        import numpy as np
        D_MODEL = 192
        D_HEAD = 16
        N_HEADS = D_MODEL // D_HEAD
        KERNEL = 7
        NEG_INF = -1e+30

        def make_neighbourhood_mask(kernel_h, kernel_w, canvas_h, canvas_w):
            h_ramp = jnp.arange(canvas_h)
            w_ramp = jnp.arange(canvas_w)
            h_pos, w_pos = jnp.meshgrid(h_ramp, w_ramp, indexing='ij')
            start_h = jnp.clip(h_pos - kernel_h // 2, 0, canvas_h - kernel_h)[..., None, None]
            end_h = start_h + kernel_h
            start_w = jnp.clip(w_pos - kernel_w // 2, 0, canvas_w - kernel_w)[..., None, None]
            end_w = start_w + kernel_w
            h_range = h_ramp.reshape(1, 1, canvas_h, 1)
            w_range = w_ramp.reshape(1, 1, 1, canvas_w)
            mask = (h_range >= start_h) & (h_range < end_h) & (w_range >= start_w) & (w_range < end_w)
            return mask.reshape(canvas_h * canvas_w, canvas_h * canvas_w)
        n, h, w, _ = x.shape
        nh, e = (N_HEADS, D_HEAD)
        s = h * w
        r = registers.shape[0]
        qkv = x @ qkv_w.T + qkv_b
        qkv = qkv.reshape(n, h, w, 3, nh, e)
        qkv = qkv.transpose(3, 0, 4, 1, 2, 5).reshape(3, n, nh, s, e)
        q, k, v = (qkv[0], qkv[1], qkv[2])
        reg_kv = registers @ qkv_w[D_MODEL:].T + qkv_b[D_MODEL:]
        reg_kv = reg_kv.reshape(r, 2, nh, e).transpose(1, 2, 0, 3)
        reg_k = jnp.broadcast_to(reg_kv[0][None], (n, nh, r, e))
        reg_v = jnp.broadcast_to(reg_kv[1][None], (n, nh, r, e))
        k_cat = jnp.concatenate([k, reg_k], axis=-2)
        v_cat = jnp.concatenate([v, reg_v], axis=-2)
        mask = make_neighbourhood_mask(KERNEL, KERNEL, h, w)
        mask_cat = jnp.concatenate([mask, jnp.ones((s, r), dtype=bool)], axis=-1)
        scale = 1.0 / jnp.sqrt(jnp.asarray(e, dtype=x.dtype))
        scores = jnp.einsum('bnqe,bnke->bnqk', q, k_cat) * scale
        scores = jnp.where(mask_cat[None, None], scores, NEG_INF)
        attn = jax.nn.softmax(scores, axis=-1)
        o = jnp.einsum('bnqk,bnke->bnqe', attn, v_cat)
        o = o.transpose(0, 2, 1, 3).reshape(n, h, w, nh * e)
        return o @ out_w.T + out_b

    def _L0_ffn_ref(x, gate_w, w1, w2, w3, sw1, sw2, sw3):
        import jax, jax.numpy as jnp
        import numpy as np
        DIM = 192
        MOE_INTER = 512
        N_EXPERTS = 16
        TOP_K = 2
        SHARED_INTER = 2 * 512
        ROUTE_SCALE = 1.0
        B, S = (8, 49)
        Bb, Ss, D = x.shape
        xf = x.reshape(-1, D)
        T = xf.shape[0]
        scores = jax.nn.softmax(xf @ gate_w.T, axis=-1)
        topw, topi = jax.lax.top_k(scores, TOP_K)
        topw = topw * ROUTE_SCALE
        comb = jnp.zeros((T, N_EXPERTS), xf.dtype).at[jnp.arange(T)[:, None], topi].set(topw)
        h = jax.nn.silu(jnp.einsum('td,eid->tei', xf, w1)) * jnp.einsum('td,eid->tei', xf, w3)
        h = h * comb[:, :, None]
        y = jnp.einsum('tei,edi->td', h, w2)
        z = jax.nn.silu(xf @ sw1.T) * (xf @ sw3.T) @ sw2.T
        return (y + z).reshape(Bb, Ss, D)

    def _gn(v, G=32, eps=1e-05):
        B_, H_, W_, C_ = v.shape
        g = v.reshape(B_, H_, W_, G, C_ // G)
        m = jnp.mean(g, axis=(1, 2, 4), keepdims=True)
        s = jnp.var(g, axis=(1, 2, 4), keepdims=True)
        return ((g - m) / jnp.sqrt(s + eps)).reshape(v.shape)

    def _ln_c(v, eps=1e-06):
        m = jnp.mean(v, axis=-1, keepdims=True)
        s = jnp.var(v, axis=-1, keepdims=True)
        return (v - m) / jnp.sqrt(s + eps)

    def _ln_t(v, eps=1e-05):
        m = jnp.mean(v, axis=-1, keepdims=True)
        s = jnp.var(v, axis=-1, keepdims=True)
        return (v - m) / jnp.sqrt(s + eps)

    def _to_tokens(v):
        B_, H_, W_, C_ = v.shape
        return v.reshape(B_, H_ * W_, C_)

    def _from_tokens(t, like):
        return t.reshape(like.shape)
    x = x + _L0_conv_ref(_ln_c(x), L0_conv_registers, L0_conv_qkv_w, L0_conv_qkv_b, L0_conv_out_w, L0_conv_out_b)
    t = _to_tokens(x)
    t = t + _L0_ffn_ref(_ln_t(t), L0_ffn_gate_w, L0_ffn_w1, L0_ffn_w2, L0_ffn_w3, L0_ffn_sw1, L0_ffn_sw2, L0_ffn_sw3)
    x = _from_tokens(t, x)
    return x

_drawn_inputs = setup_inputs


def setup_inputs(seed=0):
    import zlib

    import numpy as np

    out = dict(_drawn_inputs(seed))
    spreads = {}
    factors = {'L0_conv_qkv_b': 5.792,
     'L0_conv_out_b': 5.43,
     'L0_ffn_gate_w': 8.0,
     'L0_ffn_w1': 8.0,
     'L0_ffn_w2': 8.0,
     'L0_ffn_w3': 8.0,
     'L0_ffn_sw1': 8.0,
     'L0_ffn_sw2': 8.0,
     'L0_ffn_sw3': 8.0}
    for name, (base, spread) in spreads.items():
        noise = np.random.default_rng([zlib.crc32(name.encode()), seed]).standard_normal(out[name].shape)
        drawn = base * np.exp(spread * noise) if base else spread * noise
        out[name] = jnp.asarray(drawn.astype(out[name].dtype))
    for name, factor in factors.items():
        out[name] = (out[name] * factor).astype(out[name].dtype)
    return out
```

```python
import concourse.bass as bass
from concourse import mybir
from contextlib import ExitStack


def metaformer_block(nc, x, kv_reg_t, wqk, bqk, wv, bv, wo, bo, gate_t, w13a, w13b, w2, sw13, sw2,
                     ident, tri, mask_q, mask_k, token_ids, iota_e, iota_s, list_init, out):
    f32, bf16, i32 = mybir.dt.float32, mybir.dt.bfloat16, mybir.dt.int32
    ALU, ACT, AX = mybir.AluOpType, mybir.ActivationFunctionType, mybir.AxisListType
    ds = bass.ds

    D, SIDE, NB = 192, 48, 12
    BAND = 8 * SIDE
    T = NB * BAND
    NT = T // 128
    QR, QC, HALO = 8, 16, 3
    KR, KC = QR + 2 * HALO, QC + 2 * HALO
    NREG, H, E = 16, 12, 16
    NKEY = KR * KC
    CH = 110
    KW = 3 * CH
    PADT = HALO * SIDE
    KC0 = [min(max(QC * c - HALO, 0), SIDE - KC) for c in range(3)]
    EX, INTER = 16, 512
    SINTER = 1024
    SLOTS = 2 * T // 128 + EX
    V4 = 4
    XW = 256

    ctx = ExitStack()
    with ctx:
        def sem(name):
            return ctx.enter_context(nc.semaphore(name))

        def sems(name, n):
            return [sem(f"{name}{i}") for i in range(n)]

        v_dram = nc.dram_tensor("v_dram", (T + 2 * PADT, D), f32).ap()
        xn_dram = nc.dram_tensor("xn_dram", (T + 128, XW), f32).ap()
        xt_dram = nc.dram_tensor("xt_dram", (96, 2, T), f32).ap()
        acc_dram = nc.dram_tensor("acc_dram", (T + 128, D), f32).ap()
        list_dram = nc.dram_tensor("list_dram", (128 * SLOTS, 2), i32).ap()

        top = nc.sbuf_usable_end // 64 * 64 - 128
        cursor = [(nc.sbuf_base + 63) // 64 * 64]

        def place(name, shape, dt, at=None):
            size = 2 if dt == bf16 else 4
            for n in shape[1:]:
                size *= n
            size = (size + 31) // 32 * 32
            where = cursor[0] if at is None else at[0]
            t = nc.alloc_sbuf_tensor_at(name, shape, dt, offset=where)
            if at is None:
                cursor[0] += size
            else:
                at[0] += size
            return t

        wqk_sb = place("wqk_sb", [96, 2, 6, 128], f32)
        bqk_sb = place("bqk_sb", [128, 6], f32)
        wv_sb = place("wv_sb", [96, 2, D], f32)
        bv_sb = place("bv_sb", [128, D], f32)
        wo_sb = place("wo_sb", [96, 2, D], f32)
        bo_sb = place("bo_sb", [128, D], f32)
        gate_sb = place("gate_sb", [96, 2, E], f32)
        ident_sb = place("ident_sb", [128, 128], f32)
        tri_sb = place("tri_sb", [128, 2, 128], bf16)
        maskq_sb = place("maskq_sb", [128, 128], bf16)
        ids_sb = place("ids_sb", [128, NT], i32)
        iotae_sb = place("iotae_sb", [128, E], f32)
        iotas_sb = place("iotas_sb", [128, SLOTS], f32)
        logits = place("logits", [128, NT, E], f32)
        pair_idx = place("pair_idx", [128, NT, 2], i32)
        pair_val = place("pair_val", [128, NT, 2, 2], i32)
        slot_expert = place("slot_expert", [128, SLOTS], i32)
        lists = place("lists", [128, SLOTS, 2], i32)
        arena = cursor[0]
        at = [arena]
        kT = place("kT", [128, 3, T + 2 * PADT], f32, at)
        qT = place("qT", [128, 3, T], f32, at)
        stage = at[0]
        at = [arena]
        w13a_sb = place("w13a_sb", [128, EX, 2, INTER], f32, at)
        w13b_sb = place("w13b_sb", [128, EX, INTER], f32, at)
        s_h = place("s_h", [128, 8, BAND], f32, at)
        s_sg = place("s_sg", [128, 2, BAND], f32, at)
        assert at[0] <= stage

        at = [stage]
        a_x = place("a_x", [128, 2, 3, D], f32, at)
        a_xn = place("a_xn", [128, 2, 3, D], f32, at)
        a_xnT = place("a_xnT", [96, 2, 2, BAND], f32, at)
        a_v = place("a_v", [128, 2, 3, D], f32, at)
        a_st = place("a_st", [128, 3, 6], f32, at)
        a_mv = place("a_mv", [128, 3, 2], f32, at)
        a_ve = place("a_ve", [128, 3], f32, at)
        a_rs = place("a_rs", [128, 3], f32, at)
        minus_half = place("minus_half", [128, 3], f32, at)
        zeros = place("zeros", [128, 2 * D], f32, at)
        reg_t = place("reg_t", [96, 2, NREG], f32, at)
        reg_k = place("reg_k", [128, 3, NREG], f32, at)
        reg_v = place("reg_v", [NREG, D], f32, at)
        kst = place("kst", [128, 3, 3, KW], f32, at)
        qst = place("qst", [128, 3, 3, 128], f32, at)
        vst = place("vst", [128, 3, 3, D], f32, at)
        mst = place("mst", [128, 3, KW], bf16, at)
        probs = place("probs", [128, 2, 2, KW], f32, at)
        probsT = place("probsT", [128, 2, 2, 3 * 128], f32, at)
        nmax = place("nmax", [128, 2, 2], f32, at)
        sums = place("sums", [128, 3, H], f32, at)
        rsum = place("rsum", [128, H], f32, at)
        x_p = place("x_p", [128, 3, D], f32, at)
        xb = place("xb", [128, 3, D], f32, at)
        o_n = place("o_n", [128, D], f32, at)
        oT = place("oT", [96, 2, 128], f32, at)
        x2 = place("x2", [128, 3, D], f32, at)
        b_st = place("b_st", [128, 6], f32, at)
        b_mv = place("b_mv", [128, 2], f32, at)
        b_ve = place("b_ve", [128, 1], f32, at)
        b_rs = place("b_rs", [128, 1], f32, at)
        xn2 = place("xn2", [128, 3, XW], f32, at)
        xn2T = place("xn2T", [96, 3, 2, 128], f32, at)
        assert at[0] <= top, at[0]

        at = [stage]
        w2_sb = place("w2_sb", [128, EX, 4, D], f32, at)
        after_w2 = at[0]
        at = [stage]
        rt = [place(f"rt{i}", [128, NT, E], f32, at) for i in range(7)]
        rt_m = place("rt_m", [128, NT, E], bf16, at)
        rs1 = [place(f"rs1_{i}", [128, NT], f32, at) for i in range(4)]
        top_w = place("top_w", [128, NT, 2], f32, at)
        pos_f = place("pos_f", [128, NT, 2], f32, at)
        pos_i = place("pos_i", [128, NT, 2], i32, at)
        pos_hi = place("pos_hi", [128, NT, 2], i32, at)
        pos_lo = place("pos_lo", [128, NT, 2], i32, at)
        cnt_i = place("cnt_i", [128, E], i32, at)
        cnt = [place(f"cnt{i}", [128, E], f32, at) for i in range(4)]
        slot_cmp = place("slot_cmp", [128, SLOTS, E], f32, at)
        slot_f = place("slot_f", [128, SLOTS], f32, at)
        assert at[0] <= after_w2
        at = [after_w2]
        sw13_sb = place("sw13_sb", [96, 2, 2, SINTER], f32, at)
        sw2_sb = place("sw2_sb", [128, 8, D], f32, at)
        c_x = place("c_x", [96, 2, 2, BAND], f32, at)
        c_x2 = place("c_x2", [128, 3, D], f32, at)
        assert at[0] <= top, at[0]
        at = [after_w2]
        xg = place("xg", [128, V4, XW], f32, at)
        xa = place("xa", [128, 2, 128], f32, at)
        xb1 = place("xb1", [128, 2, 128], f32, at)
        xb3 = place("xb3", [128, 2, 128], f32, at)
        m_sg = place("m_sg", [128, 2, INTER], f32, at)
        m_h = place("m_h", [128, 2, INTER], f32, at)
        m_hT = place("m_hT", [128, 2, INTER], f32, at)
        ys = place("ys", [128, V4, D], f32, at)
        gidx = place("gidx", [128, V4, 1], i32, at)
        assert at[0] <= nc.sbuf_usable_end
        ps = ctx.enter_context(nc.psum_tensor("ps", [128, 8, 512], f32))

        s_const = sem("s_const")
        s_zero = sem("s_zero")
        s_pad = sem("s_pad")
        s_regin = sem("s_regin")
        r_ps = sem("r_ps")
        r_k = sem("r_k")
        r_v = sem("r_v")
        r_vout = sem("r_vout")
        r_vin = sem("r_vin")
        s_kpad = sem("s_kpad")
        a_xld = sems("a_xld", 2)
        a_var = sem("a_var")
        a_pow = sem("a_pow")
        b_var = sem("b_var")
        b_pow = sem("b_pow")
        s_half = sem("s_half")
        a_norm = sems("a_norm", 2)
        a_xTps = sems("a_xTps", 2)
        a_xnTev = sem("a_xnTev")
        a_qps = sems("a_qps", 2)
        a_qev = sems("a_qev", 2)
        a_kps = sems("a_kps", 2)
        a_kev = sems("a_kev", 2)
        a_vps = sems("a_vps", 2)
        a_vev = sems("a_vev", 2)
        a_vst = sems("a_vst", 2)
        dve_s = sem("dve_s")
        b_kq = sems("b_kq", 3)
        b_xld = sems("b_xld", 3)
        b_xb = sems("b_xb", 3)
        b_vld = sems("b_vld", 3)
        b_mld = sems("b_mld", 3)
        b_S = [sems(f"b_S{c}", 2) for c in range(3)]
        b_O = [sems(f"b_O{c}", 2) for c in range(3)]
        b_nm = sem("b_nm")
        b_exp = sems("b_exp", 2)
        b_T = sems("b_T", 2)
        b_TevD = sem("b_TevD")
        b_TevA = sem("b_TevA")
        b_on = sem("b_on")
        b_OTps = sem("b_OTps")
        b_OTev = sem("b_OTev")
        b_Pps = sem("b_Pps")
        b_x2 = sems("b_x2", 3)
        b_xn2 = sem("b_xn2")
        b_xTps = sem("b_xTps")
        b_xTev = sem("b_xTev")
        b_gps = sem("b_gps")
        b_lg = sem("b_lg")
        b_x2st = sems("b_x2st", 3)
        b_xn2st = sems("b_xn2st", 3)
        b_xTst = sems("b_xTst", 3)
        r_sub = sem("r_sub")
        r_exp = sem("r_exp")
        r_m = sem("r_m")
        r_rank = sem("r_rank")
        r_read = sem("r_read")
        r_done = sem("r_done")
        l_init = sem("l_init")
        l_cp = sem("l_cp")
        l_sc = sems("l_sc", 2)
        l_back = sem("l_back")
        c_w = sem("c_w")
        c_xld = sems("c_xld", 2)
        c_x2ld = sem("c_x2ld")
        c_a = sems("c_a", 2)
        c_b = sems("c_b", 2)
        c_silu = sems("c_silu", 2)
        c_h = sems("c_h", 2)
        c_zps = sems("c_zps", 2)
        c_z = sems("c_z", 2)
        c_acc = sem("c_acc")
        d_w = sem("d_w")
        d_half = sem("d_half")
        d_ix = sem("d_ix")
        d_g = sems("d_g", V4)
        d_xTps = sems("d_xTps", 2)
        d_xTev = sems("d_xTev", 2)
        d_a = sems("d_a", 2)
        d_b = sems("d_b", 2)
        d_silu = sems("d_silu", 2)
        d_h = sems("d_h", 2)
        d_hTps = sems("d_hTps", 2)
        d_hTev = sem("d_hTev")
        d_yps = sems("d_yps", 2)
        d_y = sem("d_y")
        d_sc = sems("d_sc", V4)
        s_out = sem("s_out")
        passed_pool = sem("passed_pool")
        passed_dve = sem("passed_dve")

        pair_stage = place("pair_stage", [128, 2, 2, 2], i32, [top])
        idx_stage = place("idx_stage", [128, 2, 2], i32, [top + 64])

        def patch(dram, i, c, w):
            return dram[ds(i * BAND, BAND), :].rearrange("(r c) d -> r c d", c=SIDE)[
                :, QC * c:QC * (c + 1), 0:w]

        def head(p, hh):
            h = 2 * p + hh
            return h // 4, 32 * (h % 4)

        def back(i, c):
            return (i, c - 1) if c else (i - 1, 2)

        def back2(i, c):
            return (i, 0) if c == 2 else (i - 1, c + 1)

        block = ctx.enter_context(nc.Block())

        @block.sync
        def _(sp):
            for dst, src in ((wqk_sb, wqk), (bqk_sb, bqk), (wv_sb, wv), (bv_sb, bv), (wo_sb, wo), (bo_sb, bo),
                             (gate_sb, gate_t), (ident_sb, ident), (tri_sb, tri.bitcast(bf16)),
                             (maskq_sb, mask_q.bitcast(bf16)),
                             (ids_sb, token_ids), (iotae_sb, iota_e), (iotas_sb, iota_s), (reg_t, kv_reg_t)):
                sp.dma_start(dst[:], src).then_inc(s_const, 16)
            sp.dma_start(list_dram.rearrange("(p s) w -> p (s w)", p=128), list_init).then_inc(l_init, 16)

            def load_band(n, u, j):
                sp.wait_ge(a_norm[u], j)
                sp.dma_start(a_x[:, u, :, :], x[ds(n * BAND, BAND), :].rearrange(
                    "(s p) d -> p s d", p=128)).then_inc(a_xld[u], 16)

            with sp.Fori(0, NB // 2) as j:
                for u in range(2):
                    load_band(2 * j + u, u, j)
            sp.wait_ge(s_zero, 1)
            sp.dma_start(v_dram[0:PADT, :].rearrange("(p a) d -> p (a d)", a=2),
                         zeros[0:PADT // 2, :]).then_inc(s_pad, 16)
            sp.dma_start(v_dram[PADT + T:2 * PADT + T, :].rearrange("(p a) d -> p (a d)", a=2),
                         zeros[0:PADT // 2, :]).then_inc(s_pad, 16)
            sp.dma_start(xn_dram[T:T + 128, :], zeros[:, 0:XW]).then_inc(s_pad, 16)
            sp.dma_start(acc_dram[T:T + 128, :], zeros[:, 0:D]).then_inc(s_pad, 16)
            sp.wait_ge(r_v, 1)
            sp.wait_ge(s_kpad, 4)
            for c in range(3):
                sp.dma_start(vst[NKEY - 2 * CH:NKEY - 2 * CH + NREG, c, 2, :], reg_v[:, :]).then_inc(r_vin, 16)
            sp.wait_ge(s_pad, 64)
            for u in range(2):
                sp.wait_ge(a_vst[u], 16 * NB // 2)

            def tile_in(i, c):
                sp.wait_ge(b_S[c][1], 3 * i)
                sp.dma_start(mst[:, c, :], mask_k[:, ds((i * 3 + c) * KW, KW)].bitcast(bf16)).then_inc(b_mld[c], 16)
                sp.wait_ge(b_xb[c], i)
                sp.dma_start(x_p[:, c, :], patch(x, i, c, D)).then_inc(b_xld[c], 16)
                sp.wait_ge(b_O[c][1], 3 * i)
                keys = v_dram[ds(i * BAND, KR * SIDE), :].rearrange("(r c) d -> r c d", c=SIDE)
                for k in range(3):
                    rows = min(5, KR - 5 * k)
                    sp.dma_start(vst[0:rows * KC, c, k, :],
                                 keys[5 * k:5 * k + rows, KC0[c]:KC0[c] + KC, :]).then_inc(b_vld[c], 16)

            def tile_out(i, c):
                m = 3 * i + c
                sp.wait_ge(b_x2[c], i + 1)
                sp.dma_start(patch(acc_dram, i, c, D), x2[:, c, :]).then_inc(b_x2st[c], 16)
                sp.wait_ge(b_xn2, 2 * m + 2)
                sp.dma_start(patch(xn_dram, i, c, XW), xn2[:, c, :]).then_inc(b_xn2st[c], 16)
                sp.wait_ge(b_xTev, m + 1)
                sp.dma_start(xt_dram[:, :, ds(m * 128, 128)], xn2T[:, c, :, :]).then_inc(b_xTst[c], 16)

            sp.wait_ge(r_vin, 48)
            for c in range(3):
                tile_in(0, c)
                if c == 2:
                    tile_out(*back2(0, c))
            with sp.Fori(1, NB) as i:
                for c in range(3):
                    tile_in(i, c)
                    tile_out(*back2(i, c))
            tile_out(NB - 1, 1)
            tile_out(NB - 1, 2)

            sp.wait_ge(b_gps, NT)
            sp.wait_ge(b_lg, NT)
            for c in range(3):
                sp.wait_ge(b_x2st[c], 16 * NB)
                sp.wait_ge(b_xn2st[c], 16 * NB)
                sp.wait_ge(b_xTst[c], 16 * NB)
            sp.dma_start(sw13_sb[:], sw13).then_inc(c_w, 16)
            sp.dma_start(sw2_sb[:], sw2).then_inc(c_w, 16)

            def c_rest(n, u, j, weights):
                sp.wait_ge(c_acc, 48 * n)
                for s in range(3):
                    sp.dma_start(c_x2[:, s, :], patch(acc_dram, n, s, D)).then_inc(c_x2ld, 16)
                if weights:
                    e = 2 * n
                    sp.dma_start(w13a_sb[:, ds(e, 2), :, :], w13a[:, ds(e, 2), :, :]).then_inc(d_w, 16)
                    sp.dma_start(w13b_sb[:, ds(e, 2), :], w13b[:, ds(e, 2), :]).then_inc(d_w, 16)
                    sp.dma_start(w2_sb[:, ds(e, 2), :, :], w2[:, ds(e, 2), :, :]).then_inc(d_w, 16)
                for s in range(3):
                    w = 3 * u + s
                    sp.wait_ge(c_z[w % 2], 3 * j + w // 2 + 1)
                    sp.dma_start(patch(acc_dram, n, s, D), c_x2[:, s, :]).then_inc(c_acc, 16)

            sp.dma_start(c_x[:, 0, :, :], xt_dram[:, :, 0:BAND]).then_inc(c_xld[0], 16)
            sp.dma_start(c_x[:, 1, :, :], xt_dram[:, :, BAND:2 * BAND]).then_inc(c_xld[1], 16)
            sp.wait_ge(r_done, 1)

            def c_step(j, weights, more):
                for u in range(2):
                    n = 2 * j + u
                    c_rest(n, u, j, weights)
                    if more:
                        sp.dma_start(c_x[:, u, :, :],
                                     xt_dram[:, :, ds((n + 2) * BAND, BAND)]).then_inc(c_xld[u], 16)

            with sp.Fori(0, EX // 4) as j:
                c_step(j, True, True)
            c_step(4, False, True)
            c_step(5, False, False)

            for v in range(V4):
                sp.wait_ge(d_sc[v], 16 * SLOTS // V4)
            sp.dma_start(out, acc_dram[0:T, :]).then_inc(s_out, 16)
            sp.wait_ge(s_out, 16)

        @block.gpsimd
        def _(pool):
            nc.gpsimd.memset(zeros[:], 0.0).then_inc(s_zero, 1)
            nc.gpsimd.memset(kT[:, :, 0:PADT], 0.0).then_inc(s_kpad, 1)
            nc.gpsimd.memset(kT[:, :, PADT + T:], 0.0).then_inc(s_kpad, 1)
            nc.gpsimd.memset(vst[:, :, 2, :], 0.0).then_inc(s_kpad, 1)
            nc.gpsimd.memset(kst[:, :, :, NKEY + NREG:], 0.0).then_inc(s_kpad, 1)

            nc.gpsimd.memset(minus_half[:], -0.5).then_inc(s_half, 1)
            pool.wait_ge(s_half, 1)
            with pool.Fori(0, NB // 2) as j:
                for u in range(2):
                    pool.wait_ge(a_var, 2 * j + u + 1)
                    nc.gpsimd.tensor_tensor(a_rs[:, :], a_ve[:, :], minus_half[:, :], ALU.pow).then_inc(a_pow, 1)
                    pool.wait_ge(a_vev[0], 3 * j + 2 + u)
                    pool.wait_ge(a_vev[1], 3 * j + 1 + 2 * u)
                    pool.dma_start(v_dram[ds(PADT + (2 * j + u) * BAND, BAND), :].rearrange(
                        "(s p) d -> p s d", p=128), a_v[:, u, :, :]).then_inc(a_vst[u], 16)

            pool.wait_ge(r_k, 3)
            for c in range(3):
                nc.gpsimd.tensor_copy(kst[:, c, :, NKEY:NKEY + NREG], reg_k[:, :, :]).then_inc(s_kpad, 1)
            for r in range(2):
                pool.wait_ge(a_qev[r], 3 * NB // 2)
                pool.wait_ge(a_kev[r], 3 * NB // 2)
            pool.wait_ge(s_const, 16 * 14)

            def root(i, c):
                pool.wait_ge(b_var, 3 * i + c + 1)
                nc.gpsimd.tensor_tensor(b_rs[:, :], b_ve[:, :], minus_half[:, 0:1], ALU.pow).then_inc(b_pow, 1)

            def stage_tile(i, c):
                pool.wait_ge(b_S[c][1], 3 * i)
                keys = kT[:, :, ds(i * BAND, KR * SIDE)].rearrange("p g (r c) -> p g r c", c=SIDE)
                nc.gpsimd.tensor_copy(kst[:, c, :, 0:NKEY].rearrange("p g (r c) -> p g r c", c=KC),
                                      keys[:, :, :, KC0[c]:KC0[c] + KC]).then_inc(b_kq[c], 1)
                q = qT[:, :, ds(i * BAND, BAND)].rearrange("p g (r c) -> p g r c", c=SIDE)
                nc.gpsimd.tensor_copy(qst[:, c, :, :].rearrange("p g (r c) -> p g r c", c=QC),
                                      q[:, :, :, QC * c:QC * (c + 1)]).then_inc(b_kq[c], 1)
                pool.wait_ge(b_xld[c], 16 * i + 16)
                pool.wait_ge(b_x2[c], i)
                nc.gpsimd.tensor_tensor(xb[:, c, :], x_p[:, c, :], bo_sb[:, :], ALU.add).then_inc(b_xb[c], 1)

            for c in range(3):
                stage_tile(0, c)
            root(0, 0)
            with pool.Fori(1, NB) as i:
                for c in range(3):
                    stage_tile(i, c)
                    root(*back2(i, c))
            root(NB - 1, 1)
            root(NB - 1, 2)

            pool.wait_ge(r_done, 1)
            pool.wait_ge(l_init, 16)
            with pool.Fori(0, NT // 2) as j:
                for u in range(2):
                    n = 2 * j + u
                    pool.wait_ge(l_sc[u], 32 * j)
                    nc.gpsimd.tensor_copy(idx_stage[:, u, :], pair_idx[:, ds(n, 1), :].squeeze(1)).then_inc(l_cp, 1)
                    nc.gpsimd.tensor_copy(pair_stage[:, u, :, :].rearrange("p a b -> p (a b)"), pair_val[:, ds(n, 1), :, :].rearrange("p n a b -> p (n a b)")).then_inc(l_cp, 1)
                    pool.wait_ge(l_cp, 2 * n + 2)
                    pool.sem_inc(passed_pool, 1)
                    for k in range(2):
                        nc.gpsimd.indirect_dma_start(
                            list_dram, bass.IndirectOffsetOnAxis(ap=idx_stage[:, u, k:k + 1], axis=0),
                            pair_stage[:, u, k, :], None).then_inc(l_sc[u], 16)
            for u in range(2):
                pool.wait_ge(l_sc[u], 32 * NT // 2)
            pool.dma_start(lists[:, :, :].rearrange("p s w -> p (s w)"),
                           list_dram.rearrange("(p s) w -> p (s w)", p=128)).then_inc(l_back, 16)
            pool.wait_ge(l_back, 16)
            for r in range(2):
                pool.wait_ge(c_z[r], 3 * NB // 2)
            pool.wait_ge(c_acc, 48 * NB)
            nc.gpsimd.memset(xb1[64:128, :, :], 0.0).then_inc(d_half, 1)
            pool.wait_ge(d_half, 1)
            nc.gpsimd.memset(xb3[0:64, :, :], 0.0).then_inc(d_half, 1)
            pool.wait_ge(d_half, 2)

            def gather(j, v, g):
                pool.wait_ge(d_sc[v], 16 * g)
                nc.gpsimd.tensor_copy(gidx[:, v, :], lists[:, ds(j, 1), 0]).then_inc(d_ix, 1)
                pool.wait_ge(d_ix, j + 1)
                pool.wait_ge(d_xTps[v % 2], 2 * g + v // 2)
                pool.sem_inc(passed_pool, 1)
                nc.gpsimd.indirect_dma_start(xg[:, v, :], None, xn_dram, bass.IndirectOffsetOnAxis(
                    ap=gidx[:, v, 0:1], axis=0)).then_inc(d_g[v], 16)

            def add_rows(j, v, g, first=False):
                pool.wait_ge(d_y, j + 1)
                if not first:
                    pool.wait_ge(d_sc[(v - 1) % V4], 16 * (g if v == 0 else g + 1))
                pool.sem_inc(passed_pool, 1)
                nc.gpsimd.indirect_dma_start(acc_dram, bass.IndirectOffsetOnAxis(
                    ap=gidx[:, v, 0:1], axis=0), ys[:, v, :], None, compute_op=ALU.add).then_inc(d_sc[v], 16)

            gather(0, 0, 0)
            gather(1, 1, 0)

            def d_step(g, first, last):
                for v in range(V4):
                    j = V4 * g + v
                    if not (last and v >= V4 - 2):
                        gather(j + 2, (v + 2) % V4, g + (v + 2) // V4)
                    if v:
                        add_rows(j - 1, v - 1, g, first and v == 1)
                    elif not first:
                        add_rows(j - 1, V4 - 1, g - 1)

            d_step(0, True, False)
            with pool.Fori(1, SLOTS // V4 - 1) as g:
                d_step(g, False, False)
            d_step(SLOTS // V4 - 1, False, True)
            add_rows(SLOTS - 1, V4 - 1, SLOTS // V4 - 1)

        @block.scalar
        def _(act):
            act.wait_ge(s_const, 16 * 14)
            act.wait_ge(r_ps, 1)
            for g in range(3):
                nc.scalar.activation(reg_k[:, g, :], ps[:, 2, NREG * g:NREG * (g + 1)], ACT.Identity,
                                     bias=bqk_sb[:, 3 + g:4 + g]).then_inc(r_k, 1)
            with act.Fori(0, NB // 2) as j:
                for u in range(2):
                    act.wait_ge(a_xTps[u], j + 1)
                    nc.scalar.copy(a_xnT[:, u, :, :], ps[0:96, 0:2, 0:BAND]).then_inc(a_xnTev, 1)
                    for g in range(3):
                        w = 3 * u + g
                        act.wait_ge(a_kps[w % 2], 3 * j + w // 2 + 1)
                        nc.scalar.activation(kT[:, g, ds(PADT + (2 * j + u) * BAND, BAND)],
                                             ps[:, 4 + w % 2, 0:BAND], ACT.Identity,
                                             bias=bqk_sb[:, 3 + g:4 + g]).then_inc(a_kev[w % 2], 1)

            def probsT_odd(i, c, p):
                m = 6 * (3 * i + c) + p
                act.wait_ge(b_T[1], m + 1)
                before = back(i, c) if p < 2 else (i, c)
                if type(i) is not int or i or c or p >= 2:
                    act.wait_ge(b_O[before[1]][p % 2], 3 * before[0] + (3 if p < 2 else p // 2))
                nc.scalar.copy(probsT[0:CH, p % 2, 1, :], ps[0:CH, 5, 0:3 * 128]).then_inc(b_TevA, 1)

            def b_tile(i, c, first=False):
                n = 3 * i + c
                bi, bc = back(i, c)
                for p in range(6):
                    if p:
                        probsT_odd(i, c, p - 1)
                    elif not first:
                        probsT_odd(bi, bc, 5)
                    act.wait_ge(b_nm, 6 * n + p + 1)
                    for hh in range(2):
                        ins = nc.scalar.activation(probs[:, p % 2, hh, :], ps[:, 2 * (p % 2) + hh, 0:KW], ACT.Exp,
                                                   bias=nmax[:, p % 2, hh:hh + 1],
                                                   accum_out=sums[:, c, 2 * p + hh:2 * p + hh + 1])
                    ins.then_inc(b_exp[p % 2], 1)
                    if p == 2 and not first:
                        tail_oT(n - 1)
                    if p == 5 and not first:
                        tail_xT(bi, bc)

            def tail_oT(m):
                act.wait_ge(b_OTps, m + 1)
                act.wait_ge(b_Pps, m)
                nc.scalar.copy(oT[:, :, :].rearrange("p a b -> p (a b)"), ps[0:96, 7, 0:256]).then_inc(b_OTev, 1)

            def tail_xT(i, c):
                act.wait_ge(b_xTps, 3 * i + c + 1)
                act.wait_ge(b_xTst[c], 16 * i)
                nc.scalar.copy(xn2T[:, c, :, :].rearrange("p a b -> p (a b)"),
                               ps[0:96, 7, 0:256]).then_inc(b_xTev, 1)

            b_tile(0, 0, True)
            b_tile(0, 1)
            b_tile(0, 2)
            with act.Fori(1, NB) as i:
                for c in range(3):
                    b_tile(i, c)
            probsT_odd(NB - 1, 2, 5)
            tail_oT(NT - 1)
            tail_xT(NB - 1, 2)

            act.wait_ge(r_sub, 1)
            nc.scalar.activation(rt[1][:], rt[0][:], ACT.Exp).then_inc(r_exp, 1)

            with act.Fori(0, NB) as n:
                for m in range(8):
                    act.wait_ge(c_a[m % 2], 4 * n + m // 2 + 1)
                    act.wait_ge(c_h[m % 2], 4 * n + m // 2)
                    nc.scalar.activation(s_sg[:, m % 2, :], ps[:, m % 2, 0:BAND],
                                         ACT.Silu).then_inc(c_silu[m % 2], 1)

            def xT_split(v, g):
                q = 2 * g + v // 2
                act.wait_ge(d_xTps[v % 2], q + 1)
                act.wait_ge(d_b[v % 2], q)
                bank = 6 + v % 2
                nc.scalar.copy(xa[:, v % 2, :], ps[:, bank, 0:128]).then_inc(d_xTev[v % 2], 1)
                nc.scalar.copy(xb1[0:64, v % 2, :], ps[0:64, bank, 128:256]).then_inc(d_xTev[v % 2], 1)
                nc.scalar.copy(xb3[64:128, v % 2, :], ps[64:128, bank, 128:256]).then_inc(d_xTev[v % 2], 1)

            def d_step(g, last):
                for v in range(V4):
                    q = 2 * g + v // 2
                    act.wait_ge(d_a[v % 2], q + 1)
                    act.wait_ge(d_h[v % 2], q)
                    nc.scalar.activation(m_sg[:, v % 2, :], ps[:, v % 2, :], ACT.Silu).then_inc(d_silu[v % 2], 1)
                    if not (last and v == V4 - 1):
                        xT_split((v + 1) % V4, g + (v + 1) // V4)

            xT_split(0, 0)
            with act.Fori(0, SLOTS // V4 - 1) as g:
                d_step(g, False)
            d_step(SLOTS // V4 - 1, True)

        @block.vector
        def _(dve):
            steps = [0]

            def step(ins, base=0):
                steps[0] += 1
                ins.then_inc(dve_s, 1)
                dve.wait_ge(dve_s, base + steps[0])

            dve.wait_ge(s_const, 16 * 14)
            dve.wait_ge(r_ps, 1)
            nc.vector.tensor_tensor(reg_v[:, :], ps[0:NREG, 3, 0:D], bv_sb[0:NREG, :], ALU.add).then_inc(r_v, 1)

            A_STEPS = 2
            with dve.Fori(0, NB // 2) as j:
                for u in range(2):
                    base = 2 * A_STEPS * j
                    n = 2 * j + u
                    dve.wait_ge(a_xld[u], 16 * j + 16)
                    for s in range(3):
                        ins = nc.vector.bn_stats(a_st[:, s, :], a_x[:, u, s, :])
                    step(ins, base)
                    dve.sem_inc(passed_dve, 1)
                    for s in range(3):
                        ins = nc.vector.bn_aggr(a_mv[:, s, :], a_st[:, s, :])
                    step(ins, base)
                    nc.vector.tensor_scalar(a_ve[:, :], a_mv[:, :, 1], 1e-6, None, ALU.add).then_inc(a_var, 1)
                    dve.wait_ge(a_pow, n + 1)
                    dve.wait_ge(a_xTps[u], j)
                    for s in range(3):
                        ins = nc.vector.tensor_scalar(a_xn[:, u, s, :], a_x[:, u, s, :], a_mv[:, s, 0:1],
                                                      a_rs[:, s:s + 1], ALU.subtract, ALU.mult)
                    ins.then_inc(a_norm[u], 1)
                    dve.wait_ge(a_vst[u], 16 * j)
                    for s in range(3):
                        w = 3 * u + s
                        dve.wait_ge(a_vps[w % 2], 3 * j + w // 2 + 1)
                        nc.vector.tensor_tensor(a_v[:, u, s, :], ps[:, 6 + w % 2, 0:D], bv_sb[:, :],
                                                ALU.add).then_inc(a_vev[w % 2], 1)
                    for g in range(3):
                        w = 3 * u + g
                        dve.wait_ge(a_qps[w % 2], 3 * j + w // 2 + 1)
                        nc.vector.tensor_scalar(qT[:, g, ds(n * BAND, BAND)], ps[:, 2 + w % 2, 0:BAND],
                                                bqk_sb[:, g:g + 1], 0.25, ALU.add, ALU.mult
                                                ).then_inc(a_qev[w % 2], 1)
            base_b = NB * A_STEPS
            B_STEPS = 3

            def probsT_even(i, c, p):
                m = 6 * (3 * i + c) + p
                dve.wait_ge(b_T[0], m + 1)
                before = back(i, c) if p < 2 else (i, c)
                if type(i) is not int or i or c or p >= 2:
                    dve.wait_ge(b_O[before[1]][p % 2], 3 * before[0] + (3 if p < 2 else p // 2))
                nc.vector.tensor_copy(probsT[0:CH, p % 2, 0, :], ps[0:CH, 4, 0:3 * 128]).then_inc(b_TevD, 1)

            def tail_o(i, c):
                m = 3 * i + c
                steps[0] = 0
                dve.wait_ge(b_O[c][1], 3 * i + 3)
                step(nc.vector.reciprocal(rsum[:, :], sums[:, c, :]), base_b + B_STEPS * m)
                dve.wait_ge(b_OTps, m)
                nc.vector.tensor_tensor(o_n[:, :].rearrange("p (h e) -> p h e", e=16),
                                        ps[:, 6, 0:D].rearrange("p (h e) -> p h e", e=16),
                                        rsum[:, :].unsqueeze(2).broadcast_to([128, H, 16]),
                                        ALU.mult).then_inc(b_on, 1)

            def tail_x2(i, c):
                m = 3 * i + c
                steps[0] = 1
                base = base_b + B_STEPS * m
                dve.wait_ge(b_Pps, m + 1)
                dve.wait_ge(b_xb[c], i + 1)
                dve.wait_ge(b_x2st[c], 16 * i)
                nc.vector.tensor_tensor(x2[:, c, :], ps[:, 7, 0:D], xb[:, c, :], ALU.add).then_inc(b_x2[c], 1)
                dve.wait_ge(b_x2[c], i + 1)
                step(nc.vector.bn_stats(b_st[:, :], x2[:, c, :]), base)
                dve.sem_inc(passed_dve, 1)
                step(nc.vector.bn_aggr(b_mv[:, :], b_st[:, :]), base)
                nc.vector.tensor_scalar(b_ve[:, :], b_mv[:, 1:2], 1e-5, None, ALU.add).then_inc(b_var, 1)

            def tail_norm(i, c):
                dve.wait_ge(b_pow, 3 * i + c + 1)
                dve.wait_ge(b_xn2st[c], 16 * i)
                for lo, hi, at0 in ((0, D, 0), (128, D, D)):
                    nc.vector.tensor_scalar(xn2[:, c, at0:at0 + hi - lo], x2[:, c, lo:hi], b_mv[:, 0:1],
                                            b_rs[:, 0:1], ALU.subtract, ALU.mult).then_inc(b_xn2, 1)

            def tail_logits(m):
                dve.wait_ge(b_gps, m + 1)
                nc.vector.tensor_copy(logits[:, ds(m, 1), :].squeeze(1), ps[:, 7, 0:E]).then_inc(b_lg, 1)

            def b_tile(i, c, first=False, second=False):
                n = 3 * i + c
                bi, bc = back(i, c)
                for p in range(6):
                    dve.wait_ge(b_S[c][p % 2], 3 * i + p // 2 + 1)
                    nc.vector.tensor_reduce(nmax[:, p % 2, :], ps[:, 2 * (p % 2):2 * (p % 2) + 2, 0:KW],
                                            AX.X, ALU.max, negate=True).then_inc(b_nm, 1)
                    if p:
                        probsT_even(i, c, p - 1)
                    elif not first:
                        probsT_even(bi, bc, 5)
                    if p == 1 and not first:
                        if not second:
                            tail_logits(n - 2)
                        tail_o(bi, bc)
                    if p == 4 and not first:
                        tail_x2(bi, bc)
                    if p == 5 and not first:
                        tail_norm(bi, bc)

            b_tile(0, 0, True)
            b_tile(0, 1, False, True)
            b_tile(0, 2)
            with dve.Fori(1, NB) as i:
                for c in range(3):
                    b_tile(i, c)
            probsT_even(NB - 1, 2, 5)
            tail_logits(NT - 2)
            tail_o(NB - 1, 2)
            tail_x2(NB - 1, 2)
            tail_norm(NB - 1, 2)
            tail_logits(NT - 1)

            dve.wait_ge(b_lg, NT)
            steps[0] = 0
            base_r = base_b + B_STEPS * NT

            def s_(ins):
                step(ins, base_r)

            def wide(a):
                return a[:, :].unsqueeze(2).broadcast_to([128, NT, E])

            def narrow(a):
                return a.unsqueeze(1).broadcast_to([128, NT, E])

            for c in range(3):
                dve.wait_ge(b_x2st[c], 16 * NB)
                dve.wait_ge(b_xn2st[c], 16 * NB)
                dve.wait_ge(b_xTst[c], 16 * NB)
            s_(nc.vector.tensor_reduce(rs1[0][:], logits[:], AX.X, ALU.max))
            nc.vector.tensor_tensor(rt[0][:], logits[:], wide(rs1[0]), ALU.subtract).then_inc(r_sub, 1)
            dve.wait_ge(r_exp, 1)
            s_(nc.vector.tensor_reduce(rs1[0][:], rt[1][:], AX.X, ALU.add))
            s_(nc.vector.reciprocal(rs1[1][:], rs1[0][:]))
            s_(nc.vector.tensor_tensor(rt[0][:], rt[1][:], wide(rs1[1]), ALU.mult))
            for k in range(2):
                one_hot = rt[3 + k]
                s_(nc.vector.tensor_reduce(top_w[:, :, k], rt[0][:], AX.X, ALU.max))
                s_(nc.vector.tensor_tensor(rt[1][:], rt[0][:],
                                           top_w[:, :, k:k + 1].broadcast_to([128, NT, E]), ALU.not_equal))
                s_(nc.vector.scalar_tensor_tensor(rt[2][:], rt[1][:], float(2 * E), narrow(iotae_sb[:, :]),
                                                  ALU.mult, ALU.add))
                s_(nc.vector.tensor_reduce(rs1[2][:], rt[2][:], AX.X, ALU.min))
                s_(nc.vector.tensor_tensor(one_hot[:], narrow(iotae_sb[:, :]), wide(rs1[2]), ALU.is_equal))
                if k == 0:
                    s_(nc.vector.scalar_tensor_tensor(rt[0][:], one_hot[:], -2.0, rt[0][:], ALU.mult, ALU.add))
            nc.vector.tensor_tensor(rt_m[:], rt[3][:], rt[4][:], ALU.add).then_inc(r_m, 1)
            dve.wait_ge(r_rank, 1)
            nhalf = NT // 2
            s_(nc.vector.tensor_copy(rt[0][:].rearrange("p (a n) e -> p a (n e)", a=2), ps[:, 2:4, 0:nhalf * E]))
            src, dst = rt[0], rt[1]
            d = 1
            while d < NT:
                nc.vector.tensor_copy(dst[:, 0:d, :], src[:, 0:d, :])
                s_(nc.vector.tensor_tensor(dst[:, d:, :], src[:, d:, :], src[:, 0:NT - d, :], ALU.add))
                src, dst = dst, (rt[2] if dst is rt[1] else rt[1])
                d *= 2
            incl = src
            s_(nc.vector.tensor_scalar(cnt_i[:, :], incl[:, NT - 1, :], 127.0, None, ALU.add))
            s_(nc.vector.tensor_scalar(cnt_i[:, :], cnt_i[:, :], 7, None, ALU.arith_shift_right))
            s_(nc.vector.tensor_copy(cnt[0][:, :], cnt_i[:, :]))
            a, b = cnt[0], cnt[1]
            d = 1
            while d < E:
                nc.vector.tensor_copy(b[:, 0:d], a[:, 0:d])
                s_(nc.vector.tensor_tensor(b[:, d:], a[:, d:], a[:, 0:E - d], ALU.add))
                a, b = b, (cnt[2] if b is cnt[1] else cnt[1])
                d *= 2
            ends = a
            s_(nc.vector.tensor_tensor(cnt[3][:, :], ends[:, :], cnt[0][:, :], ALU.subtract))
            s_(nc.vector.tensor_tensor(rt[5][:], incl[:], rt[0][:], ALU.subtract))
            s_(nc.vector.scalar_tensor_tensor(rt[5][:], narrow(cnt[3][:, :]), 128.0, rt[5][:], ALU.mult, ALU.add))
            s_(nc.vector.tensor_tensor(rt[5][:].rearrange("p (a n) e -> p a (n e)", a=2),
                                       rt[5][:].rearrange("p (a n) e -> p a (n e)", a=2),
                                       ps[:, 0:2, 0:nhalf * E], ALU.add))
            for k in range(2):
                s_(nc.vector.tensor_tensor(rt[6][:], rt[3 + k][:], rt[5][:], ALU.mult))
                s_(nc.vector.tensor_reduce(pos_f[:, :, k], rt[6][:], AX.X, ALU.add))
            s_(nc.vector.tensor_copy(pos_i[:], pos_f[:]))
            nc.vector.tensor_scalar(pos_hi[:], pos_i[:], 7, None, ALU.arith_shift_right)
            s_(nc.vector.tensor_scalar(pos_lo[:], pos_i[:], 127, None, ALU.bitwise_and))
            s_(nc.vector.scalar_tensor_tensor(pair_idx[:], pos_lo[:], float(SLOTS), pos_hi[:], ALU.mult, ALU.add))
            for k in range(2):
                nc.vector.tensor_copy(pair_val[:, :, k, 0], ids_sb[:, :])
            s_(nc.vector.tensor_copy(pair_val[:, :, :, 1].bitcast(f32), top_w[:, :, :]))
            s_(nc.vector.tensor_tensor(slot_cmp[:], iotas_sb[:, :].unsqueeze(2).broadcast_to([128, SLOTS, E]),
                                       ends[:, :].unsqueeze(1).broadcast_to([128, SLOTS, E]), ALU.is_ge))
            s_(nc.vector.tensor_reduce(slot_f[:], slot_cmp[:], AX.X, ALU.add))
            nc.vector.tensor_scalar(slot_expert[:], slot_f[:], float(EX - 1), None, ALU.min).then_inc(r_done, 1)

            with dve.Fori(0, NB // 2) as j:
                for u in range(2):
                    n = 2 * j + u
                    for m in range(8):
                        dve.wait_ge(c_silu[m % 2], 4 * n + m // 2 + 1)
                        dve.wait_ge(c_b[m % 2], 4 * n + m // 2 + 1)
                        nc.vector.tensor_tensor(s_h[:, m, :], s_sg[:, m % 2, :], ps[:, 2 + m % 2, 0:BAND],
                                                ALU.mult).then_inc(c_h[m % 2], 1)
                    for s in range(3):
                        w = 3 * u + s
                        dve.wait_ge(c_zps[w % 2], 3 * j + w // 2 + 1)
                        dve.wait_ge(c_x2ld, 48 * n + 48)
                        nc.vector.tensor_tensor(c_x2[:, s, :], ps[:, 4 + w % 2, 0:D], c_x2[:, s, :],
                                                ALU.add).then_inc(c_z[w % 2], 1)

            dve.wait_ge(d_half, 2)
            dve.wait_ge(l_back, 16)

            def hT_out(v, g):
                q = 2 * g + v // 2
                dve.wait_ge(d_hTps[v % 2], q + 1)
                dve.wait_ge(d_yps[v % 2], q)
                nc.vector.tensor_copy(m_hT[:, v % 2, :], ps[:, 4, :]).then_inc(d_hTev, 1)

            def y_out(j, v, g):
                dve.wait_ge(d_yps[v % 2], 2 * g + v // 2 + 1)
                dve.wait_ge(d_sc[v], 16 * g)
                nc.vector.tensor_scalar(ys[:, v, :], ps[:, 5, 0:D], lists[:, ds(j, 1), 1].bitcast(f32), None,
                                        ALU.mult).then_inc(d_y, 1)

            def d_step(g, first):
                for v in range(V4):
                    q = 2 * g + v // 2
                    pv, pg = ((v - 1), g) if v else (V4 - 1, g - 1)
                    if not (first and v == 0):
                        hT_out(pv, pg)
                    dve.wait_ge(d_silu[v % 2], q + 1)
                    dve.wait_ge(d_b[v % 2], q + 1)
                    dve.wait_ge(d_hTps[v % 2], q)
                    nc.vector.tensor_tensor(m_h[:, v % 2, :], m_sg[:, v % 2, :], ps[:, 2 + v % 2, :],
                                            ALU.mult).then_inc(d_h[v % 2], 1)
                    if not (first and v == 0):
                        y_out(V4 * g + v - 1, pv, pg)

            d_step(0, True)
            with dve.Fori(1, SLOTS // V4) as g:
                d_step(g, False)
            hT_out(V4 - 1, SLOTS // V4 - 1)
            y_out(SLOTS - 1, V4 - 1, SLOTS // V4 - 1)

        @block.tensor
        def _(pe):
            mm, tr = nc.tensor.matmul, nc.tensor.transpose
            pe.wait_ge(s_const, 16 * 14)
            for g in range(3):
                for c in range(2):
                    mm(ps[:, 2, NREG * g:NREG * (g + 1)], wqk_sb[:, c, 3 + g, :], reg_t[:, c, :],
                       start=c == 0, stop=c == 1)
            for c in range(2):
                ins = mm(ps[0:NREG, 3, 0:D], reg_t[:, c, :], wv_sb[:, c, :], start=c == 0, stop=c == 1)
            ins.then_inc(r_ps, 1)
            pe.wait_ge(r_k, 3)
            pe.wait_ge(r_v, 1)

            with pe.Fori(0, NB // 2) as j:
                for u in range(2):
                    n = 2 * j + u
                    pe.wait_ge(a_norm[u], j + 1)
                    pe.wait_ge(a_xnTev, n)
                    for c in range(2):
                        for s in range(3):
                            ins = tr(ps[0:96, c, 128 * s:128 * (s + 1)], a_xn[:, u, s, 96 * c:96 * (c + 1)],
                                     ident_sb[:, :])
                    ins.then_inc(a_xTps[u], 1)
                    pe.wait_ge(a_xnTev, n + 1)
                    for s in range(3):
                        w = 3 * u + s
                        pe.wait_ge(a_vev[w % 2], 3 * j + w // 2)
                        for c in range(2):
                            ins = mm(ps[:, 6 + w % 2, 0:D], a_xnT[:, u, c, 128 * s:128 * (s + 1)],
                                     wv_sb[:, c, :], start=c == 0, stop=c == 1)
                        ins.then_inc(a_vps[w % 2], 1)
                    for g in range(6):
                        w = 3 * u + g // 2
                        made, used, bank = ((a_qps, a_qev, 2), (a_kps, a_kev, 4))[g % 2]
                        pe.wait_ge(used[w % 2], 3 * j + w // 2)
                        for c in range(2):
                            ins = mm(ps[:, bank + w % 2, 0:BAND], wqk_sb[:, c, 3 * (g % 2) + g // 2, :],
                                     a_xnT[:, u, c, :], start=c == 0, stop=c == 1)
                        ins.then_inc(made[w % 2], 1)
            for r in range(2):
                for done in (a_qev, a_kev, a_vev):
                    pe.wait_ge(done[r], 3 * NB // 2)
            pe.wait_ge(s_kpad, 7)

            def scores(i, c, p):
                n = 3 * i + c
                if p == 0:
                    pe.wait_ge(b_kq[c], 2 * i + 2)
                    pe.wait_ge(b_mld[c], 16 * i + 16)
                pe.wait_ge(b_exp[p % 2], 3 * n + p // 2)
                for hh in range(2):
                    g, r = head(p, hh)
                    bank = 2 * (p % 2) + hh
                    mm(ps[:, bank, 0:KW], maskq_sb[r:r + 24, :], mst[r:r + 24, c, :], start=True, stop=False)
                    ins = mm(ps[:, bank, 0:KW], qst[r:r + 16, c, g, :], kst[r:r + 16, c, g, :],
                             start=False, stop=True)
                ins.then_inc(b_S[c][p % 2], 1)

            def probs_T(i, c, p):
                n = 3 * i + c
                pe.wait_ge(b_exp[p % 2], 3 * n + p // 2 + 1)
                for hh in range(2):
                    pe.wait_ge((b_TevD, b_TevA)[hh], 6 * n + p)
                    for k in range(3):
                        ins = tr(ps[0:CH, 4 + hh, 128 * k:128 * (k + 1)], probs[:, p % 2, hh, CH * k:CH * (k + 1)],
                                 ident_sb[:, :])
                    ins.then_inc(b_T[hh], 1)

            def values(i, c, p):
                n = 3 * i + c
                if p == 0:
                    pe.wait_ge(b_vld[c], 48 * i + 48)
                    pe.wait_ge(b_on, n)
                for hh in range(2):
                    pe.wait_ge((b_TevD, b_TevA)[hh], 6 * n + p + 1)
                    h = 2 * p + hh
                    for k in range(3):
                        ins = mm(ps[:, 6, 16 * h:16 * h + 16], probsT[0:CH, p % 2, hh, 128 * k:128 * (k + 1)],
                                 vst[0:CH, c, k, 16 * h:16 * h + 16], start=k == 0, stop=k == 2)
                ins.then_inc(b_O[c][p % 2], 1)

            def tail_oT(m):
                pe.wait_ge(b_on, m + 1)
                pe.wait_ge(b_lg, m)
                for c in range(2):
                    ins = tr(ps[0:96, 7, 128 * c:128 * (c + 1)], o_n[:, 96 * c:96 * (c + 1)], ident_sb[:, :])
                ins.then_inc(b_OTps, 1)

            def tail_proj(i, c):
                pe.wait_ge(b_OTev, 3 * i + c + 1)
                for c in range(2):
                    ins = mm(ps[:, 7, 0:D], oT[:, c, :], wo_sb[:, c, :], start=c == 0, stop=c == 1)
                ins.then_inc(b_Pps, 1)

            def tail_xT(i, c):
                m = 3 * i + c
                pe.wait_ge(b_xn2, 2 * m + 2)
                for k in range(2):
                    ins = tr(ps[0:96, 7, 128 * k:128 * (k + 1)], xn2[:, c, 96 * k:96 * (k + 1)], ident_sb[:, :])
                ins.then_inc(b_xTps, 1)

            def tail_gate(i, c):
                m = 3 * i + c
                pe.wait_ge(b_xTev, m + 1)
                for k in range(2):
                    ins = mm(ps[:, 7, 0:E], xn2T[:, c, k, :], gate_sb[:, k, :], start=k == 0, stop=k == 1)
                ins.then_inc(b_gps, 1)

            def b_tile(i, c, first=False, second=False):
                n = 3 * i + c
                bi, bc = back(i, c)
                for p in range(6):
                    scores(i, c, p)
                    if p:
                        probs_T(i, c, p - 1)
                    elif not first:
                        probs_T(bi, bc, 5)
                    if p > 1:
                        values(i, c, p - 2)
                    elif not first:
                        values(bi, bc, p + 4)
                    if first:
                        continue
                    if p == 0 and not second:
                        tail_gate(*back2(i, c))
                    if p == 2:
                        tail_oT(n - 1)
                    if p == 3:
                        tail_proj(bi, bc)
                    if p == 5:
                        tail_xT(bi, bc)

            b_tile(0, 0, True)
            b_tile(0, 1, False, True)
            b_tile(0, 2)
            with pe.Fori(1, NB) as i:
                for c in range(3):
                    b_tile(i, c)
            probs_T(NB - 1, 2, 5)
            values(NB - 1, 2, 4)
            values(NB - 1, 2, 5)
            tail_gate(NB - 1, 1)
            tail_oT(NT - 1)
            tail_proj(NB - 1, 2)
            tail_xT(NB - 1, 2)
            tail_gate(NB - 1, 2)

            pe.wait_ge(r_m, 1)
            for k in range(2):
                for a in range(2):
                    ins = mm(ps[:, 2 * k + a, 0:NT // 2 * E], tri_sb[:, k, :],
                             rt_m[:].rearrange("p (a n) e -> p a (n e)", a=2)[:, a, :], start=True, stop=True)
            ins.then_inc(r_rank, 1)

            pe.wait_ge(r_done, 1)
            pe.wait_ge(c_w, 32)
            with pe.Fori(0, NB // 2) as j:
                for u in range(2):
                    n = 2 * j + u
                    pe.wait_ge(c_xld[u], 16 * j + 16)
                    for m in range(8):
                        for k, (used, made) in enumerate(((c_silu, c_a), (c_h, c_b))):
                            pe.wait_ge(used[m % 2], 4 * n + m // 2)
                            for c in range(2):
                                ins = mm(ps[:, 2 * k + m % 2, 0:BAND], sw13_sb[:, c, k, 128 * m:128 * (m + 1)],
                                         c_x[:, u, c, :], start=c == 0, stop=c == 1)
                            ins.then_inc(made[m % 2], 1)
                    for r in range(2):
                        pe.wait_ge(c_h[r], 4 * n + 4)
                    for s in range(3):
                        w = 3 * u + s
                        pe.wait_ge(c_z[w % 2], 3 * j + w // 2)
                        for m in range(8):
                            ins = mm(ps[:, 4 + w % 2, 0:D], s_h[:, m, 128 * s:128 * (s + 1)], sw2_sb[:, m, :],
                                     start=m == 0, stop=m == 7)
                        ins.then_inc(c_zps[w % 2], 1)

            pe.wait_ge(d_w, 48 * EX // 2)
            pe.wait_ge(d_half, 2)
            for r in range(2):
                pe.wait_ge(c_z[r], 3 * NB // 2)

            def x_T(v, g):
                q = 2 * g + v // 2
                pe.wait_ge(d_g[v], 16 * g + 16)
                pe.wait_ge(d_xTev[v % 2], 3 * q)
                for k in range(2):
                    ins = tr(ps[:, 6 + v % 2, 128 * k:128 * (k + 1)], xg[:, v, 128 * k:128 * (k + 1)], ident_sb[:, :])
                ins.then_inc(d_xTps[v % 2], 1)

            def h_T(v, g):
                q = 2 * g + v // 2
                pe.wait_ge(d_h[v % 2], q + 1)
                pe.wait_ge(d_hTev, V4 * g + v)
                for k in range(4):
                    ins = tr(ps[:, 4, 128 * k:128 * (k + 1)], m_h[:, v % 2, 128 * k:128 * (k + 1)], ident_sb[:, :])
                ins.then_inc(d_hTps[v % 2], 1)

            def y_mm(j, v, g):
                e = pe.value_load(slot_expert[0:1, ds(j, 1)], min_val=0, max_val=EX - 1)
                pe.wait_ge(d_hTev, j + 1)
                pe.wait_ge(d_y, j)
                for k in range(4):
                    ins = mm(ps[:, 5, 0:D], m_hT[:, v % 2, 128 * k:128 * (k + 1)],
                             w2_sb[:].rearrange("p e k d -> p (e k d)")[:, ds(e * (4 * D) + k * D, D)],
                             start=k == 0, stop=k == 3)
                ins.then_inc(d_yps[v % 2], 1)

            def d_step(g, first, last):
                for v in range(V4):
                    j = V4 * g + v
                    q = 2 * g + v // 2
                    pv, pg = ((v - 1), g) if v else (V4 - 1, g - 1)
                    e = pe.value_load(slot_expert[0:1, ds(j, 1)], min_val=0, max_val=EX - 1)
                    wa = w13a_sb[:].rearrange("p e k d -> p (e k d)")
                    wb = w13b_sb[:].rearrange("p e d -> p (e d)")
                    pe.wait_ge(d_xTev[v % 2], 3 * q + 3)
                    for k, (half, used, made) in enumerate(((xb1, d_silu, d_a), (xb3, d_h, d_b))):
                        pe.wait_ge(used[v % 2], q)
                        mm(ps[:, 2 * k + v % 2, :], xa[:, v % 2, :], wa[:, ds(e * (2 * INTER) + k * INTER, INTER)],
                           start=True, stop=False)
                        mm(ps[:, 2 * k + v % 2, :], half[:, v % 2, :], wb[:, ds(e * INTER, INTER)],
                           start=False, stop=True).then_inc(made[v % 2], 1)
                        if k == 0:
                            if not (last and v == V4 - 1):
                                x_T((v + 1) % V4, g + (v + 1) // V4)
                            if not (first and v == 0):
                                h_T(pv, pg)
                    if not (first and v == 0):
                        y_mm(j - 1, pv, pg)

            x_T(0, 0)
            d_step(0, True, False)
            with pe.Fori(1, SLOTS // V4 - 1) as g:
                d_step(g, False, False)
            d_step(SLOTS // V4 - 1, False, True)
            h_T(V4 - 1, SLOTS // V4 - 1)
            y_mm(SLOTS - 1, V4 - 1, SLOTS // V4 - 1)


def _lay_out(x, L0_conv_registers, L0_conv_qkv_w, L0_conv_qkv_b, L0_conv_out_w, L0_conv_out_b,
             L0_ffn_gate_w, L0_ffn_w1, L0_ffn_w2, L0_ffn_w3, L0_ffn_sw1, L0_ffn_sw2, L0_ffn_sw3):
    import numpy as np

    def arr(a):
        return np.asarray(a)

    def halves(w):
        return np.ascontiguousarray(w.reshape(2, 96, -1).transpose(1, 0, 2))

    D, H = 192, 12
    qkv_w, qkv_b = arr(L0_conv_qkv_w), arr(L0_conv_qkv_b)
    wqk = np.zeros((D, 2, 3, 4, 32), np.float32)
    wqk[..., :16] = qkv_w[:2 * D].T.reshape(D, 2, 3, 4, 16)
    bqk = np.zeros((2, 3, 4, 32), np.float32)
    bqk[..., :16] = qkv_b[:2 * D].reshape(2, 3, 4, 16)
    o = {
        "x": arr(x).reshape(-1, D),
        "kv_reg_t": halves(arr(L0_conv_registers).T),
        "wqk": halves(wqk.reshape(D, -1)).reshape(96, 2, 6, 128),
        "bqk": np.ascontiguousarray(bqk.reshape(6, 128).T),
        "wv": halves(qkv_w[2 * D:].T),
        "bv": np.broadcast_to(qkv_b[2 * D:], (128, D)).copy(),
        "wo": halves(arr(L0_conv_out_w).T),
        "bo": np.broadcast_to(arr(L0_conv_out_b), (128, D)).copy(),
        "gate_t": halves(arr(L0_ffn_gate_w).T),
    }
    w1, w3 = (arr(w).transpose(2, 0, 1) for w in (L0_ffn_w1, L0_ffn_w3))
    o["w13a"] = np.ascontiguousarray(np.stack([w1[:128], w3[:128]], axis=2))
    o["w13b"] = np.ascontiguousarray(np.concatenate([w1[128:], w3[128:]], axis=0))
    o["w2"] = np.ascontiguousarray(arr(L0_ffn_w2).reshape(16, D, 4, 128).transpose(3, 0, 2, 1))
    o["sw13"] = np.ascontiguousarray(np.stack([halves(arr(L0_ffn_sw1).T), halves(arr(L0_ffn_sw3).T)], axis=2))
    o["sw2"] = np.ascontiguousarray(arr(L0_ffn_sw2).T.reshape(8, 128, D).transpose(1, 0, 2))

    def bf(a):
        return (np.ascontiguousarray(a, np.float32).view(np.uint32) >> 16).astype(np.uint16)

    o["ident"] = np.eye(128, dtype=np.float32)
    t = np.arange(128)
    o["tri"] = bf(np.stack([t[:, None] < t[None, :], np.ones((128, 128), bool)], axis=1))
    mq = np.zeros((24, 128), np.float32)
    mq[t // 16, t] = 1
    mq[8 + t % 16, t] = 1
    o["mask_q"] = bf(np.tile(np.pad(mq, ((0, 8), (0, 0))), (4, 1)))
    mk = np.zeros((24, 12, 3, 330), np.float32)
    for i in range(12):
        for c in range(3):
            kr0, kc0 = 8 * (i % 6) - 3, min(max(16 * c - 3, 0), 26)
            kr = kr0 + np.arange(308) // 22
            kc = kc0 + np.arange(308) % 22
            for r in range(8):
                lo = min(max(8 * (i % 6) + r - 3, 0), 41)
                mk[r, i, c, :308] = np.where((kr >= lo) & (kr < lo + 7), 0, -1e30)
            for q in range(16):
                lo = min(max(16 * c + q - 3, 0), 41)
                mk[8 + q, i, c, :308] = np.where((kc >= lo) & (kc < lo + 7), 0, -1e30)
    mk[:8, :, :, 324:] = -1e30
    o["mask_k"] = bf(np.tile(np.pad(mk.reshape(24, -1), ((0, 8), (0, 0))), (4, 1)))
    n = np.arange(36)
    p = t[:, None]
    o["token_ids"] = (n // 3 * 384 + n % 3 * 16 + p // 16 * 48 + p % 16).astype(np.int32)
    o["iota_e"] = np.broadcast_to(np.arange(16, dtype=np.float32), (128, 16)).copy()
    o["iota_s"] = np.broadcast_to(np.arange(88, dtype=np.float32), (128, 88)).copy()
    li = np.zeros((128, 88, 2), np.int32)
    li[:, :, 0] = 4608 + p
    o["list_init"] = li.reshape(128, -1)
    return o


def kernel(**inputs):
    import concourse.bacc as _bacc
    from concourse import mybir as _mybir
    from concourse.bass_utils import run_bass_kernel_spmd as _run

    nc = _bacc.Bacc("TRN2", target_bir_lowering=False, num_devices=1)
    arrays, args = {}, []
    for name, a in _lay_out(**inputs).items():
        arrays[f"in_{name}"] = a
        args.append(nc.dram_tensor(f"in_{name}", a.shape, _mybir.dt.from_np(a.dtype), kind="ExternalInput").ap())
    out = nc.dram_tensor("out", (4608, 192), _mybir.dt.float32, kind="ExternalOutput").ap()
    metaformer_block(nc, *args, out)
    r = _run(nc, [arrays], core_ids=[0])
    return r.results[0]["out"].reshape(2, 48, 48, 192)
```

```python
import itertools

import concourse.bass as bass
from concourse import mybir
from contextlib import ExitStack


def metaformer_block(nc, x, kv_reg_t, wqk, bqk, wv, bv, wo, bo, gate_t, w13a, w13b, w2, sw13, sw2,
                     ident, tri, mask_q, mask_k, token_ids, iota_e, iota_s, list_init, out):
    f32, bf16, i32 = mybir.dt.float32, mybir.dt.bfloat16, mybir.dt.int32
    ALU, ACT, AX = mybir.AluOpType, mybir.ActivationFunctionType, mybir.AxisListType
    ds = bass.ds

    D, SIDE, NB = 192, 48, 12
    BAND = 8 * SIDE
    T = NB * BAND
    NT = T // 128
    QR, QC, HALO = 8, 16, 3
    KR, KC = QR + 2 * HALO, QC + 2 * HALO
    NREG, H, E = 16, 12, 16
    NKEY = KR * KC
    CH = 110
    KW = 3 * CH
    PADT = HALO * SIDE
    KC0 = [min(max(QC * c - HALO, 0), SIDE - KC) for c in range(3)]
    EX, INTER = 16, 512
    SINTER = 1024
    SLOTS = 2 * T // 128 + EX
    V4 = 4
    XW = 256

    ctx = ExitStack()
    with ctx:
        def sem(name):
            return ctx.enter_context(nc.semaphore(name))

        def sems(name, n):
            return [sem(f"{name}{i}") for i in range(n)]

        v_dram = nc.dram_tensor("v_dram", (T + 2 * PADT, D), f32).ap()
        xn_dram = nc.dram_tensor("xn_dram", (T + 128, XW), f32).ap()
        xt_dram = nc.dram_tensor("xt_dram", (96, 2, T), f32).ap()
        acc_dram = nc.dram_tensor("acc_dram", (T + 128, D), f32).ap()
        list_dram = nc.dram_tensor("list_dram", (128 * SLOTS, 2), i32).ap()

        top = nc.sbuf_usable_end // 64 * 64 - 128
        cursor = [(nc.sbuf_base + 63) // 64 * 64]

        def place(name, shape, dt, at=None):
            size = 2 if dt == bf16 else 4
            for n in shape[1:]:
                size *= n
            size = (size + 31) // 32 * 32
            where = cursor[0] if at is None else at[0]
            t = nc.alloc_sbuf_tensor_at(name, shape, dt, offset=where)
            if at is None:
                cursor[0] += size
            else:
                at[0] += size
            return t

        wqk_sb = place("wqk_sb", [96, 2, 6, 128], f32)
        bqk_sb = place("bqk_sb", [128, 6], f32)
        wv_sb = place("wv_sb", [96, 2, D], f32)
        bv_sb = place("bv_sb", [128, D], f32)
        wo_sb = place("wo_sb", [128, 3, D], f32)
        bo_sb = place("bo_sb", [128, D], f32)
        gate_sb = place("gate_sb", [96, 2, E], f32)
        ident_sb = place("ident_sb", [128, 128], f32)
        tri_sb = place("tri_sb", [128, 2, 128], bf16)
        maskq_sb = place("maskq_sb", [128, 128], bf16)
        ids_sb = place("ids_sb", [128, NT], i32)
        iotae_sb = place("iotae_sb", [128, E], f32)
        iotas_sb = place("iotas_sb", [128, SLOTS], f32)
        logits = place("logits", [128, NT, E], f32)
        pair_idx = place("pair_idx", [128, NT, 2], i32)
        pair_val = place("pair_val", [128, NT, 2, 2], i32)
        slot_expert = place("slot_expert", [128, SLOTS], i32)
        lists = place("lists", [128, SLOTS, 2], i32)
        arena = cursor[0]
        at = [arena]
        kT = place("kT", [128, 3, T + 2 * PADT], f32, at)
        qT = place("qT", [128, 3, T], f32, at)
        stage = at[0]
        at = [arena]
        w13a_sb = place("w13a_sb", [128, EX, 2, INTER], f32, at)
        w13b_sb = place("w13b_sb", [128, EX, INTER], f32, at)
        s_h = place("s_h", [128, 8, BAND], f32, at)
        s_sg = place("s_sg", [128, 2, BAND], f32, at)
        assert at[0] <= stage

        at = [stage]
        kst = place("kst", [128, 3, 3, KW], f32, at)
        qst = place("qst", [128, 3, 3, 128], f32, at)
        vst = place("vst", [128, 3, 3, D], f32, at)
        mst = place("mst", [128, 3, KW], bf16, at)
        probs = place("probs", [128, 2, 2, KW], f32, at)
        probsT = place("probsT", [128, 2, 2, 3 * 128], f32, at)
        nmax = place("nmax", [128, 2, 2], f32, at)
        sums = place("sums", [128, 2, 2], f32, at)
        rsum = place("rsum", [128, 2, 2], f32, at)
        x_p = place("x_p", [128, 3, D], f32, at)
        xb = place("xb", [128, 3, D], f32, at)
        oT = place("oT", [128, 3, 128], f32, at)
        x2 = place("x2", [128, 3, D], f32, at)
        b_st = place("b_st", [128, 6], f32, at)
        b_mv = place("b_mv", [128, 2], f32, at)
        b_ve = place("b_ve", [128, 1], f32, at)
        b_rs = place("b_rs", [128, 1], f32, at)
        minus_half = place("minus_half", [128, 3], f32, at)
        xn2 = place("xn2", [128, 3, XW], f32, at)
        xn2T = place("xn2T", [96, 3, 2, 128], f32, at)
        b_end = at[0]
        a_x = place("a_x", [128, 2, 3, D], f32, at)
        a_xn = place("a_xn", [128, 2, 3, D], f32, at)
        a_xnT = place("a_xnT", [96, 2, 2, BAND], f32, at)
        a_v = place("a_v", [128, 2, 3, D], f32, at)
        a_st = place("a_st", [128, 3, 6], f32, at)
        a_mv = place("a_mv", [128, 3, 2], f32, at)
        a_ve = place("a_ve", [128, 3], f32, at)
        a_rs = place("a_rs", [128, 3], f32, at)
        zeros = place("zeros", [128, 2 * D], f32, at)
        reg_t = place("reg_t", [96, 2, NREG], f32, at)
        reg_k = place("reg_k", [128, 3, NREG], f32, at)
        reg_v = place("reg_v", [NREG, D], f32, at)
        assert at[0] <= top, at[0]

        at = [stage]
        w2_sb = place("w2_sb", [128, EX, 4, D], f32, at)
        after_w2 = at[0]
        at = [stage]
        rt = [place(f"rt{i}", [128, NT, E], f32, at) for i in range(6)]
        rt_m = place("rt_m", [128, E, NT], bf16, at)
        total = place("total", [128, E, NT], f32, at)
        incl = place("incl", [128, E, NT], f32, at)
        seg = place("seg", [128, E, NT], f32, at)
        first_row = place("first_row", [128, E, NT], f32, at)
        rs1 = [place(f"rs1_{i}", [128, NT], f32, at) for i in range(4)]
        top_w = place("top_w", [128, NT, 2], f32, at)
        pos_f = place("pos_f", [128, NT, 2], f32, at)
        pos_i = place("pos_i", [128, NT, 2], i32, at)
        pos_hi = place("pos_hi", [128, NT, 2], i32, at)
        pos_lo = place("pos_lo", [128, NT, 2], i32, at)
        cnt_i = place("cnt_i", [128, E], i32, at)
        cnt = [place(f"cnt{i}", [128, E], f32, at) for i in range(4)]
        slot_cmp = place("slot_cmp", [128, SLOTS, E], f32, at)
        slot_f = place("slot_f", [128, SLOTS], f32, at)
        assert at[0] <= after_w2
        at = [after_w2]
        c_x2 = place("c_x2", [128, 3, D], f32, at)
        at = [max(b_end, at[0])]
        sw13_sb = place("sw13_sb", [96, 2, 2, SINTER], f32, at)
        sw2_sb = place("sw2_sb", [128, 8, D], f32, at)
        c_x = place("c_x", [96, 2, 2, BAND], f32, at)
        assert at[0] <= top, at[0]
        at = [max(b_end, after_w2)]
        xg = place("xg", [128, V4, XW], f32, at)
        xa = place("xa", [128, 2, 128], f32, at)
        xb1 = place("xb1", [128, 2, 128], f32, at)
        xb3 = place("xb3", [128, 2, 128], f32, at)
        m_sg = place("m_sg", [128, 2, INTER], f32, at)
        m_h = place("m_h", [128, 2, INTER], f32, at)
        m_hT = place("m_hT", [128, 2, INTER], f32, at)
        ys = place("ys", [128, V4, D], f32, at)
        gidx = place("gidx", [128, V4, 1], i32, at)
        assert at[0] <= nc.sbuf_usable_end
        ps = ctx.enter_context(nc.psum_tensor("ps", [128, 8, 512], f32))

        s_const = sem("s_const")
        s_zero = sem("s_zero")
        s_pad = sem("s_pad")
        s_regin = sem("s_regin")
        r_ps = sem("r_ps")
        r_k = sem("r_k")
        r_v = sem("r_v")
        r_vout = sem("r_vout")
        r_vin = sem("r_vin")
        s_kpad = sem("s_kpad")
        a_xld = sems("a_xld", 2)
        a_var = sem("a_var")
        a_pow = sem("a_pow")
        b_var = sem("b_var")
        b_pow = sem("b_pow")
        s_half = sem("s_half")
        s_oz = sem("s_oz")
        a_norm = sems("a_norm", 2)
        a_xTps = sems("a_xTps", 2)
        a_xnTev = sem("a_xnTev")
        a_qps = sems("a_qps", 2)
        a_qev = sems("a_qev", 2)
        a_kps = sems("a_kps", 2)
        a_kev = sems("a_kev", 2)
        a_vps = sems("a_vps", 2)
        a_vev = sems("a_vev", 2)
        a_vst = sems("a_vst", 2)
        dve_s = sem("dve_s")
        b_kq = sems("b_kq", 3)
        b_xld = sems("b_xld", 3)
        b_xb = sems("b_xb", 3)
        b_vld = sems("b_vld", 3)
        b_mld = sems("b_mld", 3)
        b_S = [sems(f"b_S{c}", 2) for c in range(3)]
        b_O = [sems(f"b_O{c}", 2) for c in range(3)]
        b_nm = sem("b_nm")
        b_exp = sems("b_exp", 2)
        b_T = sems("b_T", 2)
        b_TevD = sem("b_TevD")
        b_TevA = sem("b_TevA")
        b_norm = sem("b_norm")
        b_oTev = sem("b_oTev")
        b_Pps = sem("b_Pps")
        b_x2 = sems("b_x2", 3)
        b_xn2 = sem("b_xn2")
        b_xTps = sem("b_xTps")
        b_xTev = sem("b_xTev")
        b_gps = sem("b_gps")
        b_lg = sem("b_lg")
        b_x2st = sems("b_x2st", 3)
        b_xn2st = sems("b_xn2st", 3)
        b_xTst = sems("b_xTst", 3)
        r_sub = sem("r_sub")
        r_exp = sem("r_exp")
        r_m = sem("r_m")
        r_tot = sem("r_tot")
        r_totc = sem("r_totc")
        r_rank = sem("r_rank")
        r_done = sem("r_done")
        l_init = sem("l_init")
        l_cp = sem("l_cp")
        l_sc = sems("l_sc", 2)
        l_back = sem("l_back")
        c_w = sem("c_w")
        c_xld = sems("c_xld", 2)
        c_x2ld = sem("c_x2ld")
        c_a = sems("c_a", 2)
        c_b = sems("c_b", 2)
        c_silu = sems("c_silu", 2)
        c_h = sems("c_h", 2)
        c_zps = sems("c_zps", 2)
        c_z = sems("c_z", 2)
        c_acc = sem("c_acc")
        d_w = sem("d_w")
        d_half = sem("d_half")
        d_ix = sem("d_ix")
        d_g = sems("d_g", V4)
        d_xTps = sems("d_xTps", 2)
        d_xTev = sems("d_xTev", 2)
        d_a = sems("d_a", 2)
        d_b = sems("d_b", 2)
        d_silu = sems("d_silu", 2)
        d_h = sems("d_h", 2)
        d_hTps = sems("d_hTps", 2)
        d_hTev = sem("d_hTev")
        d_yps = sems("d_yps", 2)
        d_y = sem("d_y")
        d_sc = sems("d_sc", V4)
        s_out = sem("s_out")
        passed_pool = sem("passed_pool")
        passed_dve = sem("passed_dve")

        pair_stage = place("pair_stage", [128, 2, 2, 2], i32, [top])
        idx_stage = place("idx_stage", [128, 2, 2], i32, [top + 64])

        def patch(dram, i, c, w):
            return dram[ds(i * BAND, BAND), :].rearrange("(r c) d -> r c d", c=SIDE)[
                :, QC * c:QC * (c + 1), 0:w]

        def head(p, hh):
            h = 2 * p + hh
            return h // 4, 32 * (h % 4)

        def back(i, c):
            return (i, c - 1) if c else (i - 1, 2)

        def back2(i, c):
            return (i, 0) if c == 2 else (i - 1, c + 1)

        def turns(eng, n, body, last=None):
            body(0)
            with eng.Fori(1, n - 1 if last else n) as j:
                body(j)
            if last:
                last(n - 1)

        block = ctx.enter_context(nc.Block())

        @block.sync
        def _(sp):
            for dst, src in ((wqk_sb, wqk), (bqk_sb, bqk), (wv_sb, wv), (bv_sb, bv), (wo_sb, wo), (bo_sb, bo),
                             (gate_sb, gate_t), (ident_sb, ident), (tri_sb, tri.bitcast(bf16)),
                             (maskq_sb, mask_q.bitcast(bf16)),
                             (ids_sb, token_ids), (iotae_sb, iota_e), (iotas_sb, iota_s), (reg_t, kv_reg_t)):
                sp.dma_start(dst[:], src).then_inc(s_const, 16)
            sp.dma_start(list_dram.rearrange("(p s) w -> p (s w)", p=128), list_init).then_inc(l_init, 16)

            def load_band(n, u, j):
                sp.wait_ge(a_norm[u], j)
                sp.dma_start(a_x[:, u, :, :], x[ds(n * BAND, BAND), :].rearrange(
                    "(s p) d -> p s d", p=128)).then_inc(a_xld[u], 16)

            def load_bands(j):
                for u in range(2):
                    load_band(2 * j + u, u, j)

            turns(sp, NB // 2, load_bands)
            sp.wait_ge(s_zero, 1)
            sp.dma_start(v_dram[0:PADT, :].rearrange("(p a) d -> p (a d)", a=2),
                         zeros[0:PADT // 2, :]).then_inc(s_pad, 16)
            sp.dma_start(v_dram[PADT + T:2 * PADT + T, :].rearrange("(p a) d -> p (a d)", a=2),
                         zeros[0:PADT // 2, :]).then_inc(s_pad, 16)
            sp.dma_start(xn_dram[T:T + 128, :], zeros[:, 0:XW]).then_inc(s_pad, 16)
            sp.dma_start(acc_dram[T:T + 128, :], zeros[:, 0:D]).then_inc(s_pad, 16)
            sp.wait_ge(r_v, 1)
            sp.wait_ge(s_kpad, 4)
            for c in range(3):
                sp.dma_start(vst[NKEY - 2 * CH:NKEY - 2 * CH + NREG, c, 2, :], reg_v[:, :]).then_inc(r_vin, 16)
            sp.wait_ge(s_pad, 64)
            for u in range(2):
                sp.wait_ge(a_vst[u], 16 * NB // 2)

            def tile_in(i, c):
                sp.wait_ge(b_S[c][1], 3 * i)
                sp.dma_start(mst[:, c, :], mask_k[:, ds((i * 3 + c) * KW, KW)].bitcast(bf16)).then_inc(b_mld[c], 16)
                sp.wait_ge(b_xb[c], i)
                sp.dma_start(x_p[:, c, :], patch(x, i, c, D)).then_inc(b_xld[c], 16)
                sp.wait_ge(b_O[c][1], 3 * i)
                keys = v_dram[ds(i * BAND, KR * SIDE), :].rearrange("(r c) d -> r c d", c=SIDE)
                for k in range(3):
                    rows = min(5, KR - 5 * k)
                    sp.dma_start(vst[0:rows * KC, c, k, :],
                                 keys[5 * k:5 * k + rows, KC0[c]:KC0[c] + KC, :]).then_inc(b_vld[c], 16)

            def tile_out(i, c):
                m = 3 * i + c
                sp.wait_ge(b_x2[c], i + 1)
                sp.dma_start(patch(acc_dram, i, c, D), x2[:, c, :]).then_inc(b_x2st[c], 16)
                sp.wait_ge(b_xn2, 2 * m + 2)
                sp.dma_start(patch(xn_dram, i, c, XW), xn2[:, c, :]).then_inc(b_xn2st[c], 16)
                sp.wait_ge(b_xTev, m + 1)
                sp.dma_start(xt_dram[:, :, ds(m * 128, 128)], xn2T[:, c, :, :]).then_inc(b_xTst[c], 16)

            sp.wait_ge(r_vin, 48)
            for c in range(3):
                tile_in(0, c)
                if c == 2:
                    tile_out(*back2(0, c))
            sp.wait_ge(b_S[0][0], 1)
            sp.dma_start(sw13_sb[:], sw13).then_inc(c_w, 16)
            sp.dma_start(sw2_sb[:], sw2).then_inc(c_w, 16)
            with sp.Fori(1, NB) as i:
                for c in range(3):
                    tile_in(i, c)
                    tile_out(*back2(i, c))
            tile_out(NB - 1, 1)
            tile_out(NB - 1, 2)

            sp.wait_ge(b_gps, NT)
            sp.wait_ge(b_lg, NT)
            for c in range(3):
                sp.wait_ge(b_x2st[c], 16 * NB)
                sp.wait_ge(b_xn2st[c], 16 * NB)
                sp.wait_ge(b_xTst[c], 16 * NB)

            def c_rest(n, u, j, w13, w_2):
                sp.wait_ge(c_acc, 48 * n)
                for s in range(3):
                    sp.dma_start(c_x2[:, s, :], patch(acc_dram, n, s, D)).then_inc(c_x2ld, 16)
                if w13:
                    sp.dma_start(w13a_sb[:, ds(2 * n, 2), :, :], w13a[:, ds(2 * n, 2), :, :]).then_inc(d_w, 16)
                    sp.dma_start(w13b_sb[:, ds(2 * n, 2), :], w13b[:, ds(2 * n, 2), :]).then_inc(d_w, 16)
                if w_2:
                    sp.dma_start(w2_sb[:, ds(2 * n - NW, 2), :, :],
                                 w2[:, ds(2 * n - NW, 2), :, :]).then_inc(d_w, 16)
                for s in range(3):
                    w = 3 * u + s
                    sp.wait_ge(c_z[w % 2], 3 * j + w // 2 + 1)
                    sp.dma_start(patch(acc_dram, n, s, D), c_x2[:, s, :]).then_inc(c_acc, 16)

            sp.dma_start(c_x[:, 0, :, :], xt_dram[:, :, 0:BAND]).then_inc(c_xld[0], 16)
            sp.dma_start(c_x[:, 1, :, :], xt_dram[:, :, BAND:2 * BAND]).then_inc(c_xld[1], 16)

            def c_step(j, w13, w_2, more=True):
                for u in range(2):
                    n = 2 * j + u
                    c_rest(n, u, j, w13, w_2)
                    if more:
                        sp.dma_start(c_x[:, u, :, :],
                                     xt_dram[:, :, ds((n + 2) * BAND, BAND)]).then_inc(c_xld[u], 16)

            NW = 2 * (NB - EX // 2)
            c_step(0, True, False)
            c_step(1, True, False)
            sp.wait_ge(r_done, 1)
            with sp.Fori(2, 4) as j:
                c_step(j, True, True)
            c_step(4, False, True)
            c_step(5, False, True, False)

            for v in range(V4):
                sp.wait_ge(d_sc[v], 16 * SLOTS // V4)
            sp.dma_start(out, acc_dram[0:T, :]).then_inc(s_out, 16)
            sp.wait_ge(s_out, 16)

        @block.gpsimd
        def _(pool):
            nc.gpsimd.memset(zeros[:], 0.0).then_inc(s_zero, 1)
            nc.gpsimd.memset(kT[:, :, 0:PADT], 0.0).then_inc(s_kpad, 1)
            nc.gpsimd.memset(kT[:, :, PADT + T:], 0.0).then_inc(s_kpad, 1)
            nc.gpsimd.memset(vst[:, :, 2, :], 0.0).then_inc(s_kpad, 1)
            nc.gpsimd.memset(kst[:, :, :, NKEY + NREG:], 0.0).then_inc(s_kpad, 1)

            nc.gpsimd.memset(minus_half[:], -0.5).then_inc(s_half, 1)
            pool.wait_ge(s_half, 1)
            def store_v(j):
                for u in range(2):
                    pool.wait_ge(a_vev[0], 3 * j + 2 + u)
                    pool.wait_ge(a_vev[1], 3 * j + 1 + 2 * u)
                    pool.dma_start(v_dram[ds(PADT + (2 * j + u) * BAND, BAND), :].rearrange(
                        "(s p) d -> p s d", p=128), a_v[:, u, :, :]).then_inc(a_vst[u], 16)
                    if type(j) is int and j == NB // 2 - 1 and u:
                        continue
                    root_a(2 * j + u + 1)

            def root_a(n):
                pool.wait_ge(a_var, n + 1)
                nc.gpsimd.tensor_tensor(a_rs[:, :], a_ve[:, :], minus_half[:, :], ALU.pow).then_inc(a_pow, 1)

            root_a(0)
            turns(pool, NB // 2, store_v, store_v)

            pool.wait_ge(r_k, 3)
            for c in range(3):
                nc.gpsimd.tensor_copy(kst[:, c, :, NKEY:NKEY + NREG], reg_k[:, :, :]).then_inc(s_kpad, 1)
            for r in range(2):
                pool.wait_ge(a_qev[r], 3 * NB // 2)
                pool.wait_ge(a_kev[r], 3 * NB // 2)
            pool.wait_ge(s_const, 16 * 14)

            def root(i, c):
                pool.wait_ge(b_var, 3 * i + c + 1)
                nc.gpsimd.tensor_tensor(b_rs[:, :], b_ve[:, :], minus_half[:, 0:1], ALU.pow).then_inc(b_pow, 1)

            def stage_tile(i, c):
                pool.wait_ge(b_S[c][1], 3 * i)
                keys = kT[:, :, ds(i * BAND, KR * SIDE)].rearrange("p g (r c) -> p g r c", c=SIDE)
                nc.gpsimd.tensor_copy(kst[:, c, :, 0:NKEY].rearrange("p g (r c) -> p g r c", c=KC),
                                      keys[:, :, :, KC0[c]:KC0[c] + KC]).then_inc(b_kq[c], 1)
                q = qT[:, :, ds(i * BAND, BAND)].rearrange("p g (r c) -> p g r c", c=SIDE)
                nc.gpsimd.tensor_copy(qst[:, c, :, :].rearrange("p g (r c) -> p g r c", c=QC),
                                      q[:, :, :, QC * c:QC * (c + 1)]).then_inc(b_kq[c], 1)
                pool.wait_ge(b_xld[c], 16 * i + 16)
                pool.wait_ge(b_x2[c], i)
                nc.gpsimd.tensor_tensor(xb[:, c, :], x_p[:, c, :], bo_sb[:, :], ALU.add).then_inc(b_xb[c], 1)

            for c in range(3):
                stage_tile(0, c)
            root(0, 0)
            with pool.Fori(1, NB) as i:
                for c in range(3):
                    stage_tile(i, c)
                    root(*back2(i, c))
            root(NB - 1, 1)
            root(NB - 1, 2)

            pool.wait_ge(r_done, 1)
            pool.wait_ge(l_init, 16)
            def scatter(j):
                for u in range(2):
                    n = 2 * j + u
                    pool.wait_ge(l_sc[u], 32 * j)
                    nc.gpsimd.tensor_copy(idx_stage[:, u, :], pair_idx[:, ds(n, 1), :].squeeze(1)).then_inc(l_cp, 1)
                    nc.gpsimd.tensor_copy(pair_stage[:, u, :, :].rearrange("p a b -> p (a b)"),
                                          pair_val[:, ds(n, 1), :, :].rearrange("p n a b -> p (n a b)")
                                          ).then_inc(l_cp, 1)
                    pool.wait_ge(l_cp, 2 * n + 2)
                    pool.sem_inc(passed_pool, 1)
                    for k in range(2):
                        nc.gpsimd.indirect_dma_start(
                            list_dram, bass.IndirectOffsetOnAxis(ap=idx_stage[:, u, k:k + 1], axis=0),
                            pair_stage[:, u, k, :], None).then_inc(l_sc[u], 16)

            turns(pool, NT // 2, scatter)
            for u in range(2):
                pool.wait_ge(l_sc[u], 32 * NT // 2)
            pool.dma_start(lists[:, :, :].rearrange("p s w -> p (s w)"),
                           list_dram.rearrange("(p s) w -> p (s w)", p=128)).then_inc(l_back, 16)
            pool.wait_ge(l_back, 16)
            for r in range(2):
                pool.wait_ge(c_z[r], 3 * NB // 2)
            pool.wait_ge(c_acc, 48 * NB)
            nc.gpsimd.memset(xb1[64:128, :, :], 0.0).then_inc(d_half, 1)
            pool.wait_ge(d_half, 1)
            nc.gpsimd.memset(xb3[0:64, :, :], 0.0).then_inc(d_half, 1)
            pool.wait_ge(d_half, 2)

            def gather(j, v, g):
                pool.wait_ge(d_sc[v], 16 * g)
                nc.gpsimd.tensor_copy(gidx[:, v, :], lists[:, ds(j, 1), 0]).then_inc(d_ix, 1)
                pool.wait_ge(d_ix, j + 1)
                pool.wait_ge(d_xTps[v % 2], 2 * g + v // 2)
                pool.sem_inc(passed_pool, 1)
                nc.gpsimd.indirect_dma_start(xg[:, v, :], None, xn_dram, bass.IndirectOffsetOnAxis(
                    ap=gidx[:, v, 0:1], axis=0)).then_inc(d_g[v], 16)

            def add_rows(j, v, g, first=False):
                pool.wait_ge(d_y, j + 1)
                if not first:
                    pool.wait_ge(d_sc[(v - 1) % V4], 16 * (g if v == 0 else g + 1))
                pool.sem_inc(passed_pool, 1)
                nc.gpsimd.indirect_dma_start(acc_dram, bass.IndirectOffsetOnAxis(
                    ap=gidx[:, v, 0:1], axis=0), ys[:, v, :], None, compute_op=ALU.add).then_inc(d_sc[v], 16)

            gather(0, 0, 0)
            gather(1, 1, 0)

            def d_step(g, first, last):
                for v in range(V4):
                    j = V4 * g + v
                    if not (last and v >= V4 - 2):
                        gather(j + 2, (v + 2) % V4, g + (v + 2) // V4)
                    if v:
                        add_rows(j - 1, v - 1, g, first and v == 1)
                    elif not first:
                        add_rows(j - 1, V4 - 1, g - 1)

            d_step(0, True, False)
            with pool.Fori(1, SLOTS // V4 - 1) as g:
                d_step(g, False, False)
            d_step(SLOTS // V4 - 1, False, True)
            add_rows(SLOTS - 1, V4 - 1, SLOTS // V4 - 1)

        @block.scalar
        def _(act):
            act.wait_ge(s_const, 16 * 14)
            act.wait_ge(r_ps, 1)
            for g in range(3):
                nc.scalar.activation(reg_k[:, g, :], ps[:, 2, NREG * g:NREG * (g + 1)], ACT.Identity,
                                     bias=bqk_sb[:, 3 + g:4 + g]).then_inc(r_k, 1)

            def xnT_out(u, j):
                act.wait_ge(a_xTps[u], j + 1)
                nc.scalar.copy(a_xnT[:, u, :, :], ps[0:96, 0:2, 0:BAND]).then_inc(a_xnTev, 1)

            def k_out(j, last=False):
                for u in range(2):
                    for g in range(3):
                        if g == 2 and not (last and u):
                            xnT_out(1 - u, j + u)
                        w = 3 * u + g
                        act.wait_ge(a_kps[w % 2], 3 * j + w // 2 + 1)
                        nc.scalar.activation(kT[:, g, ds(PADT + (2 * j + u) * BAND, BAND)],
                                             ps[:, 4 + w % 2, 0:BAND], ACT.Identity,
                                             bias=bqk_sb[:, 3 + g:4 + g]).then_inc(a_kev[w % 2], 1)

            xnT_out(0, 0)
            turns(act, NB // 2, k_out, lambda j: k_out(j, True))

            def probsT_odd(i, c, p):
                m = 6 * (3 * i + c) + p
                act.wait_ge(b_T[1], m + 1)
                before = back(i, c) if p < 2 else (i, c)
                if type(i) is not int or i or c or p >= 2:
                    act.wait_ge(b_O[before[1]][p % 2], 3 * before[0] + (3 if p < 2 else p // 2))
                nc.scalar.copy(probsT[0:CH, p % 2, 1, :], ps[0:CH, 5, 0:3 * 128]).then_inc(b_TevA, 1)

            def b_tile(i, c, first=False):
                n = 3 * i + c
                bi, bc = back(i, c)
                for p in range(6):
                    if p:
                        probsT_odd(i, c, p - 1)
                    elif not first:
                        probsT_odd(bi, bc, 5)
                    act.wait_ge(b_nm, 6 * n + p + 1)
                    for hh in range(2):
                        ins = nc.scalar.activation(probs[:, p % 2, hh, :], ps[:, 2 * (p % 2) + hh, 0:KW], ACT.Exp,
                                                   bias=nmax[:, p % 2, hh:hh + 1],
                                                   accum_out=sums[:, p % 2, hh:hh + 1])
                    ins.then_inc(b_exp[p % 2], 1)
                    if p == 1 and not first:
                        tail_oT(bi, bc)
                    if p == 4 and not first:
                        tail_xT(bi, bc)

            def tail_oT(i, c):
                act.wait_ge(b_O[c][1], 3 * i + 3)
                act.wait_ge(b_Pps, 3 * i + c)
                nc.scalar.copy(oT[:, :, :].rearrange("p a b -> p (a b)"), ps[:, 6, 0:3 * 128]).then_inc(b_oTev, 1)

            def tail_xT(i, c):
                act.wait_ge(b_xTps, 3 * i + c + 1)
                act.wait_ge(b_xTst[c], 16 * i)
                nc.scalar.copy(xn2T[:, c, :, :].rearrange("p a b -> p (a b)"),
                               ps[0:96, 7, 0:256]).then_inc(b_xTev, 1)

            for n in range(6):
                b_tile(n // 3, n % 3, n == 0)
            with act.Fori(2, NB) as i:
                for c in range(3):
                    b_tile(i, c)
            probsT_odd(NB - 1, 2, 5)
            tail_oT(NB - 1, 2)
            tail_xT(NB - 1, 2)

            act.wait_ge(r_sub, 1)
            nc.scalar.activation(rt[1][:], rt[0][:], ACT.Exp).then_inc(r_exp, 1)

            def silus(n):
                for m in range(8):
                    act.wait_ge(c_a[m % 2], 4 * n + m // 2 + 1)
                    act.wait_ge(c_h[m % 2], 4 * n + m // 2)
                    nc.scalar.activation(s_sg[:, m % 2, :], ps[:, m % 2, 0:BAND],
                                         ACT.Silu).then_inc(c_silu[m % 2], 1)

            def xT_split(v, g):
                q = 2 * g + v // 2
                act.wait_ge(d_xTps[v % 2], q + 1)
                act.wait_ge(d_b[v % 2], q)
                bank = 6 + v % 2
                nc.scalar.copy(xa[:, v % 2, :], ps[:, bank, 0:128]).then_inc(d_xTev[v % 2], 1)
                nc.scalar.copy(xb1[0:64, v % 2, :], ps[0:64, bank, 128:256]).then_inc(d_xTev[v % 2], 1)
                nc.scalar.copy(xb3[64:128, v % 2, :], ps[64:128, bank, 128:256]).then_inc(d_xTev[v % 2], 1)

            def d_step(g, last):
                for v in range(V4):
                    q = 2 * g + v // 2
                    act.wait_ge(d_a[v % 2], q + 1)
                    act.wait_ge(d_h[v % 2], q)
                    nc.scalar.activation(m_sg[:, v % 2, :], ps[:, v % 2, :], ACT.Silu).then_inc(d_silu[v % 2], 1)
                    if not (last and v == V4 - 1):
                        xT_split((v + 1) % V4, g + (v + 1) // V4)

            turns(act, NB, silus)
            xT_split(0, 0)
            turns(act, SLOTS // V4, lambda g: d_step(g, False), lambda g: d_step(g, True))

        @block.vector
        def _(dve):
            start, steps = [0], [0]

            def count_from(n):
                start[0], steps[0] = n, 0

            def step(ins):
                steps[0] += 1
                ins.then_inc(dve_s, 1)
                dve.wait_ge(dve_s, start[0] + steps[0])

            dve.wait_ge(s_const, 16 * 14)
            dve.wait_ge(r_ps, 1)
            nc.vector.tensor_tensor(reg_v[:, :], ps[0:NREG, 3, 0:D], bv_sb[0:NREG, :], ALU.add).then_inc(r_v, 1)

            A_STEPS = 2

            def stats(n, u, j):
                count_from(A_STEPS * n)
                dve.wait_ge(a_xld[u], 16 * j + 16)
                for s in range(3):
                    ins = nc.vector.bn_stats(a_st[:, s, :], a_x[:, u, s, :])
                step(ins)
                dve.sem_inc(passed_dve, 1)
                for s in range(3):
                    ins = nc.vector.bn_aggr(a_mv[:, s, :], a_st[:, s, :])
                step(ins)
                nc.vector.tensor_scalar(a_ve[:, :], a_mv[:, :, 1], 1e-6, None, ALU.add).then_inc(a_var, 1)

            def normalize(n, u, j):
                dve.wait_ge(a_pow, n + 1)
                dve.wait_ge(a_xTps[u], j)
                for s in range(3):
                    ins = nc.vector.tensor_scalar(a_xn[:, u, s, :], a_x[:, u, s, :], a_mv[:, s, 0:1],
                                                  a_rs[:, s:s + 1], ALU.subtract, ALU.mult)
                ins.then_inc(a_norm[u], 1)

            def vq_out(j, last=False):
                for u in range(2):
                    n = 2 * j + u
                    more = not (last and u)
                    dve.wait_ge(a_vst[u], 16 * j)
                    for s in range(3):
                        w = 3 * u + s
                        dve.wait_ge(a_vps[w % 2], 3 * j + w // 2 + 1)
                        nc.vector.tensor_tensor(a_v[:, u, s, :], ps[:, 6 + w % 2, 0:D], bv_sb[:, :],
                                                ALU.add).then_inc(a_vev[w % 2], 1)
                    if more:
                        stats(n + 1, 1 - u, j + u)
                    for g in range(3):
                        w = 3 * u + g
                        dve.wait_ge(a_qps[w % 2], 3 * j + w // 2 + 1)
                        nc.vector.tensor_scalar(qT[:, g, ds(n * BAND, BAND)], ps[:, 2 + w % 2, 0:BAND],
                                                bqk_sb[:, g:g + 1], 0.25, ALU.add, ALU.mult
                                                ).then_inc(a_qev[w % 2], 1)
                        if g == 0 and more:
                            normalize(n + 1, 1 - u, j + u)

            stats(0, 0, 0)
            normalize(0, 0, 0)
            turns(dve, NB // 2, vq_out, lambda j: vq_out(j, True))
            nc.vector.memset(ps[:, 6, :], 0.0).then_inc(s_oz, 1)
            base_b = NB * A_STEPS
            B_STEPS = 8

            def probsT_even(i, c, p):
                m = 6 * (3 * i + c) + p
                dve.wait_ge(b_T[0], m + 1)
                before = back(i, c) if p < 2 else (i, c)
                if type(i) is not int or i or c or p >= 2:
                    dve.wait_ge(b_O[before[1]][p % 2], 3 * before[0] + (3 if p < 2 else p // 2))
                nc.vector.tensor_copy(probsT[0:CH, p % 2, 0, :], ps[0:CH, 4, 0:3 * 128]).then_inc(b_TevD, 1)

            def normalize_probs(i, c, p):
                n = 3 * i + c
                dve.wait_ge(b_exp[p % 2], 3 * n + p // 2 + 1)
                step(nc.vector.reciprocal(rsum[:, p % 2, :], sums[:, p % 2, :]))
                for hh in range(2):
                    ins = nc.vector.tensor_scalar(probs[:, p % 2, hh, :], probs[:, p % 2, hh, :],
                                                  rsum[:, p % 2, hh:hh + 1], None, ALU.mult)
                ins.then_inc(b_norm, 1)

            def tail_x2(i, c):
                dve.wait_ge(b_Pps, 3 * i + c + 1)
                dve.wait_ge(b_xb[c], i + 1)
                dve.wait_ge(b_x2st[c], 16 * i)
                nc.vector.tensor_tensor(x2[:, c, :], ps[:, 7, 0:D], xb[:, c, :], ALU.add).then_inc(b_x2[c], 1)
                dve.wait_ge(b_x2[c], i + 1)
                step(nc.vector.bn_stats(b_st[:, :], x2[:, c, :]))
                dve.sem_inc(passed_dve, 1)
                step(nc.vector.bn_aggr(b_mv[:, :], b_st[:, :]))
                nc.vector.tensor_scalar(b_ve[:, :], b_mv[:, 1:2], 1e-5, None, ALU.add).then_inc(b_var, 1)

            def tail_norm(i, c):
                dve.wait_ge(b_pow, 3 * i + c + 1)
                dve.wait_ge(b_xn2st[c], 16 * i)
                for lo, hi, at0 in ((0, D, 0), (128, D, D)):
                    nc.vector.tensor_scalar(xn2[:, c, at0:at0 + hi - lo], x2[:, c, lo:hi], b_mv[:, 0:1],
                                            b_rs[:, 0:1], ALU.subtract, ALU.mult).then_inc(b_xn2, 1)

            def tail_logits(m):
                dve.wait_ge(b_gps, m + 1)
                nc.vector.tensor_copy(logits[:, ds(m, 1), :].squeeze(1), ps[:, 7, 0:E]).then_inc(b_lg, 1)

            def b_tile(i, c, first=False):
                n = 3 * i + c
                bi, bc = back(i, c)
                count_from(base_b if first else base_b + 5 + B_STEPS * (n - 1))
                for p in range(6):
                    if p:
                        normalize_probs(i, c, p - 1)
                    elif not first:
                        normalize_probs(bi, bc, 5)
                    dve.wait_ge(b_S[c][p % 2], 3 * i + p // 2 + 1)
                    nc.vector.tensor_reduce(nmax[:, p % 2, :], ps[:, 2 * (p % 2):2 * (p % 2) + 2, 0:KW],
                                            AX.X, ALU.max, negate=True).then_inc(b_nm, 1)
                    if p:
                        probsT_even(i, c, p - 1)
                    elif not first:
                        probsT_even(bi, bc, 5)
                    if first:
                        continue
                    if p == 2:
                        tail_x2(bi, bc)
                    if p == 3:
                        tail_norm(bi, bc)
                    if p == 5:
                        tail_logits(n - 1)

            for n in range(6):
                b_tile(n // 3, n % 3, n == 0)
            with dve.Fori(2, NB) as i:
                for c in range(3):
                    b_tile(i, c)
            count_from(base_b + 5 + B_STEPS * (NT - 1))
            normalize_probs(NB - 1, 2, 5)
            probsT_even(NB - 1, 2, 5)
            tail_x2(NB - 1, 2)
            tail_norm(NB - 1, 2)
            tail_logits(NT - 1)

            def wide(a):
                return a[:, :].unsqueeze(2).broadcast_to([128, NT, E])

            def narrow(a):
                return a.unsqueeze(1).broadcast_to([128, NT, E])

            def by_tile(a):
                return a[:].rearrange("p e n -> p n e")

            def flat(a):
                return a[:].rearrange("p e n -> p (e n)")

            half = E // 2 * NT
            v = nc.vector

            def scores_to_pairs():
                yield v.tensor_reduce(rs1[0][:], logits[:], AX.X, ALU.max)
                v.tensor_tensor(rt[0][:], logits[:], wide(rs1[0]), ALU.subtract).then_inc(r_sub, 1)
                yield v.memset(seg[:], 1.0)
                v.memset(seg[:, :, 0], 0.0)
                dve.wait_ge(r_exp, 1)
                yield v.tensor_reduce(rs1[0][:], rt[1][:], AX.X, ALU.add)
                yield v.reciprocal(rs1[1][:], rs1[0][:])
                yield v.tensor_tensor(rt[0][:], rt[1][:], wide(rs1[1]), ALU.mult)
                for k in range(2):
                    one_hot = rt[3 + k]
                    yield v.tensor_reduce(top_w[:, :, k], rt[0][:], AX.X, ALU.max)
                    yield v.tensor_tensor(rt[1][:], rt[0][:],
                                          top_w[:, :, k:k + 1].broadcast_to([128, NT, E]), ALU.not_equal)
                    yield v.scalar_tensor_tensor(rt[2][:], rt[1][:], float(2 * E), narrow(iotae_sb[:, :]),
                                                 ALU.mult, ALU.add)
                    yield v.tensor_reduce(rs1[2][:], rt[2][:], AX.X, ALU.min)
                    yield v.tensor_tensor(one_hot[:], narrow(iotae_sb[:, :]), wide(rs1[2]), ALU.is_equal)
                    if k == 0:
                        yield v.scalar_tensor_tensor(rt[0][:], one_hot[:], -2.0, rt[0][:], ALU.mult, ALU.add)
                v.tensor_tensor(by_tile(rt_m), rt[3][:], rt[4][:], ALU.add).then_inc(r_m, 1)

            def pairs_to_rows():
                dve.wait_ge(r_tot, 1)
                v.tensor_copy(flat(total).rearrange("p (a f) -> p a f", a=2), ps[:, 6:8, 0:half]
                              ).then_inc(r_totc, 1)
                dve.wait_ge(r_totc, 1)
                yield v.tensor_tensor_scan(flat(incl), flat(seg), flat(total), 0.0, ALU.mult, ALU.add)
                yield v.tensor_scalar(cnt_i[:, :], incl[:, :, NT - 1], 127.0, None, ALU.add)
                yield v.tensor_scalar(cnt_i[:, :], cnt_i[:, :], 7, None, ALU.arith_shift_right)
                yield v.tensor_copy(cnt[0][:, :], cnt_i[:, :])
                yield v.memset(cnt[2][:, :], 1.0)
                yield v.tensor_tensor_scan(cnt[1][:, :], cnt[2][:, :], cnt[0][:, :], 0.0, ALU.mult, ALU.add)
                yield v.tensor_tensor(cnt[3][:, :], cnt[1][:, :], cnt[0][:, :], ALU.subtract)
                yield v.tensor_tensor(first_row[:], incl[:], total[:], ALU.subtract)
                yield v.scalar_tensor_tensor(first_row[:], cnt[3][:, :].unsqueeze(2).broadcast_to([128, E, NT]),
                                             128.0, first_row[:], ALU.mult, ALU.add)
                dve.wait_ge(r_rank, 1)
                yield v.tensor_tensor(flat(first_row).rearrange("p (a f) -> p a f", a=2),
                                      flat(first_row).rearrange("p (a f) -> p a f", a=2),
                                      ps[:, 6:8, 0:half], ALU.add)
                for k in range(2):
                    yield v.tensor_tensor(rt[5][:], rt[3 + k][:], by_tile(first_row), ALU.mult)
                    yield v.tensor_reduce(pos_f[:, :, k], rt[5][:], AX.X, ALU.add)
                yield v.tensor_copy(pos_i[:], pos_f[:])
                v.tensor_scalar(pos_hi[:], pos_i[:], 7, None, ALU.arith_shift_right)
                yield v.tensor_scalar(pos_lo[:], pos_i[:], 127, None, ALU.bitwise_and)
                v.scalar_tensor_tensor(pair_idx[:], pos_lo[:], float(SLOTS), pos_hi[:], ALU.mult, ALU.add)
                for k in range(2):
                    v.tensor_copy(pair_val[:, :, k, 0], ids_sb[:, :])
                yield v.tensor_copy(pair_val[:, :, :, 1].bitcast(f32), top_w[:, :, :])
                yield v.tensor_tensor(slot_cmp[:], iotas_sb[:, :].unsqueeze(2).broadcast_to([128, SLOTS, E]),
                                      cnt[1][:, :].unsqueeze(1).broadcast_to([128, SLOTS, E]), ALU.is_ge)
                yield v.tensor_reduce(slot_f[:], slot_cmp[:], AX.X, ALU.add)
                v.tensor_scalar(slot_expert[:], slot_f[:], float(EX - 1), None, ALU.min).then_inc(r_done, 1)

            def take(route, n):
                for ins in itertools.islice(route, n):
                    step(ins)

            def band(n, u, j, route=(), pace=0):
                for m in range(8):
                    dve.wait_ge(c_silu[m % 2], 4 * n + m // 2 + 1)
                    dve.wait_ge(c_b[m % 2], 4 * n + m // 2 + 1)
                    v.tensor_tensor(s_h[:, m, :], s_sg[:, m % 2, :], ps[:, 2 + m % 2, 0:BAND],
                                    ALU.mult).then_inc(c_h[m % 2], 1)
                    take(route, pace)
                take(route, 99)
                for s in range(3):
                    w = 3 * u + s
                    dve.wait_ge(c_zps[w % 2], 3 * j + w // 2 + 1)
                    dve.wait_ge(c_x2ld, 48 * n + 48)
                    v.tensor_tensor(c_x2[:, s, :], ps[:, 4 + w % 2, 0:D], c_x2[:, s, :],
                                    ALU.add).then_inc(c_z[w % 2], 1)

            dve.wait_ge(b_lg, NT)
            count_from(base_b + 5 + B_STEPS * (NT - 1) + 3)
            for c in range(3):
                dve.wait_ge(b_x2st[c], 16 * NB)
                dve.wait_ge(b_xn2st[c], 16 * NB)
                dve.wait_ge(b_xTst[c], 16 * NB)
            route = scores_to_pairs()
            take(route, 2)
            band(0, 0, 0, route, 3)
            band(1, 1, 0, pairs_to_rows(), 4)
            with dve.Fori(1, NB // 2) as j:
                for u in range(2):
                    band(2 * j + u, u, j)

            dve.wait_ge(d_half, 2)
            dve.wait_ge(l_back, 16)

            def hT_out(v, g):
                q = 2 * g + v // 2
                dve.wait_ge(d_hTps[v % 2], q + 1)
                dve.wait_ge(d_yps[v % 2], q)
                nc.vector.tensor_copy(m_hT[:, v % 2, :], ps[:, 4, :]).then_inc(d_hTev, 1)

            def y_out(j, v, g):
                dve.wait_ge(d_yps[v % 2], 2 * g + v // 2 + 1)
                dve.wait_ge(d_sc[v], 16 * g)
                nc.vector.tensor_scalar(ys[:, v, :], ps[:, 5, 0:D], lists[:, ds(j, 1), 1].bitcast(f32), None,
                                        ALU.mult).then_inc(d_y, 1)

            def d_step(g, first):
                for v in range(V4):
                    q = 2 * g + v // 2
                    pv, pg = ((v - 1), g) if v else (V4 - 1, g - 1)
                    if not (first and v == 0):
                        hT_out(pv, pg)
                    dve.wait_ge(d_silu[v % 2], q + 1)
                    dve.wait_ge(d_b[v % 2], q + 1)
                    dve.wait_ge(d_hTps[v % 2], q)
                    nc.vector.tensor_tensor(m_h[:, v % 2, :], m_sg[:, v % 2, :], ps[:, 2 + v % 2, :],
                                            ALU.mult).then_inc(d_h[v % 2], 1)
                    if not (first and v == 0):
                        y_out(V4 * g + v - 1, pv, pg)

            d_step(0, True)
            d_step(1, False)
            with dve.Fori(2, SLOTS // V4) as g:
                d_step(g, False)
            hT_out(V4 - 1, SLOTS // V4 - 1)
            y_out(SLOTS - 1, V4 - 1, SLOTS // V4 - 1)

        @block.tensor
        def _(pe):
            mm, tr = nc.tensor.matmul, nc.tensor.transpose
            pe.wait_ge(s_const, 16 * 14)
            for g in range(3):
                for c in range(2):
                    mm(ps[:, 2, NREG * g:NREG * (g + 1)], wqk_sb[:, c, 3 + g, :], reg_t[:, c, :],
                       start=c == 0, stop=c == 1)
            for c in range(2):
                ins = mm(ps[0:NREG, 3, 0:D], reg_t[:, c, :], wv_sb[:, c, :], start=c == 0, stop=c == 1)
            ins.then_inc(r_ps, 1)
            pe.wait_ge(r_k, 3)
            pe.wait_ge(r_v, 1)

            def transpose_x(n, u, j):
                pe.wait_ge(a_norm[u], j + 1)
                pe.wait_ge(a_xnTev, n)
                for c in range(2):
                    for s in range(3):
                        ins = tr(ps[0:96, c, 128 * s:128 * (s + 1)], a_xn[:, u, s, 96 * c:96 * (c + 1)],
                                 ident_sb[:, :])
                ins.then_inc(a_xTps[u], 1)

            def qkv(j, last=False):
                for u in range(2):
                    n = 2 * j + u
                    pe.wait_ge(a_xnTev, n + 1)
                    for s in range(3):
                        w = 3 * u + s
                        pe.wait_ge(a_vev[w % 2], 3 * j + w // 2)
                        for c in range(2):
                            ins = mm(ps[:, 6 + w % 2, 0:D], a_xnT[:, u, c, 128 * s:128 * (s + 1)],
                                     wv_sb[:, c, :], start=c == 0, stop=c == 1)
                        ins.then_inc(a_vps[w % 2], 1)
                    for g in range(6):
                        if g == 4 and not (last and u):
                            transpose_x(n + 1, 1 - u, j + u)
                        w = 3 * u + g // 2
                        made, used, bank = ((a_qps, a_qev, 2), (a_kps, a_kev, 4))[g % 2]
                        pe.wait_ge(used[w % 2], 3 * j + w // 2)
                        for c in range(2):
                            ins = mm(ps[:, bank + w % 2, 0:BAND], wqk_sb[:, c, 3 * (g % 2) + g // 2, :],
                                     a_xnT[:, u, c, :], start=c == 0, stop=c == 1)
                        ins.then_inc(made[w % 2], 1)

            transpose_x(0, 0, 0)
            turns(pe, NB // 2, qkv, lambda j: qkv(j, True))
            for r in range(2):
                for done in (a_qev, a_kev, a_vev):
                    pe.wait_ge(done[r], 3 * NB // 2)
            pe.wait_ge(s_kpad, 7)
            pe.wait_ge(s_oz, 1)

            def scores(i, c, p):
                n = 3 * i + c
                if p == 0:
                    pe.wait_ge(b_kq[c], 2 * i + 2)
                    pe.wait_ge(b_mld[c], 16 * i + 16)
                pe.wait_ge(b_exp[p % 2], 3 * n + p // 2)
                for hh in range(2):
                    g, r = head(p, hh)
                    bank = 2 * (p % 2) + hh
                    mm(ps[:, bank, 0:KW], maskq_sb[r:r + 24, :], mst[r:r + 24, c, :], start=True, stop=False)
                    ins = mm(ps[:, bank, 0:KW], qst[r:r + 16, c, g, :], kst[r:r + 16, c, g, :],
                             start=False, stop=True)
                ins.then_inc(b_S[c][p % 2], 1)

            def probs_T(i, c, p):
                n = 3 * i + c
                pe.wait_ge(b_norm, 6 * n + p + 1)
                for hh in range(2):
                    pe.wait_ge((b_TevD, b_TevA)[hh], 6 * n + p)
                    for k in range(3):
                        ins = tr(ps[0:CH, 4 + hh, 128 * k:128 * (k + 1)], probs[:, p % 2, hh, CH * k:CH * (k + 1)],
                                 ident_sb[:, :])
                    ins.then_inc(b_T[hh], 1)

            def values(i, c, p):
                n = 3 * i + c
                if p == 0:
                    pe.wait_ge(b_vld[c], 48 * i + 48)
                    pe.wait_ge(b_oTev, n)
                for hh in range(2):
                    pe.wait_ge((b_TevD, b_TevA)[hh], 6 * n + p + 1)
                    h = 2 * p + hh
                    g, r = head(p, hh)
                    for k in range(3):
                        ins = mm(ps[r:r + 16, 6, 128 * g:128 * (g + 1)], vst[0:CH, c, k, 16 * h:16 * h + 16],
                                 probsT[0:CH, p % 2, hh, 128 * k:128 * (k + 1)], start=k == 0, stop=k == 2)
                ins.then_inc(b_O[c][p % 2], 1)

            def tail_proj(i, c):
                m = 3 * i + c
                pe.wait_ge(b_oTev, m + 1)
                pe.wait_ge(b_lg, m)
                for g in range(3):
                    ins = mm(ps[:, 7, 0:D], oT[:, g, :], wo_sb[:, g, :], start=g == 0, stop=g == 2)
                ins.then_inc(b_Pps, 1)

            def tail_xT(i, c):
                m = 3 * i + c
                pe.wait_ge(b_xn2, 2 * m + 2)
                for k in range(2):
                    ins = tr(ps[0:96, 7, 128 * k:128 * (k + 1)], xn2[:, c, 96 * k:96 * (k + 1)], ident_sb[:, :])
                ins.then_inc(b_xTps, 1)

            def tail_gate(i, c):
                m = 3 * i + c
                pe.wait_ge(b_xTev, m + 1)
                for k in range(2):
                    ins = mm(ps[:, 7, 0:E], xn2T[:, c, k, :], gate_sb[:, k, :], start=k == 0, stop=k == 1)
                ins.then_inc(b_gps, 1)

            def b_tile(i, c, first=False):
                n = 3 * i + c
                bi, bc = back(i, c)
                for p in range(6):
                    scores(i, c, p)
                    if p:
                        probs_T(i, c, p - 1)
                    elif not first:
                        probs_T(bi, bc, 5)
                    if p > 1:
                        values(i, c, p - 2)
                    elif not first:
                        values(bi, bc, p + 4)
                    if first:
                        continue
                    if p == 2:
                        tail_proj(bi, bc)
                    if p == 4:
                        tail_xT(bi, bc)
                    if p == 5:
                        tail_gate(bi, bc)

            b_tile(0, 0, True)
            b_tile(0, 1)
            b_tile(0, 2)
            with pe.Fori(1, NB) as i:
                for c in range(3):
                    b_tile(i, c)
            probs_T(NB - 1, 2, 5)
            values(NB - 1, 2, 4)
            values(NB - 1, 2, 5)
            tail_proj(NB - 1, 2)
            tail_xT(NB - 1, 2)
            tail_gate(NB - 1, 2)

            def count_pairs(k, made):
                for a in range(2):
                    ins = mm(ps[:, 6 + a, 0:E // 2 * NT], tri_sb[:, k, :],
                             rt_m[:, E // 2 * a:E // 2 * (a + 1), :].rearrange("p e n -> p (e n)"),
                             start=True, stop=True)
                ins.then_inc(made, 1)

            def band(n, u, j, route=False):
                pe.wait_ge(c_xld[u], 16 * j + 16)
                for m in range(8):
                    if route and m == 2:
                        pe.wait_ge(r_totc, 1)
                        count_pairs(0, r_rank)
                    for k, (used, made) in enumerate(((c_silu, c_a), (c_h, c_b))):
                        pe.wait_ge(used[m % 2], 4 * n + m // 2)
                        for c in range(2):
                            ins = mm(ps[:, 2 * k + m % 2, 0:BAND], sw13_sb[:, c, k, 128 * m:128 * (m + 1)],
                                     c_x[:, u, c, :], start=c == 0, stop=c == 1)
                        ins.then_inc(made[m % 2], 1)
                for r in range(2):
                    pe.wait_ge(c_h[r], 4 * n + 4)
                for s in range(3):
                    w = 3 * u + s
                    pe.wait_ge(c_z[w % 2], 3 * j + w // 2)
                    for m in range(8):
                        ins = mm(ps[:, 4 + w % 2, 0:D], s_h[:, m, 128 * s:128 * (s + 1)], sw2_sb[:, m, :],
                                 start=m == 0, stop=m == 7)
                    ins.then_inc(c_zps[w % 2], 1)

            pe.wait_ge(b_lg, NT)
            pe.wait_ge(c_w, 32)
            band(0, 0, 0)
            pe.wait_ge(r_m, 1)
            count_pairs(1, r_tot)
            band(1, 1, 0, True)
            with pe.Fori(1, NB // 2) as j:
                for u in range(2):
                    band(2 * j + u, u, j)

            pe.wait_ge(d_w, 48 * EX // 2)
            pe.wait_ge(r_done, 1)
            pe.wait_ge(d_half, 2)
            for r in range(2):
                pe.wait_ge(c_z[r], 3 * NB // 2)

            def x_T(v, g):
                q = 2 * g + v // 2
                pe.wait_ge(d_g[v], 16 * g + 16)
                pe.wait_ge(d_xTev[v % 2], 3 * q)
                for k in range(2):
                    ins = tr(ps[:, 6 + v % 2, 128 * k:128 * (k + 1)], xg[:, v, 128 * k:128 * (k + 1)], ident_sb[:, :])
                ins.then_inc(d_xTps[v % 2], 1)

            def h_T(v, g):
                q = 2 * g + v // 2
                pe.wait_ge(d_h[v % 2], q + 1)
                pe.wait_ge(d_hTev, V4 * g + v)
                for k in range(4):
                    ins = tr(ps[:, 4, 128 * k:128 * (k + 1)], m_h[:, v % 2, 128 * k:128 * (k + 1)], ident_sb[:, :])
                ins.then_inc(d_hTps[v % 2], 1)

            def y_mm(j, v, g):
                e = pe.value_load(slot_expert[0:1, ds(j, 1)], min_val=0, max_val=EX - 1)
                pe.wait_ge(d_hTev, j + 1)
                pe.wait_ge(d_y, j)
                for k in range(4):
                    ins = mm(ps[:, 5, 0:D], m_hT[:, v % 2, 128 * k:128 * (k + 1)],
                             w2_sb[:].rearrange("p e k d -> p (e k d)")[:, ds(e * (4 * D) + k * D, D)],
                             start=k == 0, stop=k == 3)
                ins.then_inc(d_yps[v % 2], 1)

            def d_step(g, first, last):
                for v in range(V4):
                    j = V4 * g + v
                    q = 2 * g + v // 2
                    pv, pg = ((v - 1), g) if v else (V4 - 1, g - 1)
                    e = pe.value_load(slot_expert[0:1, ds(j, 1)], min_val=0, max_val=EX - 1)
                    wa = w13a_sb[:].rearrange("p e k d -> p (e k d)")
                    wb = w13b_sb[:].rearrange("p e d -> p (e d)")
                    pe.wait_ge(d_xTev[v % 2], 3 * q + 3)
                    for k, (half, used, made) in enumerate(((xb1, d_silu, d_a), (xb3, d_h, d_b))):
                        pe.wait_ge(used[v % 2], q)
                        mm(ps[:, 2 * k + v % 2, :], xa[:, v % 2, :], wa[:, ds(e * (2 * INTER) + k * INTER, INTER)],
                           start=True, stop=False)
                        mm(ps[:, 2 * k + v % 2, :], half[:, v % 2, :], wb[:, ds(e * INTER, INTER)],
                           start=False, stop=True).then_inc(made[v % 2], 1)
                        if k == 0:
                            if not (last and v == V4 - 1):
                                x_T((v + 1) % V4, g + (v + 1) // V4)
                            if not (first and v == 0):
                                h_T(pv, pg)
                    if not (first and v == 0):
                        y_mm(j - 1, pv, pg)

            x_T(0, 0)
            d_step(0, True, False)
            with pe.Fori(1, SLOTS // V4 - 1) as g:
                d_step(g, False, False)
            d_step(SLOTS // V4 - 1, False, True)
            h_T(V4 - 1, SLOTS // V4 - 1)
            y_mm(SLOTS - 1, V4 - 1, SLOTS // V4 - 1)


def _lay_out(x, L0_conv_registers, L0_conv_qkv_w, L0_conv_qkv_b, L0_conv_out_w, L0_conv_out_b,
             L0_ffn_gate_w, L0_ffn_w1, L0_ffn_w2, L0_ffn_w3, L0_ffn_sw1, L0_ffn_sw2, L0_ffn_sw3):
    import numpy as np

    def arr(a):
        return np.asarray(a)

    def halves(w):
        return np.ascontiguousarray(w.reshape(2, 96, -1).transpose(1, 0, 2))

    D, H = 192, 12
    qkv_w, qkv_b = arr(L0_conv_qkv_w), arr(L0_conv_qkv_b)
    wqk = np.zeros((D, 2, 3, 4, 32), np.float32)
    wqk[..., :16] = qkv_w[:2 * D].T.reshape(D, 2, 3, 4, 16)
    bqk = np.zeros((2, 3, 4, 32), np.float32)
    bqk[..., :16] = qkv_b[:2 * D].reshape(2, 3, 4, 16)
    wo = np.zeros((4, 32, 3, D), np.float32)
    wo[:, :16] = arr(L0_conv_out_w).T.reshape(3, 4, 16, D).transpose(1, 2, 0, 3)
    wo = wo.reshape(128, 3, D)
    o = {
        "x": arr(x).reshape(-1, D),
        "kv_reg_t": halves(arr(L0_conv_registers).T),
        "wqk": halves(wqk.reshape(D, -1)).reshape(96, 2, 6, 128),
        "bqk": np.ascontiguousarray(bqk.reshape(6, 128).T),
        "wv": halves(qkv_w[2 * D:].T),
        "bv": np.broadcast_to(qkv_b[2 * D:], (128, D)).copy(),
        "wo": wo,
        "bo": np.broadcast_to(arr(L0_conv_out_b), (128, D)).copy(),
        "gate_t": halves(arr(L0_ffn_gate_w).T),
    }
    w1, w3 = (arr(w).transpose(2, 0, 1) for w in (L0_ffn_w1, L0_ffn_w3))
    o["w13a"] = np.ascontiguousarray(np.stack([w1[:128], w3[:128]], axis=2))
    o["w13b"] = np.ascontiguousarray(np.concatenate([w1[128:], w3[128:]], axis=0))
    o["w2"] = np.ascontiguousarray(arr(L0_ffn_w2).reshape(16, D, 4, 128).transpose(3, 0, 2, 1))
    o["sw13"] = np.ascontiguousarray(np.stack([halves(arr(L0_ffn_sw1).T), halves(arr(L0_ffn_sw3).T)], axis=2))
    o["sw2"] = np.ascontiguousarray(arr(L0_ffn_sw2).T.reshape(8, 128, D).transpose(1, 0, 2))

    def bf(a):
        return (np.ascontiguousarray(a, np.float32).view(np.uint32) >> 16).astype(np.uint16)

    o["ident"] = np.eye(128, dtype=np.float32)
    t = np.arange(128)
    o["tri"] = bf(np.stack([t[:, None] < t[None, :], np.ones((128, 128), bool)], axis=1))
    mq = np.zeros((24, 128), np.float32)
    mq[t // 16, t] = 1
    mq[8 + t % 16, t] = 1
    o["mask_q"] = bf(np.tile(np.pad(mq, ((0, 8), (0, 0))), (4, 1)))
    mk = np.zeros((24, 12, 3, 330), np.float32)
    for i in range(12):
        for c in range(3):
            kr0, kc0 = 8 * (i % 6) - 3, min(max(16 * c - 3, 0), 26)
            kr = kr0 + np.arange(308) // 22
            kc = kc0 + np.arange(308) % 22
            for r in range(8):
                lo = min(max(8 * (i % 6) + r - 3, 0), 41)
                mk[r, i, c, :308] = np.where((kr >= lo) & (kr < lo + 7), 0, -1e30)
            for q in range(16):
                lo = min(max(16 * c + q - 3, 0), 41)
                mk[8 + q, i, c, :308] = np.where((kc >= lo) & (kc < lo + 7), 0, -1e30)
    mk[:8, :, :, 324:] = -1e30
    o["mask_k"] = bf(np.tile(np.pad(mk.reshape(24, -1), ((0, 8), (0, 0))), (4, 1)))
    n = np.arange(36)
    p = t[:, None]
    o["token_ids"] = (n // 3 * 384 + n % 3 * 16 + p // 16 * 48 + p % 16).astype(np.int32)
    o["iota_e"] = np.broadcast_to(np.arange(16, dtype=np.float32), (128, 16)).copy()
    o["iota_s"] = np.broadcast_to(np.arange(88, dtype=np.float32), (128, 88)).copy()
    li = np.zeros((128, 88, 2), np.int32)
    li[:, :, 0] = 4608 + p
    o["list_init"] = li.reshape(128, -1)
    return o


def kernel(**inputs):
    import concourse.bacc as _bacc
    from concourse import mybir as _mybir
    from concourse.bass_utils import run_bass_kernel_spmd as _run

    nc = _bacc.Bacc("TRN2", target_bir_lowering=False, num_devices=1)
    arrays, args = {}, []
    for name, a in _lay_out(**inputs).items():
        arrays[f"in_{name}"] = a
        args.append(nc.dram_tensor(f"in_{name}", a.shape, _mybir.dt.from_np(a.dtype), kind="ExternalInput").ap())
    out = nc.dram_tensor("out", (4608, 192), _mybir.dt.float32, kind="ExternalOutput").ap()
    metaformer_block(nc, *args, out)
    r = _run(nc, [arrays], core_ids=[0])
    return r.results[0]["out"].reshape(2, 48, 48, 192)
```

```python
import itertools

import concourse.bass as bass
from concourse import mybir
from contextlib import ExitStack


def metaformer_block(nc, x, kv_reg_t, wqk, bqk, wv, bv, wo, bo, gate_t, w13a, w13b, w2, sw13, sw2,
                     ident, tri, mask_q, mask_k, token_ids, iota_e, iota_s, list_init, out):
    f32, bf16, i32 = mybir.dt.float32, mybir.dt.bfloat16, mybir.dt.int32
    ALU, ACT, AX = mybir.AluOpType, mybir.ActivationFunctionType, mybir.AxisListType
    ds = bass.ds

    D, SIDE, NB = 192, 48, 12
    BAND = 8 * SIDE
    T = NB * BAND
    NT = T // 128
    QR, QC, HALO = 8, 16, 3
    KR, KC = QR + 2 * HALO, QC + 2 * HALO
    NREG, H, E = 16, 12, 16
    NKEY = KR * KC
    CH = 110
    KW = 3 * CH
    PADT = HALO * SIDE
    KC0 = [min(max(QC * c - HALO, 0), SIDE - KC) for c in range(3)]
    HD = 16
    WR = QR * KC
    Q_PART, K_PART = (0, 0, 0, 1, 1, 2), (0, 1, 2, 0, 1, 0)
    EX, INTER = 16, 512
    SINTER = 1024
    SLOTS = 2 * T // 128 + EX
    V4 = 4
    XW = 256

    ctx = ExitStack()
    with ctx:
        def sem(name):
            return ctx.enter_context(nc.semaphore(name))

        def sems(name, n):
            return [sem(f"{name}{i}") for i in range(n)]

        q_dram = nc.dram_tensor("q_dram", (3, 2, 96, NT, 128), bf16).ap()
        k_dram = nc.dram_tensor("k_dram", (3, 2, 96, 3, (T // SIDE + 2 * HALO) * KC), bf16).ap()
        kreg_dram = nc.dram_tensor("kreg_dram", (3, 2, 96, NREG), bf16).ap()
        v_dram = nc.dram_tensor("v_dram", (T + 2 * PADT, D), f32).ap()
        xn_dram = nc.dram_tensor("xn_dram", (T + 128, XW), f32).ap()
        xt_dram = nc.dram_tensor("xt_dram", (96, 2, T), f32).ap()
        acc_dram = nc.dram_tensor("acc_dram", (T + 128, D), f32).ap()
        list_dram = nc.dram_tensor("list_dram", (128 * SLOTS, 2), i32).ap()

        top = nc.sbuf_usable_end // 64 * 64 - 128
        cursor = [(nc.sbuf_base + 63) // 64 * 64]

        def place(name, shape, dt, at=None):
            size = 2 if dt == bf16 else 4
            for n in shape[1:]:
                size *= n
            size = (size + 31) // 32 * 32
            where = cursor[0] if at is None else at[0]
            t = nc.alloc_sbuf_tensor_at(name, shape, dt, offset=where)
            if at is None:
                cursor[0] += size
            else:
                at[0] += size
            return t

        wqk_sb = place("wqk_sb", [96, 2, 4, 96], f32)
        bqk_sb = place("bqk_sb", [96, 4], f32)
        bq_scaled = place("bq_scaled", [96, 2], f32)
        wv_sb = place("wv_sb", [96, 2, D], f32)
        bv_sb = place("bv_sb", [128, D], f32)
        wo_sb = place("wo_sb", [128, 3, D], f32)
        bo_sb = place("bo_sb", [128, D], f32)
        gate_sb = place("gate_sb", [96, 2, E], f32)
        ident_sb = place("ident_sb", [128, 128], f32)
        tri_sb = place("tri_sb", [128, 2, 128], bf16)
        ids_sb = place("ids_sb", [128, NT], i32)
        iotae_sb = place("iotae_sb", [128, E], f32)
        iotas_sb = place("iotas_sb", [128, SLOTS], f32)
        logits = place("logits", [128, NT, E], f32)
        pair_idx = place("pair_idx", [128, NT, 2], i32)
        pair_val = place("pair_val", [128, NT, 2, 2], i32)
        slot_expert = place("slot_expert", [128, SLOTS], i32)
        lists = place("lists", [128, SLOTS, 2], i32)
        arena = cursor[0]
        at = [arena]
        ksp = place("ksp", [120, 3, H, KW], bf16, at)
        qsp = place("qsp", [120, 3, H, 128], bf16, at)
        a_qf = place("a_qf", [96, 2, 2, BAND], f32, at)
        a_kf = place("a_kf", [96, 2, 2, BAND], f32, at)
        a_qr = place("a_qr", [96, 2, 2, 3, 128], f32, at)
        a_kr = place("a_kr", [96, 2, 3, 2, WR], f32, at)
        a_qs = place("a_qs", [96, 2, 3, 2, 3, 128], bf16, at)
        a_ks = place("a_ks", [96, 2, 3, 3, 2, WR], bf16, at)
        o_raw = place("o_raw", [128, 3 * 128], f32, at)
        reg_kf = place("reg_kf", [96, 2, NREG], f32, at)
        reg_kr = place("reg_kr", [96, 2, NREG], f32, at)
        reg_ks = place("reg_ks", [96, 3, 2, NREG], bf16, at)
        qk_end = at[0]
        at = [arena]
        w13a_sb = place("w13a_sb", [128, EX, 2, INTER], f32, at)
        w13b_sb = place("w13b_sb", [128, EX, INTER], f32, at)
        s_h = place("s_h", [128, 8, BAND], f32, at)
        s_sg = place("s_sg", [128, 2, BAND], f32, at)
        stage = at[0]
        assert qk_end <= stage

        at = [stage]
        vst = place("vst", [128, 3, 3, D], f32, at)
        probs = place("probs", [128, 2, 2, KW], f32, at)
        probsT = place("probsT", [128, 2, 2, 3 * 128], f32, at)
        nmax = place("nmax", [128, 2, 2], f32, at)
        sums = place("sums", [128, 3, H], f32, at)
        rsum1 = place("rsum1", [128, H], f32, at)
        rsum = place("rsum", [128, H, 32], f32, at)
        x_p = place("x_p", [128, 3, D], f32, at)
        xb = place("xb", [128, 3, D], f32, at)
        oT = place("oT", [128, 3, 128], f32, at)
        x2 = place("x2", [128, 3, D], f32, at)
        b_st = place("b_st", [128, 6], f32, at)
        b_mv = place("b_mv", [128, 2], f32, at)
        b_ve = place("b_ve", [128, 1], f32, at)
        b_rs = place("b_rs", [128, 1], f32, at)
        minus_half = place("minus_half", [128, 3], f32, at)
        xn2 = place("xn2", [128, 3, XW], f32, at)
        xn2T = place("xn2T", [96, 3, 2, 128], f32, at)
        b_end = at[0]
        a_x = place("a_x", [128, 2, 3, D], f32, at)
        a_xn = place("a_xn", [128, 2, 3, D], f32, at)
        a_xnT = place("a_xnT", [96, 2, 2, BAND], f32, at)
        a_v = place("a_v", [128, 2, 3, D], f32, at)
        a_st = place("a_st", [128, 3, 6], f32, at)
        a_mv = place("a_mv", [128, 3, 2], f32, at)
        a_ve = place("a_ve", [128, 3], f32, at)
        a_rs = place("a_rs", [128, 3], f32, at)
        zeros = place("zeros", [128, 2 * D], f32, at)
        reg_t = place("reg_t", [96, 2, NREG], f32, at)
        reg_v = place("reg_v", [NREG, D], f32, at)
        assert at[0] <= top, at[0]

        at = [stage]
        w2_sb = place("w2_sb", [128, EX, 4, D], f32, at)
        after_w2 = at[0]
        at = [stage]
        rt = [place(f"rt{i}", [128, NT, E], f32, at) for i in range(6)]
        rt_m = place("rt_m", [128, E, NT], bf16, at)
        total = place("total", [128, E, NT], f32, at)
        incl = place("incl", [128, E, NT], f32, at)
        seg = place("seg", [128, E, NT], f32, at)
        first_row = place("first_row", [128, E, NT], f32, at)
        rs1 = [place(f"rs1_{i}", [128, NT], f32, at) for i in range(4)]
        top_w = place("top_w", [128, NT, 2], f32, at)
        pos_f = place("pos_f", [128, NT, 2], f32, at)
        pos_i = place("pos_i", [128, NT, 2], i32, at)
        pos_hi = place("pos_hi", [128, NT, 2], i32, at)
        pos_lo = place("pos_lo", [128, NT, 2], i32, at)
        cnt_i = place("cnt_i", [128, E], i32, at)
        cnt = [place(f"cnt{i}", [128, E], f32, at) for i in range(4)]
        slot_cmp = place("slot_cmp", [128, SLOTS, E], f32, at)
        slot_f = place("slot_f", [128, SLOTS], f32, at)
        assert at[0] <= after_w2
        at = [after_w2]
        c_x2 = place("c_x2", [128, 3, D], f32, at)
        at = [max(b_end, at[0])]
        sw13_sb = place("sw13_sb", [96, 2, 2, SINTER], f32, at)
        sw2_sb = place("sw2_sb", [128, 8, D], f32, at)
        c_x = place("c_x", [96, 2, 2, BAND], f32, at)
        assert at[0] <= top, at[0]
        at = [max(b_end, after_w2)]
        xg = place("xg", [128, V4, XW], f32, at)
        xa = place("xa", [128, 2, 128], f32, at)
        xb1 = place("xb1", [128, 2, 128], f32, at)
        xb3 = place("xb3", [128, 2, 128], f32, at)
        m_sg = place("m_sg", [128, 2, INTER], f32, at)
        m_h = place("m_h", [128, 2, INTER], f32, at)
        m_hT = place("m_hT", [128, 2, INTER], f32, at)
        ys = place("ys", [128, V4, D], f32, at)
        gidx = place("gidx", [128, V4, 1], i32, at)
        assert at[0] <= nc.sbuf_usable_end
        ps = ctx.enter_context(nc.psum_tensor("ps", [128, 8, 512], f32))

        s_const = sem("s_const")
        s_zero = sem("s_zero")
        s_pad = sem("s_pad")
        r_ps = sem("r_ps")
        r_k = sem("r_k")
        r_kst = sem("r_kst")
        s_bq = sem("s_bq")
        s_ksp = sem("s_ksp")
        r_v = sem("r_v")
        r_vin = sem("r_vin")
        s_kpad = sem("s_kpad")
        a_xld = sems("a_xld", 2)
        a_var = sem("a_var")
        a_pow = sem("a_pow")
        b_var = sem("b_var")
        b_pow = sem("b_pow")
        s_half = sem("s_half")
        s_oz = sem("s_oz")
        a_norm = sem("a_norm")
        a_xTps = sem("a_xTps")
        a_xnTev = sem("a_xnTev")
        a_qps = sems("a_qps", 2)
        a_qev = sems("a_qev", 2)
        a_kps = sems("a_kps", 2)
        a_kev = sems("a_kev", 2)
        a_q1, a_q2, a_q3, a_qres = (sem(f"a_{n}") for n in ("q1", "q2", "q3", "qres"))
        a_k1, a_k2, a_k3, a_kres = (sem(f"a_{n}") for n in ("k1", "k2", "k3", "kres"))
        a_st1 = sems("a_st1", 2)
        a_st23 = sems("a_st23", 2)
        a_vps = sems("a_vps", 2)
        a_vev = sems("a_vev", 2)
        a_vst = sems("a_vst", 2)
        dve_s = sem("dve_s")
        b_qld = sems("b_qld", 3)
        b_kld = sems("b_kld", 3)
        b_xld = sems("b_xld", 3)
        b_xb = sem("b_xb")
        b_vld = sems("b_vld", 3)
        b_S = sems("b_S", 2)
        b_O = sems("b_O", 2)
        b_nm = sem("b_nm")
        b_exp = sems("b_exp", 2)
        b_T = sems("b_T", 2)
        b_TevD = sem("b_TevD")
        b_TevA = sem("b_TevA")
        b_rsum = sem("b_rsum")
        b_R = sem("b_R")
        b_oraw = sem("b_oraw")
        b_oTev = sem("b_oTev")
        b_Pps = sem("b_Pps")
        b_x2 = sem("b_x2")
        b_xn2 = sem("b_xn2")
        b_xTevD = sem("b_xTevD")
        b_xTevA = sem("b_xTevA")
        b_lg = sem("b_lg")
        b_x2st = sems("b_x2st", 3)
        b_xn2st = sems("b_xn2st", 3)
        b_xTst = sems("b_xTst", 3)
        r_sub = sem("r_sub")
        r_exp = sem("r_exp")
        r_m = sem("r_m")
        r_tot = sem("r_tot")
        r_totc = sem("r_totc")
        r_rank = sem("r_rank")
        r_done = sem("r_done")
        l_init = sem("l_init")
        l_cp = sem("l_cp")
        l_sc = sems("l_sc", 2)
        l_back = sem("l_back")
        c_w = sem("c_w")
        c_xld = sems("c_xld", 2)
        c_x2ld = sem("c_x2ld")
        c_a = sems("c_a", 2)
        c_b = sems("c_b", 2)
        c_silu = sems("c_silu", 2)
        c_h = sems("c_h", 2)
        c_zps = sems("c_zps", 2)
        c_z = sems("c_z", 2)
        c_acc = sem("c_acc")
        d_w = sem("d_w")
        d_half = sem("d_half")
        d_ix = sem("d_ix")
        d_g = sems("d_g", V4)
        d_xTps = sems("d_xTps", 2)
        d_xTev = sems("d_xTev", 2)
        d_a = sems("d_a", 2)
        d_b = sems("d_b", 2)
        d_silu = sems("d_silu", 2)
        d_h = sems("d_h", 2)
        d_hTps = sems("d_hTps", 2)
        d_hTev = sem("d_hTev")
        d_yps = sems("d_yps", 2)
        d_y = sem("d_y")
        d_sc = sems("d_sc", V4)
        s_out = sem("s_out")
        passed_pool = sem("passed_pool")
        passed_dve = sem("passed_dve")

        pair_stage = place("pair_stage", [128, 2, 2, 2], i32, [top])
        idx_stage = place("idx_stage", [128, 2, 2], i32, [top + 64])

        def patch(dram, i, c, w):
            return dram[ds(i * BAND, BAND), :].rearrange("(r c) d -> r c d", c=SIDE)[
                :, QC * c:QC * (c + 1), 0:w]

        def head(p, hh):
            h = 2 * p + hh
            return h // 4, 32 * (h % 4)

        def back(i, c):
            return (i, c - 1) if c else (i - 1, 2)

        def back2(i, c):
            return (i, 0) if c == 2 else (i - 1, c + 1)

        def pair_back(i, c, p, k):
            if p >= k:
                return i, c, p - k
            return None if type(i) is int and i + c == 0 else (*back(i, c), p - k + 6)

        def tails(i, c):
            return min(3 * i + c, 2) if type(i) is int else 2

        def turns(eng, n, body, last=None, apart=1):
            for j in range(apart):
                body(j)
            with eng.Fori(apart, n - 1 if last else n) as j:
                body(j)
            if last:
                last(n - 1)

        def upto(n):
            return max(n + 1, 0) if type(n) is int else n + 1

        def one_back(u, j):
            return 1 - u, j + u - 1

        def windows(a):
            rows = a.rearrange("p g (r c) -> p (g r) c", c=SIDE)
            return [rows[:, :, KC0[c]:KC0[c] + KC] for c in range(3)]

        block = ctx.enter_context(nc.Block())

        @block.sync
        def _(sp):
            for dst, src in ((wqk_sb, wqk), (bqk_sb, bqk), (wv_sb, wv), (bv_sb, bv), (wo_sb, wo), (bo_sb, bo),
                             (gate_sb, gate_t), (ident_sb, ident), (tri_sb, tri.bitcast(bf16)),
                             (ids_sb, token_ids), (iotae_sb, iota_e), (iotas_sb, iota_s), (reg_t, kv_reg_t)):
                sp.dma_start(dst[:], src).then_inc(s_const, 16)
            sp.dma_start(list_dram.rearrange("(p s) w -> p (s w)", p=128), list_init).then_inc(l_init, 16)

            def load_band(n, u, j):
                sp.wait_ge(a_norm, upto(n - 2))
                sp.dma_start(a_x[:, u, :, :], x[ds(n * BAND, BAND), :].rearrange(
                    "(s p) d -> p s d", p=128)).then_inc(a_xld[u], 16)

            def store_parts(n, u, parts, stored):
                for s in parts:
                    sp.wait_ge((a_q1, a_q2, a_q3)[s], n + 1)
                    sp.dma_start(q_dram[s, :, :, ds(3 * n, 3), :].rearrange("g p c x -> p g (c x)"),
                                 a_qs[:, u, s, :, :, :].rearrange("p g c x -> p g (c x)")).then_inc(stored[u], 16)
                    sp.wait_ge((a_k1, a_k2, a_k3)[s], n + 1)
                    for g in range(2):
                        sp.dma_start(k_dram[s, g, :, :, ds(WR * n + HALO * KC, WR)],
                                     a_ks[:, u, s, :, g, :]).then_inc(stored[u], 16)

            sp.dma_start(qsp[96:120, :, :, :].rearrange("p c h x -> p (c h) x"),
                         mask_q.bitcast(bf16).unsqueeze(1).broadcast_to([24, 3 * H, 128])).then_inc(s_ksp, 16)
            load_band(0, 0, 0)
            load_band(1, 1, 0)
            sp.wait_ge(r_k, 1)
            sp.dma_start(kreg_dram.rearrange("s g p x -> p (s g) x"),
                         reg_ks[:, :, :, :].rearrange("p s g x -> p (s g) x")).then_inc(r_kst, 16)
            sp.wait_ge(r_kst, 16)
            for c in range(3):
                for b in range(6):
                    sp.dma_start(ksp[HD * b:HD * (b + 1), c, :, NKEY:NKEY + NREG],
                                 kreg_dram[K_PART[b]].rearrange("g (h d) x -> d (g h) x", d=HD)
                                 ).then_inc(s_ksp, 16)

            def store_1(n, u):
                store_parts(n, u, (0,), a_st1)

            def store_23(n, u):
                store_parts(n, u, (1, 2), a_st23)

            def bands(j):
                for u in range(2):
                    load_band(2 * j + u, u, j)
                    store_23(2 * j + u - 4, u)
                    store_1(2 * j + u - 2, u)

            sp.wait_ge(s_zero, 1)
            sp.dma_start(v_dram[0:PADT, :].rearrange("(p a) d -> p (a d)", a=2),
                         zeros[0:PADT // 2, :]).then_inc(s_pad, 16)
            sp.dma_start(v_dram[PADT + T:2 * PADT + T, :].rearrange("(p a) d -> p (a d)", a=2),
                         zeros[0:PADT // 2, :]).then_inc(s_pad, 16)
            sp.dma_start(xn_dram[T:T + 128, :], zeros[:, 0:XW]).then_inc(s_pad, 16)
            sp.dma_start(acc_dram[T:T + 128, :], zeros[:, 0:D]).then_inc(s_pad, 16)
            sp.wait_ge(r_v, 1)
            sp.wait_ge(s_kpad, 2)
            for c in range(3):
                sp.dma_start(vst[NKEY - 2 * CH:NKEY - 2 * CH + NREG, c, 2, :], reg_v[:, :]).then_inc(r_vin, 16)
            for side in range(2):
                at0 = (WR * NB + HALO * KC) * side
                for s, g in itertools.product(range(3), range(2)):
                    sp.dma_start(k_dram[s, g, :, :, at0:at0 + HALO * KC],
                                 zeros[0:96, 0:3 * HALO * KC // 2].bitcast(bf16).rearrange(
                                     "p (c x) -> p c x", c=3)).then_inc(s_pad, 16)
            load_band(2, 0, 1)
            load_band(3, 1, 1)
            store_1(0, 0)
            store_1(1, 1)
            with sp.Fori(2, NB // 2) as j:
                bands(j)

            def tile_in(i, c):
                sp.wait_ge(b_S[1], 3 * upto(3 * i + c - 3))
                sp.dma_start(ksp[96:120, c, :, :], mask_k[:, ds((i * 3 + c) * KW, KW)].bitcast(bf16).unsqueeze(
                    1).broadcast_to([24, H, KW])).then_inc(b_kld[c], 16)
                for b in range(6):
                    sp.dma_start(ksp[HD * b:HD * (b + 1), c, :, 0:NKEY],
                                 k_dram[K_PART[b], :, :, c, ds(WR * i, NKEY)].rearrange(
                                     "g (h d) x -> d (g h) x", d=HD)).then_inc(b_kld[c], 16)
                sp.wait_ge(b_xb, upto(3 * i + c - 3))
                sp.dma_start(x_p[:, c, :], patch(x, i, c, D)).then_inc(b_xld[c], 16)
                sp.wait_ge(b_O[1], 3 * upto(3 * i + c - 3))
                keys = v_dram[ds(i * BAND, KR * SIDE), :].rearrange("(r c) d -> r c d", c=SIDE)
                for k in range(3):
                    rows = min(5, KR - 5 * k)
                    sp.dma_start(vst[0:rows * KC, c, k, :],
                                 keys[5 * k:5 * k + rows, KC0[c]:KC0[c] + KC, :]).then_inc(b_vld[c], 16)

            def tile_out(i, c):
                m = 3 * i + c
                sp.wait_ge(b_x2, m + 1)
                sp.dma_start(patch(acc_dram, i, c, D), x2[:, c, :]).then_inc(b_x2st[c], 16)
                sp.wait_ge(b_xn2, 2 * m + 2)
                sp.dma_start(patch(xn_dram, i, c, XW), xn2[:, c, :]).then_inc(b_xn2st[c], 16)
                sp.wait_ge(b_xTevD, m + 1)
                sp.wait_ge(b_xTevA, m + 1)
                sp.dma_start(xt_dram[:, :, ds(m * 128, 128)], xn2T[:, c, :, :]).then_inc(b_xTst[c], 16)

            sp.wait_ge(r_vin, 48)
            sp.wait_ge(s_pad, 16 * 16)
            for u in range(2):
                sp.wait_ge(a_vst[u], 16)
                sp.wait_ge(a_st1[u], 48)
                sp.wait_ge(a_st23[u], 96)
            store_23(NB - 4, 0)
            tile_in(0, 0)
            store_1(NB - 2, 0)
            store_23(NB - 3, 1)
            tile_in(0, 1)
            store_1(NB - 1, 1)
            store_23(NB - 2, 0)
            tile_in(0, 2)
            store_23(NB - 1, 1)
            for u in range(2):
                sp.wait_ge(a_vst[u], 16 * NB // 2)
                sp.wait_ge(a_st1[u], 48 * NB // 2)
                sp.wait_ge(a_st23[u], 96 * NB // 2)
            sp.wait_ge(b_S[0], 1)
            sp.dma_start(sw13_sb[:], sw13).then_inc(c_w, 16)
            sp.dma_start(sw2_sb[:], sw2).then_inc(c_w, 16)
            with sp.Fori(1, NB) as i:
                for c in range(3):
                    tile_in(i, c)
                    tile_out(i - 1, c)
            for c in range(3):
                tile_out(NB - 1, c)

            sp.wait_ge(b_lg, NT)
            for c in range(3):
                sp.wait_ge(b_x2st[c], 16 * NB)
                sp.wait_ge(b_xn2st[c], 16 * NB)
                sp.wait_ge(b_xTst[c], 16 * NB)

            def c_rest(n, u, j, w13, w_2):
                sp.wait_ge(c_acc, 48 * n)
                for s in range(3):
                    sp.dma_start(c_x2[:, s, :], patch(acc_dram, n, s, D)).then_inc(c_x2ld, 16)
                if w13:
                    sp.dma_start(w13a_sb[:, ds(2 * n, 2), :, :], w13a[:, ds(2 * n, 2), :, :]).then_inc(d_w, 16)
                    sp.dma_start(w13b_sb[:, ds(2 * n, 2), :], w13b[:, ds(2 * n, 2), :]).then_inc(d_w, 16)
                if w_2:
                    sp.dma_start(w2_sb[:, ds(2 * n - NW, 2), :, :],
                                 w2[:, ds(2 * n - NW, 2), :, :]).then_inc(d_w, 16)
                for s in range(3):
                    w = 3 * u + s
                    sp.wait_ge(c_z[w % 2], 3 * j + w // 2 + 1)
                    sp.dma_start(patch(acc_dram, n, s, D), c_x2[:, s, :]).then_inc(c_acc, 16)

            sp.dma_start(c_x[:, 0, :, :], xt_dram[:, :, 0:BAND]).then_inc(c_xld[0], 16)
            sp.dma_start(c_x[:, 1, :, :], xt_dram[:, :, BAND:2 * BAND]).then_inc(c_xld[1], 16)

            def c_step(j, w13, w_2, more=True):
                for u in range(2):
                    n = 2 * j + u
                    c_rest(n, u, j, w13, w_2)
                    if more:
                        sp.dma_start(c_x[:, u, :, :],
                                     xt_dram[:, :, ds((n + 2) * BAND, BAND)]).then_inc(c_xld[u], 16)

            NW = 2 * (NB - EX // 2)
            c_step(0, True, False)
            c_step(1, True, False)
            sp.wait_ge(r_done, 1)
            with sp.Fori(2, 4) as j:
                c_step(j, True, True)
            c_step(4, False, True)
            c_step(5, False, True, False)

            for v in range(V4):
                sp.wait_ge(d_sc[v], 16 * SLOTS // V4)
            sp.dma_start(out, acc_dram[0:T, :]).then_inc(s_out, 16)
            sp.wait_ge(s_out, 16)

        @block.gpsimd
        def _(pool):
            nc.gpsimd.memset(zeros[:], 0.0).then_inc(s_zero, 1)
            nc.gpsimd.memset(vst[:, :, 2, :], 0.0).then_inc(s_kpad, 1)
            nc.gpsimd.memset(ksp[0:96, :, :, NKEY + NREG:].rearrange("p c h x -> p (c h) x"), 0.0).then_inc(s_kpad, 1)
            nc.gpsimd.memset(minus_half[:], -0.5).then_inc(s_half, 1)
            pool.wait_ge(s_half, 1)

            def load_q(i, c, blocks=range(6)):
                pool.wait_ge(b_S[1], 3 * upto(3 * i + c - 3))
                for b in blocks:
                    pool.dma_start(qsp[HD * b:HD * (b + 1), c, :, :],
                                   q_dram[Q_PART[b], :, :, ds(3 * i + c, 1), :].rearrange(
                                       "g (h d) n x -> d (g h) (n x)", d=HD)).then_inc(b_qld[c], 16)

            def store_v(j, tile=None, last=False):
                for u in range(2):
                    if not (last and u):
                        root_a(2 * j + u + 1)
                    if type(j) is not int or j or u:
                        second_q(*one_back(u, j))
                    pool.wait_ge(a_vev[0], 3 * j + 2 + u)
                    pool.wait_ge(a_vev[1], 3 * j + 1 + 2 * u)
                    pool.dma_start(v_dram[ds(PADT + (2 * j + u) * BAND, BAND), :].rearrange(
                        "(s p) d -> p s d", p=128), a_v[:, u, :, :]).then_inc(a_vst[u], 16)
                    if tile is not None:
                        if tile + u == 0:
                            pool.wait_ge(a_st1[0], 48)
                            pool.wait_ge(a_st23[0], 96)
                        load_q(0, tile, range(3 * u, 3 * u + 3))

            def second_q(u, j):
                pool.wait_ge(a_qres, 2 * j + u + 1)
                pool.wait_ge(a_st23[u], 96 * j)
                pool.sem_inc(passed_pool, 1)
                nc.gpsimd.tensor_copy(a_qs[:, u, 1, :, :, :].rearrange("p c g x -> p (c g x)"),
                                      a_qr[:, u, :, :, :].rearrange("p c g x -> p (c g x)")).then_inc(a_q2, 1)

            def root_a(n):
                pool.wait_ge(a_var, n + 1)
                nc.gpsimd.tensor_tensor(a_rs[:, :], a_ve[:, :], minus_half[:, :], ALU.pow).then_inc(a_pow, 1)

            root_a(0)
            turns(pool, NB // 2 - 1, store_v, lambda j: store_v(j, 0), apart=2)
            store_v(NB // 2 - 1, 1, True)
            second_q(1, NB // 2 - 1)

            pool.wait_ge(s_const, 16 * 13)

            def root(i, c):
                pool.wait_ge(b_var, 3 * i + c + 1)
                nc.gpsimd.tensor_tensor(b_rs[:, :], b_ve[:, :], minus_half[:, 0:1], ALU.pow).then_inc(b_pow, 1)

            def stage_tile(i, c):
                pool.wait_ge(b_xld[c], 16 * i + 16)
                pool.wait_ge(b_x2, upto(3 * i + c - 3))
                nc.gpsimd.tensor_tensor(xb[:, c, :], x_p[:, c, :], bo_sb[:, :], ALU.add).then_inc(b_xb, 1)

            load_q(0, 2)
            for u in range(2):
                pool.wait_ge(a_st1[u], 48 * NB // 2)
                pool.wait_ge(a_st23[u], 96 * NB // 2)
            for c in range(3):
                stage_tile(0, c)
            root(0, 0)
            with pool.Fori(1, NB) as i:
                for c in range(3):
                    load_q(i, c)
                    stage_tile(i, c)
                    root(*back2(i, c))
            root(NB - 1, 1)
            root(NB - 1, 2)

            pool.wait_ge(r_done, 1)
            pool.wait_ge(l_init, 16)
            def scatter(j):
                for u in range(2):
                    n = 2 * j + u
                    pool.wait_ge(l_sc[u], 32 * j)
                    nc.gpsimd.tensor_copy(idx_stage[:, u, :], pair_idx[:, ds(n, 1), :].squeeze(1)).then_inc(l_cp, 1)
                    nc.gpsimd.tensor_copy(pair_stage[:, u, :, :].rearrange("p a b -> p (a b)"),
                                          pair_val[:, ds(n, 1), :, :].rearrange("p n a b -> p (n a b)")
                                          ).then_inc(l_cp, 1)
                    pool.wait_ge(l_cp, 2 * n + 2)
                    pool.sem_inc(passed_pool, 1)
                    for k in range(2):
                        nc.gpsimd.indirect_dma_start(
                            list_dram, bass.IndirectOffsetOnAxis(ap=idx_stage[:, u, k:k + 1], axis=0),
                            pair_stage[:, u, k, :], None).then_inc(l_sc[u], 16)

            turns(pool, NT // 2, scatter)
            for u in range(2):
                pool.wait_ge(l_sc[u], 32 * NT // 2)
            pool.dma_start(lists[:, :, :].rearrange("p s w -> p (s w)"),
                           list_dram.rearrange("(p s) w -> p (s w)", p=128)).then_inc(l_back, 16)
            pool.wait_ge(l_back, 16)
            for r in range(2):
                pool.wait_ge(c_z[r], 3 * NB // 2)
            pool.wait_ge(c_acc, 48 * NB)
            nc.gpsimd.memset(xb1[64:128, :, :], 0.0).then_inc(d_half, 1)
            pool.wait_ge(d_half, 1)
            nc.gpsimd.memset(xb3[0:64, :, :], 0.0).then_inc(d_half, 1)
            pool.wait_ge(d_half, 2)

            def gather(j, v, g):
                pool.wait_ge(d_sc[v], 16 * g)
                nc.gpsimd.tensor_copy(gidx[:, v, :], lists[:, ds(j, 1), 0]).then_inc(d_ix, 1)
                pool.wait_ge(d_ix, j + 1)
                pool.wait_ge(d_xTps[v % 2], 2 * g + v // 2)
                pool.sem_inc(passed_pool, 1)
                nc.gpsimd.indirect_dma_start(xg[:, v, :], None, xn_dram, bass.IndirectOffsetOnAxis(
                    ap=gidx[:, v, 0:1], axis=0)).then_inc(d_g[v], 16)

            def add_rows(j, v, g, first=False):
                pool.wait_ge(d_y, j + 1)
                if not first:
                    pool.wait_ge(d_sc[(v - 1) % V4], 16 * (g if v == 0 else g + 1))
                pool.sem_inc(passed_pool, 1)
                nc.gpsimd.indirect_dma_start(acc_dram, bass.IndirectOffsetOnAxis(
                    ap=gidx[:, v, 0:1], axis=0), ys[:, v, :], None, compute_op=ALU.add).then_inc(d_sc[v], 16)

            gather(0, 0, 0)
            gather(1, 1, 0)

            def d_step(g, first, last):
                for v in range(V4):
                    j = V4 * g + v
                    if not (last and v >= V4 - 2):
                        gather(j + 2, (v + 2) % V4, g + (v + 2) // V4)
                    if v:
                        add_rows(j - 1, v - 1, g, first and v == 1)
                    elif not first:
                        add_rows(j - 1, V4 - 1, g - 1)

            d_step(0, True, False)
            with pool.Fori(1, SLOTS // V4 - 1) as g:
                d_step(g, False, False)
            d_step(SLOTS // V4 - 1, False, True)
            add_rows(SLOTS - 1, V4 - 1, SLOTS // V4 - 1)

        @block.scalar
        def _(act):
            act.wait_ge(s_const, 16 * 13)
            act.wait_ge(s_bq, 1)

            def xnT_out(u, j):
                act.wait_ge(a_xTps, 2 * j + u + 1)
                nc.scalar.copy(a_xnT[:, u, :, :], ps[0:96, 0:2, 0:BAND]).then_inc(a_xnTev, 1)

            def second_k(u, j):
                act.wait_ge(a_kres, 2 * j + u + 1)
                act.wait_ge(a_st23[u], 96 * j)
                nc.scalar.copy(a_ks[:, u, 1, :, :, :].rearrange("p c g x -> p (c g x)"),
                               a_kr[:, u, :, :, :].rearrange("p c g x -> p (c g x)")).then_inc(a_k2, 1)

            def qk_out(j, last=False):
                for u in range(2):
                    act.wait_ge(a_qres, upto(2 * j + u - 2))
                    act.wait_ge(a_kres, upto(2 * j + u - 2))
                    for g in range(2):
                        act.wait_ge(a_qps[g], 2 * j + u + 1)
                        nc.scalar.activation(a_qf[:, u, g, :], ps[0:96, 2 + g, 0:BAND], ACT.Identity,
                                             bias=bq_scaled[:, g:g + 1], scale=0.25).then_inc(a_qev[g], 1)
                        if g == 1:
                            if not (last and u):
                                xnT_out(1 - u, j + u)
                        act.wait_ge(a_kps[g], 2 * j + u + 1)
                        nc.scalar.activation(a_kf[:, u, g, :], ps[0:96, 4 + g, 0:BAND], ACT.Identity,
                                             bias=bqk_sb[:, 2 + g:3 + g]).then_inc(a_kev[g], 1)
                    if type(j) is not int or j or u:
                        second_k(*one_back(u, j))
                    act.wait_ge(a_st1[u], 48 * j)
                    for g in range(2):
                        act.wait_ge(a_qev[g], 2 * j + u + 1)
                        act.wait_ge(a_kev[g], 2 * j + u + 1)
                    for c in range(3):
                        q = a_qf[:, u, :, :].rearrange("p g (r c) -> p g r c", c=SIDE)[:, :, :, QC * c:QC * (c + 1)]
                        ins = nc.scalar.copy(a_qs[:, u, 0, :, c, :].rearrange("p g (r c) -> p g r c", c=QC), q)
                    ins.then_inc(a_q1, 1)
                    for c in range(3):
                        ins = nc.scalar.copy(a_ks[:, u, 0, c, :, :].rearrange("p g (r c) -> p (g r) c", c=KC),
                                             windows(a_kf[:, u, :, :])[c])
                    ins.then_inc(a_k1, 1)

            xnT_out(0, 0)
            turns(act, NB // 2, qk_out, lambda j: qk_out(j, True), apart=2)
            second_k(1, NB // 2 - 1)

            def probsT_odd(i, c, p):
                n = 3 * i + c
                act.wait_ge(b_T[1], 6 * n + p + 1)
                if p == 1 and tails(i, c) > 1:
                    tail_xT(*back2(i, c))
                if type(n) is not int or n or p > 1:
                    act.wait_ge(b_O[p % 2], 3 * n + p // 2)
                nc.scalar.copy(probsT[0:CH, p % 2, 1, :], ps[0:CH, 5, 0:3 * 128]).then_inc(b_TevA, 1)

            def b_tile(i, c):
                n = 3 * i + c
                for p in range(6):
                    act.wait_ge(b_nm, 6 * n + p + 1)
                    for hh in range(2):
                        ins = nc.scalar.activation(probs[:, p % 2, hh, :], ps[:, 2 * (p % 2) + hh, 0:KW], ACT.Exp,
                                                   bias=nmax[:, p % 2, hh:hh + 1],
                                                   accum_out=sums[:, c, 2 * p + hh:2 * p + hh + 1])
                    ins.then_inc(b_exp[p % 2], 1)
                    if p == 2 and tails(i, c):
                        tail_oraw(*back(i, c))
                    if pair_back(i, c, p, 1):
                        probsT_odd(*pair_back(i, c, p, 1))

            def tail_oraw(i, c):
                act.wait_ge(b_O[1], 3 * (3 * i + c) + 3)
                act.wait_ge(b_oTev, 3 * i + c)
                nc.scalar.copy(o_raw[:, :], ps[:, 6, 0:3 * 128]).then_inc(b_oraw, 1)

            def tail_xT(i, c):
                act.wait_ge(b_xTst[c], 16 * i)
                nc.scalar.copy(xn2T[:, c, 1, :], ps[0:96, 5, 384:512]).then_inc(b_xTevA, 1)

            for n in range(6):
                b_tile(n // 3, n % 3)
            with act.Fori(2, NB) as i:
                for c in range(3):
                    b_tile(i, c)
            act.wait_ge(b_T[1], 6 * NT)
            tail_xT(NB - 1, 1)
            probsT_odd(NB - 1, 2, 5)
            tail_oraw(NB - 1, 2)
            act.wait_ge(b_T[1], 6 * NT + 1)
            tail_xT(NB - 1, 2)

            act.wait_ge(r_sub, 1)
            nc.scalar.activation(rt[1][:], rt[0][:], ACT.Exp).then_inc(r_exp, 1)

            def silus(n):
                for m in range(8):
                    act.wait_ge(c_a[m % 2], 4 * n + m // 2 + 1)
                    act.wait_ge(c_h[m % 2], 4 * n + m // 2)
                    nc.scalar.activation(s_sg[:, m % 2, :], ps[:, m % 2, 0:BAND],
                                         ACT.Silu).then_inc(c_silu[m % 2], 1)

            def xT_split(v, g):
                q = 2 * g + v // 2
                act.wait_ge(d_xTps[v % 2], q + 1)
                act.wait_ge(d_b[v % 2], q)
                bank = 6 + v % 2
                nc.scalar.copy(xa[:, v % 2, :], ps[:, bank, 0:128]).then_inc(d_xTev[v % 2], 1)
                nc.scalar.copy(xb1[0:64, v % 2, :], ps[0:64, bank, 128:256]).then_inc(d_xTev[v % 2], 1)
                nc.scalar.copy(xb3[64:128, v % 2, :], ps[64:128, bank, 128:256]).then_inc(d_xTev[v % 2], 1)

            def d_step(g, last):
                for v in range(V4):
                    q = 2 * g + v // 2
                    act.wait_ge(d_a[v % 2], q + 1)
                    act.wait_ge(d_h[v % 2], q)
                    nc.scalar.activation(m_sg[:, v % 2, :], ps[:, v % 2, :], ACT.Silu).then_inc(d_silu[v % 2], 1)
                    if not (last and v == V4 - 1):
                        xT_split((v + 1) % V4, g + (v + 1) // V4)

            turns(act, NB, silus)
            xT_split(0, 0)
            turns(act, SLOTS // V4, lambda g: d_step(g, False), lambda g: d_step(g, True))

        @block.vector
        def _(dve):
            start, steps = [0], [0]

            def count_from(n):
                start[0], steps[0] = n, 0

            def signal(ins):
                steps[0] += 1
                ins.then_inc(dve_s, 1)

            def signalled():
                dve.wait_ge(dve_s, start[0] + steps[0])

            def step(ins):
                signal(ins)
                signalled()

            dve.wait_ge(s_const, 16 * 13)
            dve.wait_ge(r_ps, 1)
            nc.vector.tensor_tensor(reg_v[:, :], ps[0:NREG, 3, 0:D], bv_sb[0:NREG, :], ALU.add).then_inc(r_v, 1)
            nc.vector.tensor_scalar(bq_scaled[:, :], bqk_sb[:, 0:2], 0.25, None, ALU.mult).then_inc(s_bq, 1)
            for g in range(2):
                ins = nc.vector.tensor_scalar(reg_kf[:, g, :], ps[0:96, 2, NREG * g:NREG * (g + 1)],
                                              bqk_sb[:, 2 + g:3 + g], None, ALU.add)
            step(ins)
            step(nc.vector.tensor_copy(reg_ks[:, 0, :, :], reg_kf[:, :, :]))
            step(nc.vector.tensor_tensor(reg_kr[:, :, :], reg_kf[:, :, :], reg_ks[:, 0, :, :], ALU.subtract))
            step(nc.vector.tensor_copy(reg_ks[:, 1, :, :], reg_kr[:, :, :]))
            nc.vector.tensor_tensor(reg_ks[:, 2, :, :], reg_kr[:, :, :], reg_ks[:, 1, :, :],
                                    ALU.subtract).then_inc(r_k, 1)

            REG_STEPS = 4
            A_STEPS = 2

            def stats(n, u, j):
                count_from(REG_STEPS + A_STEPS * n)
                dve.wait_ge(a_xld[u], 16 * j + 16)
                for s in range(3):
                    ins = nc.vector.bn_stats(a_st[:, s, :], a_x[:, u, s, :])
                step(ins)
                dve.sem_inc(passed_dve, 1)
                for s in range(3):
                    ins = nc.vector.bn_aggr(a_mv[:, s, :], a_st[:, s, :])
                step(ins)
                nc.vector.tensor_scalar(a_ve[:, :], a_mv[:, :, 1], 1e-6, None, ALU.add).then_inc(a_var, 1)

            def normalize(n, u, j):
                dve.wait_ge(a_pow, n + 1)
                dve.wait_ge(a_xTps, upto(n - 2))
                for s in range(3):
                    ins = nc.vector.tensor_scalar(a_xn[:, u, s, :], a_x[:, u, s, :], a_mv[:, s, 0:1],
                                                  a_rs[:, s:s + 1], ALU.subtract, ALU.mult)
                ins.then_inc(a_norm, 1)

            def first_left(u, j):
                dve.wait_ge(a_q1, 2 * j + u + 1)
                for c in range(3):
                    q = a_qf[:, u, :, :].rearrange("p g (r c) -> p g r c", c=SIDE)[:, :, :, QC * c:QC * (c + 1)]
                    ins = nc.vector.tensor_tensor(a_qr[:, u, :, c, :].rearrange("p g (r c) -> p g r c", c=QC), q,
                                                  a_qs[:, u, 0, :, c, :].rearrange("p g (r c) -> p g r c", c=QC),
                                                  ALU.subtract)
                ins.then_inc(a_qres, 1)
                dve.wait_ge(a_k1, 2 * j + u + 1)
                for c in range(3):
                    ins = nc.vector.tensor_tensor(a_kr[:, u, c, :, :].rearrange("p g (r c) -> p (g r) c", c=KC),
                                                  windows(a_kf[:, u, :, :])[c],
                                                  a_ks[:, u, 0, c, :, :].rearrange("p g (r c) -> p (g r) c", c=KC),
                                                  ALU.subtract)
                ins.then_inc(a_kres, 1)

            def third(u, j):
                for left, parts, second, made in ((a_qr, a_qs, a_q2, a_q3), (a_kr, a_ks, a_k2, a_k3)):
                    dve.wait_ge(second, 2 * j + u + 1)
                    nc.vector.tensor_tensor(*(a.rearrange("p c g x -> p (c g x)") for a in (
                        parts[:, u, 2, :, :, :], left[:, u, :, :, :], parts[:, u, 1, :, :, :])),
                        ALU.subtract).then_inc(made, 1)

            def v_out(j, last=False):
                for u in range(2):
                    n = 2 * j + u
                    before = type(j) is not int or j or u

                    def v_add(s):
                        w = 3 * u + s
                        dve.wait_ge(a_vps[w % 2], 3 * j + w // 2 + 1)
                        nc.vector.tensor_tensor(a_v[:, u, s, :], ps[:, 6 + w % 2, 0:D], bv_sb[:, :],
                                                ALU.add).then_inc(a_vev[w % 2], 1)

                    dve.wait_ge(a_vst[u], 16 * j)
                    v_add(0)
                    v_add(1)
                    if not (last and u):
                        stats(n + 1, 1 - u, j + u)
                        normalize(n + 1, 1 - u, j + u)
                    if type(j) is not int or j:
                        third(u, j - 1)
                    if before:
                        first_left(*one_back(u, j))
                    v_add(2)

            stats(0, 0, 0)
            normalize(0, 0, 0)
            turns(dve, NB // 2, v_out, lambda j: v_out(j, True), apart=2)
            dve.wait_ge(a_vev[0], 3 * NB // 2)
            nc.vector.memset(ps[:, 6, :], 0.0).then_inc(s_oz, 1)
            third(0, NB // 2 - 1)
            first_left(1, NB // 2 - 1)
            third(1, NB // 2 - 1)
            base_b = REG_STEPS + NB * A_STEPS
            B_STEPS = 3

            def probsT_even(i, c, p):
                n = 3 * i + c
                dve.wait_ge(b_T[0], 6 * n + p + 1)
                if p == 1 and tails(i, c) > 1:
                    tail_xT(*back2(i, c))
                if p == 3 and tails(i, c) > 1:
                    tail_logits(n - 2)
                if type(n) is not int or n or p > 1:
                    dve.wait_ge(b_O[p % 2], 3 * n + p // 2)
                nc.vector.tensor_copy(probsT[0:CH, p % 2, 0, :], ps[0:CH, 4, 0:3 * 128]).then_inc(b_TevD, 1)

            def tail_sums(i, c):
                dve.wait_ge(b_exp[1], 3 * (3 * i + c) + 3)
                signal(nc.vector.reciprocal(rsum1[:, :], sums[:, c, :]))

            def tail_rsum(i, c):
                signalled()
                dve.wait_ge(b_R, 3 * i + c)
                nc.vector.tensor_copy(rsum[:, :, :], rsum1[:, :].unsqueeze(2).broadcast_to([128, H, 32])
                                      ).then_inc(b_rsum, 1)

            def tail_oT(i, c):
                dve.wait_ge(b_oraw, 3 * i + c + 1)
                dve.wait_ge(b_R, 3 * i + c + 1)
                dve.wait_ge(b_Pps, 3 * i + c)
                nc.vector.tensor_tensor(oT[:, :, :].rearrange("p a b -> p (a b)"), o_raw[:, :],
                                        ps[:, 7, 0:3 * 128], ALU.mult).then_inc(b_oTev, 1)

            def tail_x2(i, c):
                dve.wait_ge(b_Pps, 3 * i + c + 1)
                dve.wait_ge(b_xb, 3 * i + c + 1)
                dve.wait_ge(b_x2st[c], 16 * i)
                nc.vector.tensor_tensor(x2[:, c, :], ps[:, 7, 0:D], xb[:, c, :], ALU.add).then_inc(b_x2, 1)

            def tail_stats(i, c):
                dve.wait_ge(b_x2, 3 * i + c + 1)
                signal(nc.vector.bn_stats(b_st[:, :], x2[:, c, :]))

            def tail_mean():
                signalled()
                dve.sem_inc(passed_dve, 1)
                signal(nc.vector.bn_aggr(b_mv[:, :], b_st[:, :]))

            def tail_var():
                signalled()
                nc.vector.tensor_scalar(b_ve[:, :], b_mv[:, 1:2], 1e-5, None, ALU.add).then_inc(b_var, 1)

            def tail_norm(i, c):
                dve.wait_ge(b_pow, 3 * i + c + 1)
                dve.wait_ge(b_xn2st[c], 16 * i)
                for lo, hi, at0 in ((0, D, 0), (128, D, D)):
                    nc.vector.tensor_scalar(xn2[:, c, at0:at0 + hi - lo], x2[:, c, lo:hi], b_mv[:, 0:1],
                                            b_rs[:, 0:1], ALU.subtract, ALU.mult).then_inc(b_xn2, 1)

            def tail_xT(i, c):
                dve.wait_ge(b_xTst[c], 16 * i)
                nc.vector.tensor_copy(xn2T[:, c, 0, :], ps[0:96, 4, 384:512]).then_inc(b_xTevD, 1)

            def tail_logits(m):
                nc.vector.tensor_copy(logits[:, ds(m, 1), :].squeeze(1), ps[:, 4, 384:384 + E]).then_inc(b_lg, 1)

            def b_tile(i, c):
                n = 3 * i + c
                if tails(i, c):
                    count_from(base_b + B_STEPS * (n - 1) - (1 if tails(i, c) > 1 else 0))
                for p in range(6):
                    dve.wait_ge(b_S[p % 2], 3 * n + p // 2 + 1)
                    nc.vector.tensor_reduce(nmax[:, p % 2, :], ps[:, 2 * (p % 2):2 * (p % 2) + 2, 0:KW],
                                            AX.X, ALU.max, negate=True).then_inc(b_nm, 1)
                    if p == 5 and tails(i, c):
                        tail_x2(*back(i, c))
                    if p == 0 and tails(i, c) > 1:
                        tail_mean()
                    if p == 1 and tails(i, c):
                        tail_sums(*back(i, c))
                    if pair_back(i, c, p, 2):
                        probsT_even(*pair_back(i, c, p, 2))
                    if p == 0 and tails(i, c) > 1:
                        tail_var()
                    if p == 1 and tails(i, c):
                        tail_rsum(*back(i, c))
                    if p == 1 and tails(i, c) > 1:
                        tail_norm(*back2(i, c))
                    if p == 3 and tails(i, c):
                        tail_oT(*back(i, c))
                    if p == 5 and tails(i, c):
                        tail_stats(*back(i, c))

            for n in range(6):
                b_tile(n // 3, n % 3)
            with dve.Fori(2, NB) as i:
                for c in range(3):
                    b_tile(i, c)
            count_from(base_b + B_STEPS * (NT - 1) - 1)
            tail_mean()
            probsT_even(NB - 1, 2, 4)
            tail_var()
            tail_norm(NB - 1, 1)
            dve.wait_ge(b_T[0], 6 * NT)
            tail_xT(NB - 1, 1)
            probsT_even(NB - 1, 2, 5)
            tail_sums(NB - 1, 2)
            tail_rsum(NB - 1, 2)
            dve.wait_ge(b_T[0], 6 * NT + 1)
            tail_logits(NT - 2)
            tail_oT(NB - 1, 2)
            tail_x2(NB - 1, 2)
            tail_stats(NB - 1, 2)
            tail_mean()
            tail_var()
            tail_norm(NB - 1, 2)
            dve.wait_ge(b_T[0], 6 * NT + 2)
            tail_xT(NB - 1, 2)
            dve.wait_ge(b_T[0], 6 * NT + 3)
            tail_logits(NT - 1)

            def wide(a):
                return a[:, :].unsqueeze(2).broadcast_to([128, NT, E])

            def narrow(a):
                return a.unsqueeze(1).broadcast_to([128, NT, E])

            def by_tile(a):
                return a[:].rearrange("p e n -> p n e")

            def flat(a):
                return a[:].rearrange("p e n -> p (e n)")

            half = E // 2 * NT
            v = nc.vector

            def scores_to_pairs():
                yield v.tensor_reduce(rs1[0][:], logits[:], AX.X, ALU.max)
                v.tensor_tensor(rt[0][:], logits[:], wide(rs1[0]), ALU.subtract).then_inc(r_sub, 1)
                yield v.memset(seg[:], 1.0)
                v.memset(seg[:, :, 0], 0.0)
                dve.wait_ge(r_exp, 1)
                yield v.tensor_reduce(rs1[0][:], rt[1][:], AX.X, ALU.add)
                yield v.reciprocal(rs1[1][:], rs1[0][:])
                yield v.tensor_tensor(rt[0][:], rt[1][:], wide(rs1[1]), ALU.mult)
                for k in range(2):
                    one_hot = rt[3 + k]
                    yield v.tensor_reduce(top_w[:, :, k], rt[0][:], AX.X, ALU.max)
                    yield v.tensor_tensor(rt[1][:], rt[0][:],
                                          top_w[:, :, k:k + 1].broadcast_to([128, NT, E]), ALU.not_equal)
                    yield v.scalar_tensor_tensor(rt[2][:], rt[1][:], float(2 * E), narrow(iotae_sb[:, :]),
                                                 ALU.mult, ALU.add)
                    yield v.tensor_reduce(rs1[2][:], rt[2][:], AX.X, ALU.min)
                    yield v.tensor_tensor(one_hot[:], narrow(iotae_sb[:, :]), wide(rs1[2]), ALU.is_equal)
                    if k == 0:
                        yield v.scalar_tensor_tensor(rt[0][:], one_hot[:], -2.0, rt[0][:], ALU.mult, ALU.add)
                v.tensor_tensor(by_tile(rt_m), rt[3][:], rt[4][:], ALU.add).then_inc(r_m, 1)

            def pairs_to_rows():
                dve.wait_ge(r_tot, 1)
                v.tensor_copy(flat(total).rearrange("p (a f) -> p a f", a=2), ps[:, 6:8, 0:half]
                              ).then_inc(r_totc, 1)
                dve.wait_ge(r_totc, 1)
                yield v.tensor_tensor_scan(flat(incl), flat(seg), flat(total), 0.0, ALU.mult, ALU.add)
                yield v.tensor_scalar(cnt_i[:, :], incl[:, :, NT - 1], 127.0, None, ALU.add)
                yield v.tensor_scalar(cnt_i[:, :], cnt_i[:, :], 7, None, ALU.arith_shift_right)
                yield v.tensor_copy(cnt[0][:, :], cnt_i[:, :])
                yield v.memset(cnt[2][:, :], 1.0)
                yield v.tensor_tensor_scan(cnt[1][:, :], cnt[2][:, :], cnt[0][:, :], 0.0, ALU.mult, ALU.add)
                yield v.tensor_tensor(cnt[3][:, :], cnt[1][:, :], cnt[0][:, :], ALU.subtract)
                yield v.tensor_tensor(first_row[:], incl[:], total[:], ALU.subtract)
                yield v.scalar_tensor_tensor(first_row[:], cnt[3][:, :].unsqueeze(2).broadcast_to([128, E, NT]),
                                             128.0, first_row[:], ALU.mult, ALU.add)
                dve.wait_ge(r_rank, 1)
                yield v.tensor_tensor(flat(first_row).rearrange("p (a f) -> p a f", a=2),
                                      flat(first_row).rearrange("p (a f) -> p a f", a=2),
                                      ps[:, 6:8, 0:half], ALU.add)
                for k in range(2):
                    yield v.tensor_tensor(rt[5][:], rt[3 + k][:], by_tile(first_row), ALU.mult)
                    yield v.tensor_reduce(pos_f[:, :, k], rt[5][:], AX.X, ALU.add)
                yield v.tensor_copy(pos_i[:], pos_f[:])
                v.tensor_scalar(pos_hi[:], pos_i[:], 7, None, ALU.arith_shift_right)
                yield v.tensor_scalar(pos_lo[:], pos_i[:], 127, None, ALU.bitwise_and)
                v.scalar_tensor_tensor(pair_idx[:], pos_lo[:], float(SLOTS), pos_hi[:], ALU.mult, ALU.add)
                for k in range(2):
                    v.tensor_copy(pair_val[:, :, k, 0], ids_sb[:, :])
                yield v.tensor_copy(pair_val[:, :, :, 1].bitcast(f32), top_w[:, :, :])
                yield v.tensor_tensor(slot_cmp[:], iotas_sb[:, :].unsqueeze(2).broadcast_to([128, SLOTS, E]),
                                      cnt[1][:, :].unsqueeze(1).broadcast_to([128, SLOTS, E]), ALU.is_ge)
                yield v.tensor_reduce(slot_f[:], slot_cmp[:], AX.X, ALU.add)
                v.tensor_scalar(slot_expert[:], slot_f[:], float(EX - 1), None, ALU.min).then_inc(r_done, 1)

            def take(route, n):
                for ins in itertools.islice(route, n):
                    step(ins)

            def band(n, u, j, route=(), pace=0):
                for m in range(8):
                    dve.wait_ge(c_silu[m % 2], 4 * n + m // 2 + 1)
                    dve.wait_ge(c_b[m % 2], 4 * n + m // 2 + 1)
                    v.tensor_tensor(s_h[:, m, :], s_sg[:, m % 2, :], ps[:, 2 + m % 2, 0:BAND],
                                    ALU.mult).then_inc(c_h[m % 2], 1)
                    take(route, pace)
                take(route, 99)
                for s in range(3):
                    w = 3 * u + s
                    dve.wait_ge(c_zps[w % 2], 3 * j + w // 2 + 1)
                    dve.wait_ge(c_x2ld, 48 * n + 48)
                    v.tensor_tensor(c_x2[:, s, :], ps[:, 4 + w % 2, 0:D], c_x2[:, s, :],
                                    ALU.add).then_inc(c_z[w % 2], 1)

            dve.wait_ge(b_lg, NT)
            count_from(base_b + B_STEPS * NT)
            for c in range(3):
                dve.wait_ge(b_x2st[c], 16 * NB)
                dve.wait_ge(b_xn2st[c], 16 * NB)
                dve.wait_ge(b_xTst[c], 16 * NB)
            route = scores_to_pairs()
            take(route, 2)
            band(0, 0, 0, route, 3)
            band(1, 1, 0, pairs_to_rows(), 4)
            with dve.Fori(1, NB // 2) as j:
                for u in range(2):
                    band(2 * j + u, u, j)

            dve.wait_ge(d_half, 2)
            dve.wait_ge(l_back, 16)

            def hT_out(v, g):
                q = 2 * g + v // 2
                dve.wait_ge(d_hTps[v % 2], q + 1)
                dve.wait_ge(d_yps[v % 2], q)
                nc.vector.tensor_copy(m_hT[:, v % 2, :], ps[:, 4, :]).then_inc(d_hTev, 1)

            def y_out(j, v, g):
                dve.wait_ge(d_yps[v % 2], 2 * g + v // 2 + 1)
                dve.wait_ge(d_sc[v], 16 * g)
                nc.vector.tensor_scalar(ys[:, v, :], ps[:, 5, 0:D], lists[:, ds(j, 1), 1].bitcast(f32), None,
                                        ALU.mult).then_inc(d_y, 1)

            def d_step(g, first):
                for v in range(V4):
                    q = 2 * g + v // 2
                    pv, pg = ((v - 1), g) if v else (V4 - 1, g - 1)
                    if not (first and v == 0):
                        hT_out(pv, pg)
                    dve.wait_ge(d_silu[v % 2], q + 1)
                    dve.wait_ge(d_b[v % 2], q + 1)
                    dve.wait_ge(d_hTps[v % 2], q)
                    nc.vector.tensor_tensor(m_h[:, v % 2, :], m_sg[:, v % 2, :], ps[:, 2 + v % 2, :],
                                            ALU.mult).then_inc(d_h[v % 2], 1)
                    if not (first and v == 0):
                        y_out(V4 * g + v - 1, pv, pg)

            d_step(0, True)
            d_step(1, False)
            with dve.Fori(2, SLOTS // V4) as g:
                d_step(g, False)
            hT_out(V4 - 1, SLOTS // V4 - 1)
            y_out(SLOTS - 1, V4 - 1, SLOTS // V4 - 1)

        @block.tensor
        def _(pe):
            mm, tr = nc.tensor.matmul, nc.tensor.transpose
            pe.wait_ge(s_const, 16 * 13)
            for g in range(2):
                for c in range(2):
                    mm(ps[0:96, 2, NREG * g:NREG * (g + 1)], wqk_sb[:, c, 2 + g, :], reg_t[:, c, :],
                       start=c == 0, stop=c == 1)
            for c in range(2):
                ins = mm(ps[0:NREG, 3, 0:D], reg_t[:, c, :], wv_sb[:, c, :], start=c == 0, stop=c == 1)
            ins.then_inc(r_ps, 1)
            pe.wait_ge(r_k, 1)
            pe.wait_ge(r_v, 1)

            def transpose_x(n, u, j):
                pe.wait_ge(a_norm, n + 1)
                pe.wait_ge(a_xnTev, n)
                for c in range(2):
                    for s in range(3):
                        ins = tr(ps[0:96, c, 128 * s:128 * (s + 1)], a_xn[:, u, s, 96 * c:96 * (c + 1)],
                                 ident_sb[:, :])
                ins.then_inc(a_xTps, 1)

            def qkv(j, last=False):
                for u in range(2):
                    n = 2 * j + u
                    pe.wait_ge(a_xnTev, n + 1)

                    def v_mm(s):
                        w = 3 * u + s
                        pe.wait_ge(a_vev[w % 2], 3 * j + w // 2)
                        for c in range(2):
                            ins = mm(ps[:, 6 + w % 2, 0:D], a_xnT[:, u, c, 128 * s:128 * (s + 1)],
                                     wv_sb[:, c, :], start=c == 0, stop=c == 1)
                        ins.then_inc(a_vps[w % 2], 1)

                    v_mm(0)
                    v_mm(1)
                    for g in range(4):
                        if g == 3 and not (last and u):
                            transpose_x(n + 1, 1 - u, j + u)
                        made, used, bank = ((a_qps, a_qev, 2), (a_kps, a_kev, 4))[g % 2]
                        pe.wait_ge(used[g // 2], n)
                        for c in range(2):
                            ins = mm(ps[0:96, bank + g // 2, 0:BAND], wqk_sb[:, c, 2 * (g % 2) + g // 2, :],
                                     a_xnT[:, u, c, :], start=c == 0, stop=c == 1)
                        ins.then_inc(made[g // 2], 1)
                    v_mm(2)

            transpose_x(0, 0, 0)
            turns(pe, NB // 2, qkv, lambda j: qkv(j, True))
            for r in range(2):
                pe.wait_ge(a_qev[r], NB)
                pe.wait_ge(a_kev[r], NB)
                pe.wait_ge(a_vev[r], 3 * NB // 2)
            pe.wait_ge(s_kpad, 2)
            pe.wait_ge(s_ksp, 16 * 19)
            pe.wait_ge(s_oz, 1)

            def scores(i, c, p):
                n = 3 * i + c
                if p == 0:
                    pe.wait_ge(b_qld[c], 96 * i + 96)
                    pe.wait_ge(b_kld[c], 112 * i + 112)
                pe.wait_ge(b_exp[p % 2], 3 * n + p // 2)
                for hh in range(2):
                    ins = mm(ps[:, 2 * (p % 2) + hh, 0:KW], qsp[0:120, c, 2 * p + hh, :],
                             ksp[0:120, c, 2 * p + hh, :], start=True, stop=True)
                ins.then_inc(b_S[p % 2], 1)

            def token_T(i, c, half):
                if half == 0:
                    pe.wait_ge(b_xn2, 2 * (3 * i + c) + 2)
                return tr(ps[0:96, 4 + half, 384:512], xn2[:, c, 96 * half:96 * (half + 1)], ident_sb[:, :])

            def gate(i, c):
                m = 3 * i + c
                pe.wait_ge(b_xTevD, m + 1)
                pe.wait_ge(b_xTevA, m + 1)
                for k in range(2):
                    ins = mm(ps[:, 4, 384:384 + E], xn2T[:, c, k, :], gate_sb[:, k, :], start=k == 0, stop=k == 1)
                return ins

            def probs_T(i, c, p):
                n = 3 * i + c
                last = type(i) is int and (i, c, p) == (NB - 1, 2, 5)
                pe.wait_ge(b_exp[p % 2], 3 * n + p // 2 + 1)
                for hh in range(2):
                    pe.wait_ge((b_TevD, b_TevA)[hh], 6 * n + p)
                    if p == 1 and tails(i, c) > 1:
                        token_T(*back2(i, c), hh)
                    if last:
                        token_T(i, 1, hh)
                    if p == 3 and tails(i, c) > 1 and hh == 0:
                        gate(*back2(i, c))
                    for k in range(3):
                        ins = tr(ps[0:CH, 4 + hh, 128 * k:128 * (k + 1)], probs[:, p % 2, hh, CH * k:CH * (k + 1)],
                                 ident_sb[:, :])
                    ins.then_inc(b_T[hh], 1)

            def values(i, c, p):
                n = 3 * i + c
                if p == 0:
                    pe.wait_ge(b_vld[c], 48 * i + 48)
                    pe.wait_ge(b_oraw, n)
                for hh in range(2):
                    pe.wait_ge((b_TevD, b_TevA)[hh], 6 * n + p + 1)
                    h = 2 * p + hh
                    g, r = head(p, hh)
                    for k in range(3):
                        ins = mm(ps[r:r + 16, 6, 128 * g:128 * (g + 1)], vst[0:CH, c, k, 16 * h:16 * h + 16],
                                 probsT[0:CH, p % 2, hh, 128 * k:128 * (k + 1)], start=k == 0, stop=k == 2)
                ins.then_inc(b_O[p % 2], 1)

            def tail_R(i, c):
                m = 3 * i + c
                pe.wait_ge(b_rsum, m + 1)
                pe.wait_ge(b_x2, m)
                for g in range(3):
                    ins = tr(ps[:, 7, 128 * g:128 * (g + 1)],
                             rsum[:, 4 * g:4 * g + 4, :].rearrange("p h x -> p (h x)"), ident_sb[:, :])
                ins.then_inc(b_R, 1)

            def tail_proj(i, c):
                m = 3 * i + c
                pe.wait_ge(b_oTev, m + 1)
                tail_proj_g(0)
                tail_proj_g(1)

            def tail_proj_g(g):
                ins = mm(ps[:, 7, 0:D], oT[:, g, :], wo_sb[:, g, :], start=g == 0, stop=g == 2)
                if g == 2:
                    ins.then_inc(b_Pps, 1)

            def b_tile(i, c):
                for p in range(6):
                    scores(i, c, p)
                    if tails(i, c):
                        if p == 3:
                            tail_R(*back(i, c))
                        if p == 4:
                            tail_proj(*back(i, c))
                        if p == 5:
                            tail_proj_g(2)
                    if pair_back(i, c, p, 2):
                        probs_T(*pair_back(i, c, p, 2))
                    if pair_back(i, c, p, 3):
                        values(*pair_back(i, c, p, 3))
            for n in range(3):
                b_tile(0, n)
            with pe.Fori(1, NB) as i:
                for c in range(3):
                    b_tile(i, c)
            probs_T(NB - 1, 2, 4)
            values(NB - 1, 2, 3)
            probs_T(NB - 1, 2, 5)
            values(NB - 1, 2, 4)
            values(NB - 1, 2, 5)
            tail_R(NB - 1, 2)
            gate(NB - 1, 1).then_inc(b_T[0], 1)
            tail_proj(NB - 1, 2)
            tail_proj_g(2)
            for half in range(2):
                token_T(NB - 1, 2, half).then_inc(b_T[half], 1)
            gate(NB - 1, 2).then_inc(b_T[0], 1)

            def count_pairs(k, made):
                for a in range(2):
                    ins = mm(ps[:, 6 + a, 0:E // 2 * NT], tri_sb[:, k, :],
                             rt_m[:, E // 2 * a:E // 2 * (a + 1), :].rearrange("p e n -> p (e n)"),
                             start=True, stop=True)
                ins.then_inc(made, 1)

            def band(n, u, j, route=False):
                pe.wait_ge(c_xld[u], 16 * j + 16)
                for m in range(8):
                    if route and m == 2:
                        pe.wait_ge(r_totc, 1)
                        count_pairs(0, r_rank)
                    for k, (used, made) in enumerate(((c_silu, c_a), (c_h, c_b))):
                        pe.wait_ge(used[m % 2], 4 * n + m // 2)
                        for c in range(2):
                            ins = mm(ps[:, 2 * k + m % 2, 0:BAND], sw13_sb[:, c, k, 128 * m:128 * (m + 1)],
                                     c_x[:, u, c, :], start=c == 0, stop=c == 1)
                        ins.then_inc(made[m % 2], 1)
                for r in range(2):
                    pe.wait_ge(c_h[r], 4 * n + 4)
                for s in range(3):
                    w = 3 * u + s
                    pe.wait_ge(c_z[w % 2], 3 * j + w // 2)
                    for m in range(8):
                        ins = mm(ps[:, 4 + w % 2, 0:D], s_h[:, m, 128 * s:128 * (s + 1)], sw2_sb[:, m, :],
                                 start=m == 0, stop=m == 7)
                    ins.then_inc(c_zps[w % 2], 1)

            pe.wait_ge(b_lg, NT)
            pe.wait_ge(c_w, 32)
            band(0, 0, 0)
            pe.wait_ge(r_m, 1)
            count_pairs(1, r_tot)
            band(1, 1, 0, True)
            with pe.Fori(1, NB // 2) as j:
                for u in range(2):
                    band(2 * j + u, u, j)

            pe.wait_ge(d_w, 48 * EX // 2)
            pe.wait_ge(r_done, 1)
            pe.wait_ge(d_half, 2)
            for r in range(2):
                pe.wait_ge(c_z[r], 3 * NB // 2)

            def x_T(v, g):
                q = 2 * g + v // 2
                pe.wait_ge(d_g[v], 16 * g + 16)
                pe.wait_ge(d_xTev[v % 2], 3 * q)
                for k in range(2):
                    ins = tr(ps[:, 6 + v % 2, 128 * k:128 * (k + 1)], xg[:, v, 128 * k:128 * (k + 1)], ident_sb[:, :])
                ins.then_inc(d_xTps[v % 2], 1)

            def h_T(v, g):
                q = 2 * g + v // 2
                pe.wait_ge(d_h[v % 2], q + 1)
                pe.wait_ge(d_hTev, V4 * g + v)
                for k in range(4):
                    ins = tr(ps[:, 4, 128 * k:128 * (k + 1)], m_h[:, v % 2, 128 * k:128 * (k + 1)], ident_sb[:, :])
                ins.then_inc(d_hTps[v % 2], 1)

            def y_mm(j, v, g):
                e = pe.value_load(slot_expert[0:1, ds(j, 1)], min_val=0, max_val=EX - 1)
                pe.wait_ge(d_hTev, j + 1)
                pe.wait_ge(d_y, j)
                for k in range(4):
                    ins = mm(ps[:, 5, 0:D], m_hT[:, v % 2, 128 * k:128 * (k + 1)],
                             w2_sb[:].rearrange("p e k d -> p (e k d)")[:, ds(e * (4 * D) + k * D, D)],
                             start=k == 0, stop=k == 3)
                ins.then_inc(d_yps[v % 2], 1)

            def d_step(g, first, last):
                for v in range(V4):
                    j = V4 * g + v
                    q = 2 * g + v // 2
                    pv, pg = ((v - 1), g) if v else (V4 - 1, g - 1)
                    e = pe.value_load(slot_expert[0:1, ds(j, 1)], min_val=0, max_val=EX - 1)
                    wa = w13a_sb[:].rearrange("p e k d -> p (e k d)")
                    wb = w13b_sb[:].rearrange("p e d -> p (e d)")
                    pe.wait_ge(d_xTev[v % 2], 3 * q + 3)
                    for k, (half, used, made) in enumerate(((xb1, d_silu, d_a), (xb3, d_h, d_b))):
                        pe.wait_ge(used[v % 2], q)
                        mm(ps[:, 2 * k + v % 2, :], xa[:, v % 2, :], wa[:, ds(e * (2 * INTER) + k * INTER, INTER)],
                           start=True, stop=False)
                        mm(ps[:, 2 * k + v % 2, :], half[:, v % 2, :], wb[:, ds(e * INTER, INTER)],
                           start=False, stop=True).then_inc(made[v % 2], 1)
                        if k == 0:
                            if not (last and v == V4 - 1):
                                x_T((v + 1) % V4, g + (v + 1) // V4)
                            if not (first and v == 0):
                                h_T(pv, pg)
                    if not (first and v == 0):
                        y_mm(j - 1, pv, pg)

            x_T(0, 0)
            d_step(0, True, False)
            with pe.Fori(1, SLOTS // V4 - 1) as g:
                d_step(g, False, False)
            d_step(SLOTS // V4 - 1, False, True)
            h_T(V4 - 1, SLOTS // V4 - 1)
            y_mm(SLOTS - 1, V4 - 1, SLOTS // V4 - 1)


def _lay_out(x, L0_conv_registers, L0_conv_qkv_w, L0_conv_qkv_b, L0_conv_out_w, L0_conv_out_b,
             L0_ffn_gate_w, L0_ffn_w1, L0_ffn_w2, L0_ffn_w3, L0_ffn_sw1, L0_ffn_sw2, L0_ffn_sw3):
    import numpy as np

    def arr(a):
        return np.asarray(a)

    def halves(w):
        return np.ascontiguousarray(w.reshape(2, 96, -1).transpose(1, 0, 2))

    D, H = 192, 12
    qkv_w, qkv_b = arr(L0_conv_qkv_w), arr(L0_conv_qkv_b)
    wo = np.zeros((4, 32, 3, D), np.float32)
    wo[:, :16] = arr(L0_conv_out_w).T.reshape(3, 4, 16, D).transpose(1, 2, 0, 3)
    wo = wo.reshape(128, 3, D)
    o = {
        "x": arr(x).reshape(-1, D),
        "kv_reg_t": halves(arr(L0_conv_registers).T),
        "wqk": halves(qkv_w[:2 * D].T).reshape(96, 2, 4, 96),
        "bqk": np.ascontiguousarray(qkv_b[:2 * D].reshape(4, 96).T),
        "wv": halves(qkv_w[2 * D:].T),
        "bv": np.broadcast_to(qkv_b[2 * D:], (128, D)).copy(),
        "wo": wo,
        "bo": np.broadcast_to(arr(L0_conv_out_b), (128, D)).copy(),
        "gate_t": halves(arr(L0_ffn_gate_w).T),
    }
    w1, w3 = (arr(w).transpose(2, 0, 1) for w in (L0_ffn_w1, L0_ffn_w3))
    o["w13a"] = np.ascontiguousarray(np.stack([w1[:128], w3[:128]], axis=2))
    o["w13b"] = np.ascontiguousarray(np.concatenate([w1[128:], w3[128:]], axis=0))
    o["w2"] = np.ascontiguousarray(arr(L0_ffn_w2).reshape(16, D, 4, 128).transpose(3, 0, 2, 1))
    o["sw13"] = np.ascontiguousarray(np.stack([halves(arr(L0_ffn_sw1).T), halves(arr(L0_ffn_sw3).T)], axis=2))
    o["sw2"] = np.ascontiguousarray(arr(L0_ffn_sw2).T.reshape(8, 128, D).transpose(1, 0, 2))

    def bf(a):
        return (np.ascontiguousarray(a, np.float32).view(np.uint32) >> 16).astype(np.uint16)

    o["ident"] = np.eye(128, dtype=np.float32)
    t = np.arange(128)
    o["tri"] = bf(np.stack([t[:, None] < t[None, :], np.ones((128, 128), bool)], axis=1))
    mq = np.zeros((24, 128), np.float32)
    mq[t // 16, t] = 1
    mq[8 + t % 16, t] = 1
    o["mask_q"] = bf(mq)
    mk = np.zeros((24, 12, 3, 330), np.float32)
    for i in range(12):
        for c in range(3):
            kr0, kc0 = 8 * (i % 6) - 3, min(max(16 * c - 3, 0), 26)
            kr = kr0 + np.arange(308) // 22
            kc = kc0 + np.arange(308) % 22
            for r in range(8):
                lo = min(max(8 * (i % 6) + r - 3, 0), 41)
                mk[r, i, c, :308] = np.where((kr >= lo) & (kr < lo + 7), 0, -1e30)
            for q in range(16):
                lo = min(max(16 * c + q - 3, 0), 41)
                mk[8 + q, i, c, :308] = np.where((kc >= lo) & (kc < lo + 7), 0, -1e30)
    mk[:8, :, :, 324:] = -1e30
    o["mask_k"] = bf(mk.reshape(24, -1))
    n = np.arange(36)
    p = t[:, None]
    o["token_ids"] = (n // 3 * 384 + n % 3 * 16 + p // 16 * 48 + p % 16).astype(np.int32)
    o["iota_e"] = np.broadcast_to(np.arange(16, dtype=np.float32), (128, 16)).copy()
    o["iota_s"] = np.broadcast_to(np.arange(88, dtype=np.float32), (128, 88)).copy()
    li = np.zeros((128, 88, 2), np.int32)
    li[:, :, 0] = 4608 + p
    o["list_init"] = li.reshape(128, -1)
    return o


def kernel(**inputs):
    import concourse.bacc as _bacc
    from concourse import mybir as _mybir
    from concourse.bass_utils import run_bass_kernel_spmd as _run

    nc = _bacc.Bacc("TRN2", target_bir_lowering=False, num_devices=1)
    arrays, args = {}, []
    for name, a in _lay_out(**inputs).items():
        arrays[f"in_{name}"] = a
        args.append(nc.dram_tensor(f"in_{name}", a.shape, _mybir.dt.from_np(a.dtype), kind="ExternalInput").ap())
    out = nc.dram_tensor("out", (4608, 192), _mybir.dt.float32, kind="ExternalOutput").ap()
    metaformer_block(nc, *args, out)
    r = _run(nc, [arrays], core_ids=[0])
    return r.results[0]["out"].reshape(2, 48, 48, 192)
```
